# Optimizing a Trainium2 kernel written in Bass

```python
import numpy as np
import jax
import jax.numpy as jnp

def _softmax(x, axis=-1):
    return jax.nn.softmax(x, axis=axis)

def _gelu(x):
    return jax.nn.gelu(x, approximate=True)

def _silu(x):
    return jax.nn.silu(x)

def _sigmoid(x):
    return jax.nn.sigmoid(x)

def _layernorm(x, axis=-1, eps=1e-05):
    m = jnp.mean(x, axis=axis, keepdims=True)
    v = jnp.var(x, axis=axis, keepdims=True)
    return (x - m) / jnp.sqrt(v + eps)

def _scatter_add(tgt, idx, src, axis=0):
    return tgt.at[idx].add(src)

def _segment_sum(src, seg, n):
    return jax.ops.segment_sum(src, seg, n)
kernel_name = 'mk_prb_d2_jaxref_r8_669eb8'

def setup_inputs(seed: int=0):
    np.random.seed(seed)
    _w = jnp.asarray

    def _L0_attn_setup():
        import jax, jax.numpy as jnp
        import numpy as np
        D_MODEL = 256
        HEADS = 16
        HEAD_DIM = D_MODEL // HEADS
        key = jax.random.key(seed)
        k1, k2, k3 = jax.random.split(key, 3)
        B, S = (1, 256)
        x = jax.random.normal(k1, (B, S, D_MODEL), dtype=jnp.float32)
        Wqkv_w = jax.random.normal(k2, (D_MODEL + 2 * HEAD_DIM, D_MODEL), dtype=jnp.float32) * D_MODEL ** (-0.5)
        Wqkv_b = jnp.zeros((D_MODEL + 2 * HEAD_DIM,), dtype=jnp.float32)
        out_w = jax.random.normal(k3, (D_MODEL, D_MODEL), dtype=jnp.float32) * D_MODEL ** (-0.5)
        out_b = jnp.zeros((D_MODEL,), dtype=jnp.float32)
        return {'x': x, 'Wqkv_w': Wqkv_w, 'Wqkv_b': Wqkv_b, 'out_w': out_w, 'out_b': out_b}
    _L0_attn_in = _L0_attn_setup()

    def _L0_ffn_setup():
        import jax, jax.numpy as jnp
        import numpy as np
        DIM = 256
        HID = 704
        ZERO_POINT = 128.0

        def _qlinear(x, wq, scale):
            W = (wq.astype(jnp.float32) - ZERO_POINT) * scale[:, None]
            return jnp.einsum('bsd,hd->bsh', x, W)
        key = jax.random.key(seed)
        ks = jax.random.split(key, 7)
        B, S = (4, 256)
        sg = jax.random.uniform(ks[1], (HID,)) * (0.02 / np.sqrt(DIM)) + 0.0001
        su = jax.random.uniform(ks[3], (HID,)) * (0.02 / np.sqrt(DIM)) + 0.0001
        sd = jax.random.uniform(ks[5], (DIM,)) * (0.02 / np.sqrt(HID)) + 0.0001
        return {'x': jax.random.normal(ks[0], (B, S, DIM), dtype=jnp.float32), 'wq_gate': jax.random.randint(ks[2], (HID, DIM), 0, 32, dtype=jnp.int32), 's_gate': sg, 'wq_up': jax.random.randint(ks[4], (HID, DIM), 0, 32, dtype=jnp.int32), 's_up': su, 'wq_down': jax.random.randint(ks[6], (DIM, HID), 0, 32, dtype=jnp.int32), 's_down': sd}
    _L0_ffn_in = _L0_ffn_setup()

    def _L1_attn_setup():
        import jax, jax.numpy as jnp
        import numpy as np
        BLOCK = 32
        NUM_HEADS = 16
        HEAD_DIM = 128
        FP4_GRID = jnp.array([0.0, 0.5, 1.0, 1.5, 2.0, 3.0, 4.0, 6.0], dtype=jnp.float32)

        def quantize_to_mxfp4(w, block_size=BLOCK):
            D, F = w.shape
            blocks = w.reshape(D // block_size, block_size, F)
            amax = jnp.max(jnp.abs(blocks), axis=1)
            e = jnp.floor(jnp.log2(jnp.maximum(amax, 1e-12) / 6.0))
            scale = jnp.exp2(e)
            v = blocks / scale[:, None, :]
            idx = jnp.argmin(jnp.abs(jnp.abs(v)[..., None] - FP4_GRID), axis=-1)
            codes = jnp.sign(v) * FP4_GRID[idx]
            return (codes.reshape(D, F).astype(jnp.float32), scale.astype(jnp.float32))

        def _mxfp4_matmul(x, codes, scales, block_size=BLOCK):
            w = codes * jnp.repeat(scales, block_size, axis=0)
            return x @ w
        key = jax.random.key(seed)
        ks = jax.random.split(key, 9)
        B, S, D = (2, 256, 256)
        feat = NUM_HEADS * HEAD_DIM
        x = jax.random.normal(ks[0], (B, S, D), dtype=jnp.float32)

        def make_w(k, din, dout):
            w = jax.random.normal(k, (din, dout), dtype=jnp.float32) * (1.0 / np.sqrt(din))
            return quantize_to_mxfp4(w, BLOCK)
        wq_codes, wq_scales = make_w(ks[1], D, feat)
        wk_codes, wk_scales = make_w(ks[2], D, feat)
        wv_codes, wv_scales = make_w(ks[3], D, feat)
        wo_codes, wo_scales = make_w(ks[4], feat, D)
        bq = jnp.zeros((feat,), jnp.float32)
        bk = jnp.zeros((feat,), jnp.float32)
        bv = jnp.zeros((feat,), jnp.float32)
        bo = jnp.zeros((D,), jnp.float32)
        return {'x': x, 'wq_codes': wq_codes, 'wq_scales': wq_scales, 'bq': bq, 'wk_codes': wk_codes, 'wk_scales': wk_scales, 'bk': bk, 'wv_codes': wv_codes, 'wv_scales': wv_scales, 'bv': bv, 'wo_codes': wo_codes, 'wo_scales': wo_scales, 'bo': bo}
    _L1_attn_in = _L1_attn_setup()

    def _L1_ffn_setup():
        import jax, jax.numpy as jnp
        import numpy as np
        DIM = 256
        INTER = 176
        N_EXPERTS = 16
        TOP_K = 2
        N_SHARED = 2
        SHARED_INTER = N_SHARED * INTER

        def _swiglu(t, wa, wb, wo):
            h = jax.nn.silu(t @ wa.T) * (t @ wb.T)
            return h @ wo.T
        key = jax.random.key(seed)
        ks = jax.random.split(key, 9)
        s = 0.02
        return {'x': jax.random.normal(ks[0], (4, 256, DIM), dtype=jnp.float32), 'gate_w': jax.random.normal(ks[1], (N_EXPERTS, DIM), dtype=jnp.float32) * s, 'w1': jax.random.normal(ks[2], (N_EXPERTS, INTER, DIM), dtype=jnp.float32) * s, 'w2': jax.random.normal(ks[3], (N_EXPERTS, DIM, INTER), dtype=jnp.float32) * s, 'w3': jax.random.normal(ks[4], (N_EXPERTS, INTER, DIM), dtype=jnp.float32) * s, 'sw1': jax.random.normal(ks[5], (SHARED_INTER, DIM), dtype=jnp.float32) * s, 'sw2': jax.random.normal(ks[6], (DIM, SHARED_INTER), dtype=jnp.float32) * s, 'sw3': jax.random.normal(ks[7], (SHARED_INTER, DIM), dtype=jnp.float32) * s}
    _L1_ffn_in = _L1_ffn_setup()
    _d = {'L0_attn_x': _L0_attn_in['x'], 'L0_attn_Wqkv_w': _L0_attn_in['Wqkv_w'], 'L0_attn_Wqkv_b': _L0_attn_in['Wqkv_b'], 'L0_attn_out_w': _L0_attn_in['out_w'], 'L0_attn_out_b': _L0_attn_in['out_b'], 'L0_ffn_wq_gate': _L0_ffn_in['wq_gate'], 'L0_ffn_s_gate': _L0_ffn_in['s_gate'], 'L0_ffn_wq_up': _L0_ffn_in['wq_up'], 'L0_ffn_s_up': _L0_ffn_in['s_up'], 'L0_ffn_wq_down': _L0_ffn_in['wq_down'], 'L0_ffn_s_down': _L0_ffn_in['s_down'], 'L1_attn_wq_codes': _L1_attn_in['wq_codes'], 'L1_attn_wq_scales': _L1_attn_in['wq_scales'], 'L1_attn_bq': _L1_attn_in['bq'], 'L1_attn_wk_codes': _L1_attn_in['wk_codes'], 'L1_attn_wk_scales': _L1_attn_in['wk_scales'], 'L1_attn_bk': _L1_attn_in['bk'], 'L1_attn_wv_codes': _L1_attn_in['wv_codes'], 'L1_attn_wv_scales': _L1_attn_in['wv_scales'], 'L1_attn_bv': _L1_attn_in['bv'], 'L1_attn_wo_codes': _L1_attn_in['wo_codes'], 'L1_attn_wo_scales': _L1_attn_in['wo_scales'], 'L1_attn_bo': _L1_attn_in['bo'], 'L1_ffn_gate_w': _L1_ffn_in['gate_w'], 'L1_ffn_w1': _L1_ffn_in['w1'], 'L1_ffn_w2': _L1_ffn_in['w2'], 'L1_ffn_w3': _L1_ffn_in['w3'], 'L1_ffn_sw1': _L1_ffn_in['sw1'], 'L1_ffn_sw2': _L1_ffn_in['sw2'], 'L1_ffn_sw3': _L1_ffn_in['sw3']}
    _x0 = _d['L0_attn_x']
    _d['L0_attn_x'] = jax.random.normal(jax.random.fold_in(jax.random.key(seed), 1), (8, 256, 256), dtype=_x0.dtype)
    del _x0
    return _d

def reference(L0_attn_x, L0_attn_Wqkv_w, L0_attn_Wqkv_b, L0_attn_out_w, L0_attn_out_b, L0_ffn_wq_gate, L0_ffn_s_gate, L0_ffn_wq_up, L0_ffn_s_up, L0_ffn_wq_down, L0_ffn_s_down, L1_attn_wq_codes, L1_attn_wq_scales, L1_attn_bq, L1_attn_wk_codes, L1_attn_wk_scales, L1_attn_bk, L1_attn_wv_codes, L1_attn_wv_scales, L1_attn_bv, L1_attn_wo_codes, L1_attn_wo_scales, L1_attn_bo, L1_ffn_gate_w, L1_ffn_w1, L1_ffn_w2, L1_ffn_w3, L1_ffn_sw1, L1_ffn_sw2, L1_ffn_sw3):

    def _L0_attn_ref(x, Wqkv_w, Wqkv_b, out_w, out_b):
        import jax, jax.numpy as jnp
        import numpy as np
        D_MODEL = 256
        HEADS = 16
        HEAD_DIM = D_MODEL // HEADS
        B, S, _ = x.shape
        qkv = jnp.einsum('bsd,ed->bse', x, Wqkv_w) + Wqkv_b
        q = qkv[..., :D_MODEL]
        k = qkv[..., D_MODEL:D_MODEL + HEAD_DIM]
        v = qkv[..., D_MODEL + HEAD_DIM:]
        q = q.reshape(B, S, HEADS, HEAD_DIM)
        scale = 1.0 / np.sqrt(HEAD_DIM)
        scores = jnp.einsum('bqhd,bkd->bhqk', q, k) * scale
        min_val = jnp.finfo(scores.dtype).min
        causal = jnp.tril(jnp.ones((S, S), dtype=bool))
        scores = jnp.where(causal[None, None], scores, min_val)
        attn = jax.nn.softmax(scores, axis=-1)
        ctx = jnp.einsum('bhqk,bkd->bqhd', attn, v)
        ctx = ctx.reshape(B, S, D_MODEL)
        out = jnp.einsum('bsd,ed->bse', ctx, out_w) + out_b
        return out

    def _L0_ffn_ref(x, wq_gate, s_gate, wq_up, s_up, wq_down, s_down):
        import jax, jax.numpy as jnp
        import numpy as np
        DIM = 256
        HID = 704
        ZERO_POINT = 128.0

        def _qlinear(x, wq, scale):
            W = (wq.astype(jnp.float32) - ZERO_POINT) * scale[:, None]
            return jnp.einsum('bsd,hd->bsh', x, W)
        gate = _qlinear(x, wq_gate, s_gate)
        gate = jax.nn.silu(gate)
        up = _qlinear(x, wq_up, s_up)
        return _qlinear(gate * up, wq_down, s_down)

    def _L1_attn_ref(x, wq_codes, wq_scales, bq, wk_codes, wk_scales, bk, wv_codes, wv_scales, bv, wo_codes, wo_scales, bo):
        import jax, jax.numpy as jnp
        import numpy as np
        BLOCK = 32
        NUM_HEADS = 16
        HEAD_DIM = 128
        FP4_GRID = jnp.array([0.0, 0.5, 1.0, 1.5, 2.0, 3.0, 4.0, 6.0], dtype=jnp.float32)

        def quantize_to_mxfp4(w, block_size=BLOCK):
            D, F = w.shape
            blocks = w.reshape(D // block_size, block_size, F)
            amax = jnp.max(jnp.abs(blocks), axis=1)
            e = jnp.floor(jnp.log2(jnp.maximum(amax, 1e-12) / 6.0))
            scale = jnp.exp2(e)
            v = blocks / scale[:, None, :]
            idx = jnp.argmin(jnp.abs(jnp.abs(v)[..., None] - FP4_GRID), axis=-1)
            codes = jnp.sign(v) * FP4_GRID[idx]
            return (codes.reshape(D, F).astype(jnp.float32), scale.astype(jnp.float32))

        def _mxfp4_matmul(x, codes, scales, block_size=BLOCK):
            w = codes * jnp.repeat(scales, block_size, axis=0)
            return x @ w
        B, S, D = x.shape
        q = _mxfp4_matmul(x, wq_codes, wq_scales) + bq
        k = _mxfp4_matmul(x, wk_codes, wk_scales) + bk
        v = _mxfp4_matmul(x, wv_codes, wv_scales) + bv
        q = q.reshape(B, S, NUM_HEADS, HEAD_DIM)
        k = k.reshape(B, S, NUM_HEADS, HEAD_DIM)
        v = v.reshape(B, S, NUM_HEADS, HEAD_DIM)
        scores = jnp.einsum('bqhd,bkhd->bhqk', q, k) / jnp.sqrt(jnp.float32(HEAD_DIM))
        attn = jax.nn.softmax(scores, axis=-1)
        out = jnp.einsum('bhqk,bkhd->bqhd', attn, v).reshape(B, S, NUM_HEADS * HEAD_DIM)
        return _mxfp4_matmul(out, wo_codes, wo_scales) + bo

    def _L1_ffn_ref(x, gate_w, w1, w2, w3, sw1, sw2, sw3):
        import jax, jax.numpy as jnp
        import numpy as np
        DIM = 256
        INTER = 176
        N_EXPERTS = 16
        TOP_K = 2
        N_SHARED = 2
        SHARED_INTER = N_SHARED * INTER

        def _swiglu(t, wa, wb, wo):
            h = jax.nn.silu(t @ wa.T) * (t @ wb.T)
            return h @ wo.T
        shape = x.shape
        t = x.reshape(-1, DIM)
        scores = jax.nn.softmax(t @ gate_w.T, axis=-1)
        weights, indices = jax.lax.top_k(scores, TOP_K)
        y = jnp.zeros_like(t)
        for e in range(N_EXPERTS):
            w_e = jnp.sum(jnp.where(indices == e, weights, 0.0), axis=-1)
            y = y + _swiglu(t, w1[e], w3[e], w2[e]) * w_e[:, None]
        z = _swiglu(t, sw1, sw3, sw2)
        return (y + z).reshape(shape)
    x = L0_attn_x
    xn = _layernorm(x, axis=-1)
    x = x + _L0_attn_ref(xn, L0_attn_Wqkv_w, L0_attn_Wqkv_b, L0_attn_out_w, L0_attn_out_b) + _L0_ffn_ref(xn, L0_ffn_wq_gate, L0_ffn_s_gate, L0_ffn_wq_up, L0_ffn_s_up, L0_ffn_wq_down, L0_ffn_s_down)
    xn = _layernorm(x, axis=-1)
    x = x + _L1_attn_ref(xn, L1_attn_wq_codes, L1_attn_wq_scales, L1_attn_bq, L1_attn_wk_codes, L1_attn_wk_scales, L1_attn_bk, L1_attn_wv_codes, L1_attn_wv_scales, L1_attn_bv, L1_attn_wo_codes, L1_attn_wo_scales, L1_attn_bo) + _L1_ffn_ref(xn, L1_ffn_gate_w, L1_ffn_w1, L1_ffn_w2, L1_ffn_w3, L1_ffn_sw1, L1_ffn_sw2, L1_ffn_sw3)
    return x

_drawn_inputs = setup_inputs


def setup_inputs(seed=0):
    import zlib

    import numpy as np

    out = dict(_drawn_inputs(seed))
    spreads = {'L0_attn_Wqkv_b': (0.0, 0.1),
     'L0_attn_out_b': (0.0, 0.1),
     'L1_attn_bq': (0.0, 0.8),
     'L1_attn_bk': (0.0, 2.0),
     'L1_attn_bv': (0.0, 0.776),
     'L1_attn_bo': (0.0, 0.8)}
    factors = {'L0_ffn_s_gate': 8.0,
     'L0_ffn_s_up': 8.0,
     'L0_ffn_s_down': 8.0,
     'L1_attn_wq_scales': 3.774,
     'L1_attn_wk_scales': 3.751,
     'L1_ffn_gate_w': 8.0,
     'L1_ffn_w1': 8.0,
     'L1_ffn_w2': 8.0,
     'L1_ffn_w3': 8.0,
     'L1_ffn_sw1': 3.174,
     'L1_ffn_sw2': 3.161,
     'L1_ffn_sw3': 3.162,
     'L1_attn_wv_scales': 3.201}
    for name, (base, spread) in spreads.items():
        noise = np.random.default_rng([zlib.crc32(name.encode()), seed]).standard_normal(out[name].shape)
        drawn = base * np.exp(spread * noise) if base else spread * noise
        out[name] = jnp.asarray(drawn.astype(out[name].dtype))
    for name, factor in factors.items():
        out[name] = (out[name] * factor).astype(out[name].dtype)
    return out
```

```python
from contextlib import ExitStack

import numpy as np

import concourse.bass as bass
from concourse import mybir

F32 = mybir.dt.float32
R32 = mybir.dt.float32r
I32 = mybir.dt.int32
U32 = mybir.dt.uint32
ALU = mybir.AluOpType
ACT = mybir.ActivationFunctionType
AX = mybir.AxisListType
ds = bass.ds

P = 128
SEQS, SEQ, D = 8, 256, 256
TOKENS = SEQS * SEQ
DC = D // P
PAIR = 2 * SEQ
TURNS = TOKENS // PAIR
TP = PAIR // P
EPS = 1e-5
HEADS0, HD0 = 16, 16
QKV0 = D + 2 * HD0
HID = 704
ZERO_POINT = 128.0
HT = [min(m, HID - P) for m in range(0, HID, P)]
HEADS1, HD1 = 16, 128
FEAT = HEADS1 * HD1
BLOCK = 32
EXPERTS, INTER, SHARED = 16, 176, 352
ST = [min(m, SHARED - P) for m in range(0, SHARED, P)]
REP = P // HD0
TILES = TOKENS // P
MASKED = -1.0e30


class Signal:

    def __init__(self, sem, per_turn=0, head=0):
        self.sem, self.per_turn, self.head = sem, per_turn, head

    def at(self, turn, n):
        return turn * self.per_turn + (self.head + n)


def stage_layer0(nc, dram):
    QW = D + P + HD0
    DUP_H, DUP_S = 5 * P - HT[5], 2 * P - ST[2]
    with ExitStack() as ctx:
        def sb(name, shape, dt=F32):
            return ctx.enter_context(nc.sbuf_tensor(name, shape, dt))

        def psum(name):
            return ctx.enter_context(nc.psum_tensor(name, [P, 512], F32))

        def sem(name):
            return ctx.enter_context(nc.semaphore(name))

        ident = sb("ident", [P, P])
        ident_r = sb("ident_r", [P, P], R32)
        mask_r = sb("mask_r", [P, 4, P], R32)
        ones_r = sb("ones_r", [1, P], R32)
        w_qkv = [sb(f"w_qkv{i}", [P, DC, QW], R32) for i in range(2)]
        w_o = [sb(f"w_o{i}", [P, DC, D], R32) for i in range(2)]
        ob = [sb(f"ob{i}", [1, D], R32) for i in range(2)]
        w_gate = sb("w_gate", [P, DC, HID], R32)
        w_up = sb("w_up", [P, DC, HID], R32)
        w_down = sb("w_down", [P, len(HT), D], R32)
        w_s13 = [sb(f"w_s13{i}", [P, DC, 2 * SHARED], R32) for i in range(2)]
        w_s2 = [sb(f"w_s2{i}", [P, len(ST), D], R32) for i in range(2)]
        w_gw = [sb(f"w_gw{i}", [P, DC, EXPERTS], R32) for i in range(2)]
        bq = sb("bq", [P, DC])
        bk = sb("bk", [48, 1])
        bv = sb("bv", [P, 2, HD0])
        s_gate = sb("s_gate", [P, len(HT)])
        s_up = sb("s_up", [P, len(HT)])
        half_gate = sb("half_gate", [P, len(HT)])
        scale_h = sb("scale_h", [P, len(HT)])
        s_down = sb("s_down", [P, D])
        with ExitStack() as staging:
            def stage(name, shape, dt=F32):
                return staging.enter_context(nc.sbuf_tensor(name, shape, dt))

            def stage_sem(name):
                return staging.enter_context(nc.semaphore(name))

            mask_f = stage("mask_f", [P, 4, P])
            ones_f = stage("ones_f", [1, P])
            raw_qkv = stage("raw_qkv", [P, DC, QW])
            raw_o = stage("raw_o", [P, DC, D])
            raw_ob = stage("raw_ob", [1, D])
            raw_int = stage("raw_int", [P, DC, HID], I32)
            raw_down = stage("raw_down", [P, len(HT), D], I32)
            raw_s13 = raw_int[:].bitcast(F32)
            raw_s2 = stage("raw_s2", [P, len(ST), D])
            raw_gw = stage("raw_gw", [P, DC, EXPERTS])
            raw_in = stage_sem("raw_in")
            const_ok = stage_sem("const_ok")
            prep_act = stage_sem("prep_act")
            prep_dve = stage_sem("prep_dve")
            block = staging.enter_context(nc.Block())

            loads = [
                (raw_qkv[:, :, 0:D], dram["WqkvT"][:, 0:D].rearrange("(c p) n -> p c n", p=P)),
                *[(raw_qkv[:, :, D + HD0 * i:D + HD0 * (i + 1)], dram["WqkvT"][:, D:D + HD0].rearrange("(c p) n -> p c n", p=P))
                  for i in range(REP)],
                (raw_qkv[:, :, D + P:], dram["WqkvT"][:, D + HD0:].rearrange("(c p) n -> p c n", p=P)),
                (raw_o[:], dram["out_wT"].rearrange("(c p) n -> p c n", p=P)),
                (raw_ob[:], dram["out_b"].rearrange("(a n) -> a n", a=1)),
                *[(bq[:, c:c + 1], dram["Wqkv_b"][c * P:(c + 1) * P].rearrange("(p a) -> p a", a=1)) for c in range(DC)],
                *[(bk[HD0 * i:HD0 * (i + 1), :], dram["Wqkv_b"][D:D + HD0].rearrange("(p a) -> p a", a=1)) for i in range(3)],
                *[(bv[:, i, :], dram["Wqkv_b"][D + HD0:].rearrange("(a n) -> a n", a=1).partition_broadcast(P)) for i in range(2)],
                *[(t[:, m:m + 1], dram[n][at:at + P].rearrange("(p a) -> p a", a=1))
                  for t, n in ((s_gate, "s_gate"), (s_up, "s_up")) for m, at in enumerate(HT)],
                (s_down[:], dram["s_down"].rearrange("(a n) -> a n", a=1).partition_broadcast(P)),
                (raw_down[:, 0:5, :], dram["wdownT"][0:5 * P, :].rearrange("(m p) n -> p m n", p=P)),
                (raw_down[DUP_H:, 5, :], dram["wdownT"][5 * P:, :]),
                (raw_s2[:, 0:2, :], dram["sw2T"][0:2 * P, :].rearrange("(m p) n -> p m n", p=P)),
                (raw_s2[DUP_S:, 2, :], dram["sw2T"][2 * P:, :]),
                (raw_gw[:], dram["gate_wT"].rearrange("(c p) n -> p c n", p=P)),
                (raw_int[:], dram["wgateT"].rearrange("(c p) n -> p c n", p=P)),
            ]
            FIRST = 16 * len(loads)

            splits = [(raw_qkv[:], w_qkv[0][:], w_qkv[1][:]), (raw_o[:], w_o[0][:], w_o[1][:]), (raw_ob[:], ob[0][:], ob[1][:]),
                      (raw_s2[:], w_s2[0][:], w_s2[1][:]),
                      (raw_gw[:], w_gw[0][:], w_gw[1][:]),
                      (raw_s13, w_s13[0][:], w_s13[1][:])]

            @block.sync
            def _(sp):
                for dst, src in loads:
                    sp.dma_start(dst, src).then_inc(raw_in, 16)
                sp.wait_ge(prep_dve, 1)
                sp.dma_start(raw_int[:], dram["wupT"].rearrange("(c p) n -> p c n", p=P)).then_inc(raw_in, 16)
                sp.wait_ge(prep_dve, 2)
                for i, n in enumerate(("sw1T", "sw3T")):
                    sp.dma_start(raw_s13[:, :, SHARED * i:SHARED * (i + 1)],
                                 dram[n].rearrange("(c p) n -> p c n", p=P)).then_inc(raw_in, 16)

            @block.gpsimd
            def _(pool):
                pool.memset(ident[:], 0.0).then_inc(const_ok, 1)
                pool.memset(mask_f[:], 0.0).then_inc(const_ok, 1)
                pool.memset(ones_f[:], 1.0).then_inc(const_ok, 1)
                pool.wait_ge(const_ok, 3)
                pool.affine_select(out=ident[:], in_=ident[:], compare_op=ALU.not_equal, fill=1.0, base=0,
                                   pattern=[[-1, P]], channel_multiplier=1).then_inc(const_ok, 1)
                pool.memset(raw_down[0:DUP_H, 5, :], int(ZERO_POINT)).then_inc(const_ok, 1)
                pool.memset(raw_s2[0:DUP_S, 2, :], 0.0).then_inc(const_ok, 1)
                pool.affine_select(out=mask_f[:], in_=mask_f[:], compare_op=ALU.is_ge, fill=MASKED, base=0,
                                   pattern=[[0, 4], [-1, P]], channel_multiplier=1).then_inc(const_ok, 1)

            @block.scalar
            def _(act):
                act.wait_ge(const_ok, 7)
                act.activation(ident_r[:], ident[:], ACT.Copy).then_inc(prep_act, 1)
                act.activation(mask_r[:], mask_f[:], ACT.Copy).then_inc(prep_act, 1)
                act.activation(ones_r[:], ones_f[:], ACT.Copy).then_inc(prep_act, 1)
                act.wait_ge(prep_dve, 3)
                for n, (raw, high, _) in enumerate(splits):
                    if n == len(splits) - 1:
                        act.wait_ge(raw_in, FIRST + 48)
                    act.activation(high, raw, ACT.Copy).then_inc(prep_act, 1)

            @block.vector
            def _(dve):
                dve.wait_ge(raw_in, FIRST)
                dve.tensor_scalar(w_gate[:], raw_int[:], ZERO_POINT, None, ALU.subtract).then_inc(prep_dve, 1)
                dve.wait_ge(raw_in, FIRST + 16)
                dve.tensor_scalar(w_up[:], raw_int[:], ZERO_POINT, None, ALU.subtract).then_inc(prep_dve, 1)
                dve.tensor_scalar(raw_qkv[:, :, 0:D], raw_qkv[:, :, 0:D], HD0 ** -0.5, None, ALU.mult).then_inc(prep_dve, 1)
                dve.tensor_scalar(bq[:], bq[:], HD0 ** -0.5, None, ALU.mult).then_inc(prep_dve, 1)
                dve.wait_ge(const_ok, 7)
                dve.tensor_scalar(w_down[:], raw_down[:], ZERO_POINT, None, ALU.subtract).then_inc(prep_dve, 1)
                dve.tensor_scalar(half_gate[:], s_gate[:], 0.5, None, ALU.mult).then_inc(prep_dve, 1)
                dve.wait_ge(prep_dve, 6)
                dve.tensor_tensor(scale_h[:], half_gate[:], s_up[:], ALU.mult).then_inc(prep_dve, 1)
                for n, (raw, high, low) in enumerate(splits):
                    dve.wait_ge(prep_act, 4 + n)
                    dve.tensor_tensor(low, raw, high.bitcast(F32), ALU.subtract).then_inc(prep_dve, 1)

        x_in = sb("x_in", [P, TP, D])
        stats = sb("stats", [P, 2 * TP, 6])
        mv = sb("mv", [P, 2 * TP, 2])
        var_eps = sb("var_eps", [P, 2 * TP])
        rstd = sb("rstd", [P, 2 * TP])
        minus_half = sb("minus_half", [P, 2 * TP])
        xn = sb("xn", [P, TP, D])
        xnT = [sb(f"xnT{i}", [P, DC, PAIR], R32) for i in range(2)]
        qT = [sb(f"qT{i}", [P, DC, PAIR], R32) for i in range(2)]
        q3 = sb("q3", [48, HEADS0, PAIR], R32)
        k3 = sb("k3", [48, 2, SEQ], R32)
        vf = sb("vf", [P, 2, 2, HD0])
        vs = sb("vs", [P, TP, 2, HD0], R32)
        neg_max = sb("neg_max", [P, 2, 4])
        sums = sb("sums", [P, TP, HEADS0])
        probs = sb("probs", [P, 2, 512])
        pT = [sb(f"pT{i}", [P, 2, 512], R32) for i in range(2)]
        ctx_f = sb("ctx_f", [P, HEADS0, HD0])
        rinv = sb("rinv", [P, HEADS0])
        ctx_n = sb("ctx_n", [P, D])
        cT = [sb(f"cT{i}", [P, TP, DC, P], R32) for i in range(2)]
        tanh_g = sb("tanh_g", [P, 2, PAIR])
        gated = sb("gated", [P, 2, PAIR])
        h_f = sb("h_f", [P, 2, PAIR])
        hT = [sb(f"hT{i}", [P, len(HT), PAIR], R32) for i in range(2)]
        sT = [sb(f"sT{i}", [P, len(ST), PAIR], R32) for i in range(2)]
        down_f = sb("down_f", [P, D])
        both_f = sb("both_f", [P, D])
        x1 = sb("x1", [P, TP, D])
        xn1 = sb("xn1", [P, TP, D])
        xn1T = [sb(f"xn1T{i}", [P, DC, PAIR], R32) for i in range(2)]
        lg = sb("lg", [P, TP, EXPERTS])

        ps_m = [psum(f"ps_m{i}") for i in range(3)]
        ps_s = [psum(f"ps_s{i}") for i in range(2)]
        ps_t = psum("ps_t")
        ps_c = psum("ps_c")

        units = []
        for s in range(2):
            units += [(s, 0, h, 4) for h in range(0, HEADS0, 4)]
            units += [(s, 1, h, 2) for h in range(0, HEADS0, 2)]
        NU = len(units)
        last_unit = {(s, t): max(n for n, u in enumerate(units) if u[:2] == (s, t)) for s, t, _, _ in units}
        steps = [[] for _ in range(NU + 3)]
        for n in range(2 * len(HT)):
            steps[n].append(("ffn", n))
        for (s, t), n in last_unit.items():
            steps[n + 3].append(("ctx", 2 * s + t))
        for n, at in enumerate((15, 16, 20, NU + 2)):
            steps[at].append(("out", n))
        for n, at in enumerate((18, 19, 22, NU + 2)):
            steps[at].append(("norm", n))
        front = [("xT", 0), ("xT", 1), ("q", 0), ("q", 1), ("k", 0), ("v", 0), ("k", 1), ("v", 1)]
        back = [("ffs", n) for n in range(2 * len(ST))] + [("sum", n) for n in range(TP)]
        order = front + [i for step in steps for i in step] + back
        NI = len(order)
        assert NI % len(ps_m) == 0 and NU % 2 == 0
        number = {item: n for n, item in enumerate(order)}
        acted = [i for i in order if i[0] in ("xT", "q", "k", "ctx", "norm") or (i[0] in ("ffn", "ffs") and i[1] % 2 == 0)]
        act_number = {item: n for n, item in enumerate(acted)}
        NH = len(HT) + len(ST)
        LINKS = 4 + 8 * TP

        def bank(item):
            return ps_m[number[item] % len(ps_m)]

        own = Signal(sem("dve_own"), 0)
        x_got = Signal(sem("x_got"), 16)
        var_ok = Signal(sem("var_ok"), 1 + TP)
        half_ok = sem("half_ok")
        rstd_ok = Signal(sem("rstd_ok"), 1 + TP)
        ln_done = Signal(sem("ln_done"), TP)
        item_full = Signal(sem("item_full"), NI)
        item_act = Signal(sem("item_act"), len(acted))
        item_done = Signal(sem("item_done"), NI, len(ps_m))
        q_out = Signal(sem("q_out"), 32 * DC)
        q3_got = Signal(sem("q3_got"), 48)
        s_full = Signal(sem("s_full"), NU)
        max_ok = Signal(sem("max_ok"), NU)
        p_ok = Signal(sem("p_ok"), NU, 2)
        t_full = Signal(sem("t_full"), NU)
        t_high = Signal(sem("t_high"), NU)
        t_low = Signal(sem("t_low"), NU, 1)
        pv_ok = Signal(sem("pv_ok"), NU, 2)
        ctx_free = Signal(sem("ctx_free"), TP, 1)
        ctx_ok = Signal(sem("ctx_ok"), TP)
        norm1_ok = Signal(sem("norm1_ok"), TP)
        h_high = Signal(sem("h_high"), NH)
        h_low = Signal(sem("h_low"), NH, 2)
        stored = Signal(sem("stored"), 80, 1)

        block = ctx.enter_context(nc.Block())

        @block.sync
        def _(sp):
            sp.dma_start(x_in[:], dram["x"][0:PAIR, :].rearrange("(t p) n -> p t n", p=P)).then_inc(x_got.sem, 16)
            sp.sem_inc(stored.sem, 1)
            with sp.Fori(0, TURNS) as p:
                for c in range(DC):
                    sp.wait_ge(item_done.sem, item_done.at(p, number["q", c] + 1))
                    for i in range(2):
                        sp.dma_start(dram["q_scr"][i, c * P:(c + 1) * P, :], qT[i][:, c, :].bitcast(F32)).then_inc(q_out.sem, 16)
                sp.wait_ge(q_out.sem, q_out.at(p, 32 * DC))
                sp.wait_ge(p_ok.sem, p_ok.at(p, 0))
                for r, i in enumerate((0, 1, 0)):
                    sp.dma_start(q3[HD0 * r:HD0 * (r + 1), :, :].bitcast(F32),
                                 dram["q_scr"][i].rearrange("(h d) t -> d h t", d=HD0)).then_inc(q3_got.sem, 16)
                sp.wait_ge(item_done.sem, item_done.at(p, number["norm", TP - 1] + 1))
                sp.dma_start(x_in[:], dram["x"].rearrange("(u t p) n -> u p t n", t=TP, p=P)[ds((p + 1) % TURNS, 1)]
                             .rearrange("o p t n -> (o p) t n")).then_inc(x_got.sem, 16)
                sp.dma_start(dram["xn1"][ds(p, 1)].rearrange("o p n -> (o p) n"),
                             xn1[:].rearrange("p t n -> p (t n)")).then_inc(stored.sem, 16)
                for i in range(2):
                    sp.dma_start(dram["xn1T"][ds(2 * p + i, 1)].rearrange("o p n -> (o p) n"),
                                 xn1T[i][:].bitcast(F32).rearrange("p c n -> p (c n)")).then_inc(stored.sem, 16)
                sp.wait_ge(item_done.sem, item_done.at(p, NI))
                sp.dma_start(dram["x1"][ds(p, 1)].rearrange("o p n -> (o p) n"),
                             x1[:].rearrange("p t n -> p (t n)")).then_inc(stored.sem, 16)
                sp.dma_start(dram["logits"][ds(p, 1)].rearrange("o p n -> (o p) n"),
                             lg[:].rearrange("p t n -> p (t n)")).then_inc(stored.sem, 16)
            sp.wait_ge(stored.sem, stored.at(TURNS, 0))
            sp.wait_ge(x_got.sem, 16 * (TURNS + 1))

        @block.gpsimd
        def _(pool):
            pool.sem_inc(h_low.sem, 2)
            pool.memset(minus_half[:], -0.5).then_inc(half_ok, 1)
            pool.wait_ge(half_ok, 1)

            def inverse_root(p, n, k):
                pool.wait_ge(var_ok.sem, var_ok.at(p, n + 1))
                at = 0 if n == 0 else TP - 1 + n
                pool.tensor_tensor(rstd[:, at:at + k], var_eps[:, at:at + k], minus_half[:, at:at + k], ALU.pow).then_inc(rstd_ok.sem, 1)

            with pool.Fori(0, TURNS) as p:
                inverse_root(p, 0, TP)
                for n, ((high, low), m) in enumerate([(hT, m) for m in range(len(HT))] + [(sT, m) for m in range(len(ST))]):
                    if n == len(HT):
                        for i in range(TP):
                            inverse_root(p, 1 + i, 1)
                    pool.wait_ge(h_high.sem, h_high.at(p, n + 1))
                    pool.tensor_tensor(low[:, m, :], h_f[:, n % 2, :], high[:, m, :].bitcast(F32),
                                       ALU.subtract).then_inc(h_low.sem, 1)

        @block.scalar
        def _(act):
            act.sem_inc(p_ok.sem, 2)

            def exps(p, n):
                s, t, h0, nh = units[n]
                w = (t + 1) * P
                act.wait_ge(max_ok.sem, max_ok.at(p, n + 1))
                for h in range(nh):
                    last = act.activation(probs[:, n % 2, h * w:(h + 1) * w], ps_s[n % 2][:, h * w:(h + 1) * w], ACT.Exp,
                                          bias=neg_max[:, n % 2, h:h + 1], scale=1.0,
                                          accum_out=sums[:, 2 * s + t, h0 + h:h0 + h + 1])
                last.then_inc(p_ok.sem, 1)

            def high_probs(p, n):
                act.wait_ge(t_full.sem, t_full.at(p, n + 1))
                act.wait_ge(pv_ok.sem, pv_ok.at(p, n - 1))
                act.activation(pT[0][:, n % 2, :], ps_t[:], ACT.Copy).then_inc(t_high.sem, 1)

            def tanh_of(p, item, m, scale):
                act.wait_ge(item_full.sem, item_full.at(p, number[item] + 1))
                act.activation(tanh_g[:, m % 2, :], bank(item)[:], ACT.Tanh, scale=scale).then_inc(item_act.sem, 1)

            def high_hidden(p, item, m, n, dst):
                act.wait_ge(item_done.sem, item_done.at(p, number[item] + 1))
                act.activation(dst[:, m, :], h_f[:, n % 2, :], ACT.Copy).then_inc(h_high.sem, 1)

            def high_of(p, item, dst, src, bias=None):
                act.wait_ge(item_full.sem, item_full.at(p, number[item] + 1))
                if bias is None:
                    act.activation(dst, src, ACT.Copy).then_inc(item_act.sem, 1)
                else:
                    act.activation(dst, src, ACT.Identity, bias=bias).then_inc(item_act.sem, 1)

            with act.Fori(0, TURNS) as p:
                for c in range(DC):
                    high_of(p, ("xT", c), xnT[0][:, c, :], bank(("xT", c))[:])
                for c in range(DC):
                    high_of(p, ("q", c), qT[0][:, c, :], bank(("q", c))[:], bq[:, c:c + 1])
                for s in range(2):
                    high_of(p, ("k", s), k3[:, s, :], bank(("k", s))[0:48, 0:SEQ], bk[:])
                for n, step in enumerate(steps):
                    if n < NU:
                        exps(p, n)
                    if n >= 2 and n % 2 == 0 and n // 2 - 1 < len(HT):
                        m = n // 2 - 1
                        high_hidden(p, ("ffn", n - 1), m, m, hT[0])
                    for kind, i in step:
                        if kind == "ffn" and i % 2 == 0:
                            tanh_of(p, (kind, i), i // 2, half_gate[:, i // 2:i // 2 + 1])
                    if 1 <= n <= NU:
                        high_probs(p, n - 1)
                    for kind, i in step:
                        if kind == "ctx":
                            high_of(p, (kind, i), cT[0][:, i, :, :].rearrange("p c n -> p (c n)"), bank((kind, i))[:, 0:D])
                        if kind == "norm":
                            if i == 0:
                                act.wait_ge(stored.sem, stored.at(p, 0))
                            high_of(p, (kind, i), xn1T[0][:, :, i * P:(i + 1) * P],
                                    bank((kind, i))[:, 0:D].rearrange("p (c n) -> p c n", c=DC))
                for m in range(len(ST)):
                    if m >= 1:
                        high_hidden(p, ("ffs", 2 * m - 1), m - 1, len(HT) + m - 1, sT[0])
                    tanh_of(p, ("ffs", 2 * m), m, 0.5)
                high_hidden(p, ("ffs", 2 * len(ST) - 1), len(ST) - 1, NH - 1, sT[0])

        @block.vector
        def _(dve):
            dve.sem_inc(item_done.sem, len(ps_m))
            dve.sem_inc(t_low.sem, 1)
            dve.sem_inc(ctx_free.sem, 1)

            per_turn = [0]

            def link(p, ins):
                per_turn[0] += 1
                ins.then_inc(own.sem, 1)
                dve.wait_ge(own.sem, own.at(p, per_turn[0]))

            def count(ins):
                per_turn[0] += 1
                ins.then_inc(own.sem, 1)

            def settle(p):
                dve.wait_ge(own.sem, own.at(p, per_turn[0]))

            def norm(p, n, xs, outs, done):
                k = len(xs)
                at = 0 if n == 0 else TP - 1 + n
                for t in range(k):
                    count(dve.bn_stats(stats[:, at + t, :], xs[t]))
                settle(p)
                dve.memset(var_eps[:, at:at + k], 0.0)
                for t in range(k):
                    count(dve.bn_aggr(mv[:, at + t, :], stats[:, at + t, :]))
                settle(p)
                dve.tensor_scalar(var_eps[:, at:at + k], mv[:, at:at + k, 1], EPS, None, ALU.add).then_inc(var_ok.sem, 1)
                dve.wait_ge(rstd_ok.sem, rstd_ok.at(p, n + 1))
                for t in range(k):
                    dve.tensor_scalar(outs[t], xs[t], mv[:, at + t, 0:1], rstd[:, at + t:at + t + 1], ALU.subtract, ALU.mult)\
                        .then_inc(done.sem, 1)

            def low_of(p, item, dst, src, high, bias=None):
                dve.wait_ge(item_act.sem, item_act.at(p, act_number[item] + 1))
                if bias is None:
                    dve.tensor_tensor(dst, src, high.bitcast(F32), ALU.subtract).then_inc(item_done.sem, 1)
                else:
                    dve.scalar_tensor_tensor(out=dst, in0=src, scalar=bias, in1=high.bitcast(F32), op0=ALU.add,
                                             op1=ALU.subtract).then_inc(item_done.sem, 1)

            def gate_tile(p, item, m):
                dve.wait_ge(item_act.sem, item_act.at(p, act_number[item] + 1))
                dve.scalar_tensor_tensor(out=gated[:, m % 2, :], in0=tanh_g[:, m % 2, :], scalar=1.0, in1=bank(item)[:],
                                         op0=ALU.add, op1=ALU.mult).then_inc(item_done.sem, 1)

            def up_tile(p, item, n, scale):
                dve.wait_ge(item_full.sem, item_full.at(p, number[item] + 1))
                dve.wait_ge(item_done.sem, item_done.at(p, number[item[0], item[1] - 1] + 1))
                dve.wait_ge(h_low.sem, h_low.at(p, n - 1))
                dve.scalar_tensor_tensor(out=h_f[:, n % 2, :], in0=bank(item)[:], scalar=scale, in1=gated[:, item[1] // 2 % 2, :],
                                         op0=ALU.mult, op1=ALU.mult).then_inc(item_done.sem, 1)

            def context(p, s, t):
                n = last_unit[s, t]
                dve.wait_ge(pv_ok.sem, pv_ok.at(p, n + 1))
                dve.tensor_reduce(ctx_f[:], ps_c[:].rearrange("p (h i d) -> p h d i", i=2, d=HD0), AX.X, ALU.add)\
                    .then_inc(ctx_free.sem, 1)
                link(p, dve.reciprocal(rinv[:], sums[:, 2 * s + t, :]))
                dve.wait_ge(ctx_free.sem, ctx_free.at(p, 2 * s + t + 1))
                dve.tensor_tensor(ctx_n[:].rearrange("p (h d) -> p h d", h=HEADS0), ctx_f[:],
                                  rinv[:].unsqueeze(2).to_broadcast([P, HEADS0, HD0]), ALU.mult).then_inc(ctx_ok.sem, 1)

            def body(p):
                dve.wait_ge(x_got.sem, x_got.at(p, 16))
                norm(p, 0, [x_in[:, t, :] for t in range(TP)], [xn[:, t, :] for t in range(TP)], ln_done)
                for c in range(DC):
                    low_of(p, ("xT", c), xnT[1][:, c, :], bank(("xT", c))[:], xnT[0][:, c, :])
                for c in range(DC):
                    low_of(p, ("q", c), qT[1][:, c, :], bank(("q", c))[:], qT[0][:, c, :], bq[:, c:c + 1])
                for s in range(2):
                    low_of(p, ("k", s), k3[32:48, s, :], bank(("k", s))[32:48, 0:SEQ], k3[32:48, s, :], bk[32:48, :])
                    dve.wait_ge(item_full.sem, item_full.at(p, number["v", s] + 1))
                    link(p, dve.tensor_tensor(vf[:, s], bank(("v", s))[:, 0:2 * HD0].rearrange("p (t d) -> p t d", t=2), bv[:], ALU.add))
                    link(p, dve.tensor_copy(vs[:, 2 * s:2 * s + 2, 0, :], vf[:, s]))
                    dve.tensor_tensor(vs[:, 2 * s:2 * s + 2, 1, :], vf[:, s], vs[:, 2 * s:2 * s + 2, 0, :].bitcast(F32), ALU.subtract)\
                        .then_inc(item_done.sem, 1)
                for n, step in enumerate(steps):
                    if n < NU:
                        s, t, h0, nh = units[n]
                        dve.wait_ge(s_full.sem, s_full.at(p, n + 1))
                        dve.tensor_reduce(neg_max[:, n % 2, 0:nh], ps_s[n % 2][:].rearrange("p (h k) -> p h k", h=nh), AX.X,
                                          ALU.max, negate=True).then_inc(max_ok.sem, 1)
                    for item in step:
                        if item[0] == "ffn":
                            m = item[1] // 2
                            if item[1] % 2 == 0:
                                gate_tile(p, item, m)
                            else:
                                up_tile(p, item, m, scale_h[:, m:m + 1])
                    if 1 <= n <= NU:
                        dve.wait_ge(t_high.sem, t_high.at(p, n))
                        dve.tensor_tensor(pT[1][:, (n - 1) % 2, :], ps_t[:], pT[0][:, (n - 1) % 2, :].bitcast(F32), ALU.subtract)\
                            .then_inc(t_low.sem, 1)
                    if n >= 2:
                        for (s, t), last in last_unit.items():
                            if last == n - 2:
                                context(p, s, t)
                    for item in step:
                        kind, i = item
                        if kind == "ctx":
                            low_of(p, item, cT[1][:, i, :, :].rearrange("p c n -> p (c n)"), bank(item)[:, 0:D],
                                   cT[0][:, i, :, :].rearrange("p c n -> p (c n)"))
                        if kind == "out":
                            dve.wait_ge(item_full.sem, item_full.at(p, number[item] + 1))
                            link(p, dve.tensor_tensor(down_f[:], bank(item)[:, D:2 * D], s_down[:], ALU.mult))
                            dve.tensor_tensor(both_f[:], bank(item)[:, 0:D], down_f[:], ALU.add).then_inc(item_done.sem, 1)
                            dve.wait_ge(item_done.sem, item_done.at(p, number[item] + 1))
                            if i == 0:
                                dve.wait_ge(stored.sem, stored.at(p, 0))
                            link(p, dve.tensor_tensor(x1[:, i, :], x_in[:, i, :], both_f[:], ALU.add))
                            norm(p, 1 + i, [x1[:, i, :]], [xn1[:, i, :]], norm1_ok)
                        if kind == "norm":
                            low_of(p, item, xn1T[1][:, :, i * P:(i + 1) * P],
                                   bank(item)[:, 0:D].rearrange("p (c n) -> p c n", c=DC), xn1T[0][:, :, i * P:(i + 1) * P])
                for m in range(len(ST)):
                    gate_tile(p, ("ffs", 2 * m), m)
                    up_tile(p, ("ffs", 2 * m + 1), len(HT) + m, 0.5)
                for i in range(TP):
                    dve.wait_ge(item_full.sem, item_full.at(p, number["sum", i] + 1))
                    link(p, dve.tensor_copy(lg[:, i, :], bank(("sum", i))[:, D:D + EXPERTS]))
                    dve.tensor_tensor(x1[:, i, :], x1[:, i, :], bank(("sum", i))[:, 0:D], ALU.add).then_inc(item_done.sem, 1)

            own.per_turn = LINKS
            with dve.Fori(0, TURNS) as p:
                body(p)
            assert per_turn[0] == LINKS, per_turn[0]

        @block.tensor
        def _(pe):
            pe.sem_inc(pv_ok.sem, 2)

            def product3(out, lhs, rhs, start, stop):
                for n, (i, j) in enumerate(((0, 0), (0, 1), (1, 0))):
                    last = pe.matmul(out, lhs[i], rhs[j], start=start and n == 0, stop=stop and n == 2, skip_group_check=True)
                return last

            def body(p):
                def begin(item):
                    pe.wait_ge(item_done.sem, item_done.at(p, number[item] + 1 - len(ps_m)))
                    return bank(item)

                def full(last):
                    last.then_inc(item_full.sem, 1)

                def after(item):
                    pe.wait_ge(item_done.sem, item_done.at(p, number[item] + 1))

                for c in range(DC):
                    out = begin(("xT", c))
                    for t in range(TP):
                        if c == 0:
                            pe.wait_ge(ln_done.sem, ln_done.at(p, t + 1))
                        last = pe.transpose(out[:, t * P:(t + 1) * P], xn[:, t, c * P:(c + 1) * P], ident[:])
                    full(last)
                after(("xT", 1))
                for m in range(DC):
                    out = begin(("q", m))
                    for c in range(DC):
                        last = product3(out[:], [w[:, c, m * P:(m + 1) * P] for w in w_qkv], [x[:, c, :] for x in xnT],
                                        c == 0, c == DC - 1)
                    full(last)
                for s in range(2):
                    out = begin(("k", s))
                    for c in range(DC):
                        last = product3(out[:, 0:SEQ], [w[:, c, D:D + P] for w in w_qkv],
                                        [x[:, c, s * SEQ:(s + 1) * SEQ] for x in xnT], c == 0, c == DC - 1)
                    full(last)
                    out = begin(("v", s))
                    for t in range(2):
                        for c in range(DC):
                            last = product3(out[:, t * HD0:(t + 1) * HD0],
                                            [x[:, c, (2 * s + t) * P:(2 * s + t + 1) * P] for x in xnT],
                                            [w[:, c, D + P:] for w in w_qkv], c == 0, c == DC - 1)
                    full(last)

                def scores(n):
                    s, t, h0, nh = units[n]
                    w = (t + 1) * P
                    out = ps_s[n % 2]
                    pe.wait_ge(p_ok.sem, p_ok.at(p, n - 1))
                    by_head = out[:].rearrange("p (h k) -> p h k", h=nh)
                    pe.matmul(by_head[:, :, t * P:w], ident_r[:], mask_r[:, 0:nh, :], start=True, stop=False, skip_group_check=True)
                    for h in range(nh):
                        last = pe.matmul(out[:, h * w:(h + 1) * w], q3[:, h0 + h, (2 * s + t) * P:(2 * s + t + 1) * P],
                                         k3[:, s, 0:w], start=False, stop=(h == nh - 1), skip_group_check=True)
                    last.then_inc(s_full.sem, 1)

                def transposes(n):
                    pe.wait_ge(p_ok.sem, p_ok.at(p, n + 1))
                    pe.wait_ge(t_low.sem, t_low.at(p, n))
                    for b in range(4):
                        last = pe.transpose(ps_t[:, b * P:(b + 1) * P], probs[:, n % 2, b * P:(b + 1) * P], ident[:])
                    last.then_inc(t_full.sem, 1)

                def context(n):
                    s, t, h0, nh = units[n]
                    pe.wait_ge(t_low.sem, t_low.at(p, n + 1))
                    if h0 == 0:
                        pe.wait_ge(ctx_free.sem, ctx_free.at(p, 2 * s + t))
                    for h in range(nh):
                        at = (h0 + h) * 2 * HD0
                        for k in range(t + 1):
                            b = h * (t + 1) + k
                            v = vs[:, 2 * s + k, :, :].rearrange("p i d -> p (i d)")
                            pe.matmul(ps_c[:, at:at + 2 * HD0], pT[0][:, n % 2, b * P:(b + 1) * P], v,
                                      start=(h0 + h == 0 and k == 0), stop=False, skip_group_check=True)
                            last = pe.matmul(ps_c[:, at:at + HD0], pT[1][:, n % 2, b * P:(b + 1) * P], v[:, 0:HD0],
                                             start=False, stop=(h0 + h == HEADS0 - 1 and k == t), skip_group_check=True)
                    last.then_inc(pv_ok.sem, 1)

                def item_work(item):
                    kind, i = item
                    if kind == "norm":
                        pe.wait_ge(norm1_ok.sem, norm1_ok.at(p, i + 1))
                    if kind == "ctx":
                        pe.wait_ge(ctx_ok.sem, ctx_ok.at(p, i + 1))
                    if kind == "out":
                        after(("ctx", i))
                        if i == 0:
                            pe.wait_ge(h_low.sem, h_low.at(p, len(HT)))
                    out = begin(item)
                    if kind == "ffn":
                        w = w_gate if i % 2 == 0 else w_up
                        for c in range(DC):
                            for j in range(2):
                                last = pe.matmul(out[:], w[:, c, HT[i // 2]:HT[i // 2] + P], xnT[j][:, c, :],
                                                 start=(c == 0 and j == 0), stop=(c == DC - 1 and j == 1))
                    if kind in ("ctx", "norm"):
                        src = ctx_n[:] if kind == "ctx" else xn1[:, i, :]
                        for c in range(DC):
                            last = pe.transpose(out[:, c * P:(c + 1) * P], src[:, c * P:(c + 1) * P], ident[:])
                    if kind == "out":
                        pe.matmul(out[:, 0:D], ones_r[:], ob[0][:], start=True, stop=False, skip_group_check=True)
                        pe.matmul(out[:, 0:D], ones_r[:], ob[1][:], start=False, stop=False, skip_group_check=True)
                        for c in range(DC):
                            product3(out[:, 0:D], [x[:, i, c, :] for x in cT], [w[:, c, :] for w in w_o], False, False)
                        for m in range(len(HT)):
                            for j in range(2):
                                last = pe.matmul(out[:, D:2 * D], hT[j][:, m, i * P:(i + 1) * P], w_down[:, m, :],
                                                 start=False, stop=(m == len(HT) - 1 and j == 1), skip_group_check=True)
                    if kind == "ffs":
                        at = (i % 2) * SHARED + ST[i // 2]
                        for c in range(DC):
                            last = product3(out[:], [w[:, c, at:at + P] for w in w_s13], [x[:, c, :] for x in xn1T],
                                            c == 0, c == DC - 1)
                    if kind == "sum":
                        for m in range(len(ST)):
                            product3(out[:, 0:D], [x[:, m, i * P:(i + 1) * P] for x in sT], [w[:, m, :] for w in w_s2],
                                     m == 0, False)
                        for c in range(DC):
                            for a in range(2):
                                for b in range(2):
                                    last = pe.matmul(out[:, D:D + EXPERTS], xn1T[a][:, c, i * P:(i + 1) * P], w_gw[b][:, c, :],
                                                     start=False, stop=(c == DC - 1 and a + b == 2), skip_group_check=True)
                    full(last)

                pe.wait_ge(q3_got.sem, q3_got.at(p, 48))
                for n, step in enumerate(steps):
                    if n < NU:
                        scores(n)
                    for item in step:
                        if item[0] == "ffn":
                            item_work(item)
                    if 1 <= n <= NU:
                        transposes(n - 1)
                    if 2 <= n <= NU + 1:
                        context(n - 2)
                    for item in step:
                        if item[0] != "ffn":
                            item_work(item)
                after(("norm", TP - 1))
                for item in back:
                    if item == ("sum", 0):
                        pe.wait_ge(h_low.sem, h_low.at(p, NH))
                    item_work(item)

            with pe.Fori(0, TURNS) as p:
                body(p)

QKV_COLS = 6 * D
W_A = QKV_COLS + 4
W_B = 2 * D + 4


def stage_attention_weights(nc, dram):
    with ExitStack() as ctx:
        def sb(name, shape, dt=F32):
            return ctx.enter_context(nc.sbuf_tensor(name, shape, dt))

        def sem(name):
            return ctx.enter_context(nc.semaphore(name))

        MATS = ("wq", "wk", "wv", "wo")
        N = DC * FEAT
        codes = [sb(f"codes{i}", [P, N]) for i in range(2)]
        scales = [sb(f"scales{i}", [P, N]) for i in range(2)]
        high = [sb(f"high{i}", [P, N], R32) for i in range(2)]
        low = sb("low", [P, N], R32)
        rows = sb("rows", [3 * HEADS1, HD1])
        columns = sb("columns", [P, HEADS1, 8])
        ident = sb("ident_w", [P, P])
        ps = ctx.enter_context(nc.psum_tensor("ps_w", [P, 512], F32))

        got = [sem(f"w_got{i}") for i in range(4)]
        rows_got = sem("rows_got")
        id_ok = sem("id_ok")
        turned = sem("turned")
        columns_ok = sem("columns_ok")
        prod_ok = sem("prod_ok")
        high_ok = sem("high_ok")
        low_ok = sem("low_ok")
        low_out = sem("low_out")
        out = [sem(f"w_out{i}") for i in range(2)]
        block = ctx.enter_context(nc.Block())

        @block.sync
        def _(sp):
            for m in range(3):
                sp.dma_start(rows[m * HEADS1:(m + 1) * HEADS1, :], dram["b" + "qkv"[m]].rearrange("(h p) -> h p", p=HD1))\
                    .then_inc(rows_got, 16)
            for n, m in enumerate(MATS):
                if n >= 2:
                    sp.wait_ge(low_ok, n - 1)
                c, sc = dram[m + "_codes"], dram[m + "_scales"]
                if m == "wo":
                    sp.dma_start(codes[n % 2][:].rearrange("p (h n) -> p h n", h=HEADS1), c.rearrange("(h p) n -> p h n", p=P))\
                        .then_inc(got[n], 16)
                else:
                    sp.dma_start(codes[n % 2][:].rearrange("p (c n) -> p c n", c=DC), c.rearrange("(c p) n -> p c n", p=P))\
                        .then_inc(got[n], 16)
                chunks = HEADS1 if m == "wo" else DC
                for b in range(P // BLOCK):
                    src = sc.rearrange("(c b) n -> b c n", b=P // BLOCK)[b:b + 1].partition_broadcast(BLOCK)
                    sp.dma_start(scales[n % 2][b * BLOCK:(b + 1) * BLOCK, :].rearrange("p (c n) -> p c n", c=chunks),
                                 src.rearrange("q o c n -> q (o c) n")).then_inc(got[n], 16)

        @block.scalar
        def _(act):
            for n in range(4):
                act.wait_ge(prod_ok, n + 1)
                if n >= 2:
                    act.wait_ge(out[n % 2], 16 * (n // 2))
                if MATS[n] == "wo":
                    act.activation(high[n % 2][:], codes[n % 2][:], ACT.Copy).then_inc(high_ok, 1)
                else:
                    act.activation(high[n % 2][:].rearrange("p (h c n) -> p c h n", c=DC, n=HD1),
                                   codes[n % 2][:].rearrange("p (c h n) -> p c h n", c=DC, n=HD1), ACT.Copy).then_inc(high_ok, 1)
                act.wait_ge(high_ok, n + 1)
                act.dma_start(dram["w_head"][:, :, (2 * n) * D:(2 * n + 1) * D].rearrange("h p n -> p h n") if n < 3 else
                              dram["w_head"][:, :, W_A:W_A + D].rearrange("h p n -> p h n"),
                              high[n % 2][:].bitcast(F32).rearrange("p (h n) -> p h n", n=D)).then_inc(out[n % 2], 16)
            for i in range(2):
                act.wait_ge(out[i], 32)

        @block.gpsimd
        def _(pool):
            pool.memset(ident[:], 0.0).then_inc(id_ok, 1)
            pool.memset(columns[:], 0.0).then_inc(id_ok, 1)
            pool.wait_ge(id_ok, 2)
            pool.affine_select(out=ident[:], in_=ident[:], compare_op=ALU.not_equal, fill=1.0, base=0,
                               pattern=[[-1, P]], channel_multiplier=1).then_inc(id_ok, 1)
            for n in range(4):
                pool.wait_ge(low_ok, n + 1)
                at = (2 * n + 1) * D if n < 3 else W_A + D
                pool.dma_start(dram["w_head"][:, :, at:at + D].rearrange("h p n -> p h n"),
                               low[:].bitcast(F32).rearrange("p (h n) -> p h n", n=D)).then_inc(low_out, 16)
            pool.wait_ge(columns_ok, 3)
            for at, m in ((QKV_COLS, 0), (W_A + 2 * D, 4)):
                pool.dma_start(dram["w_head"][:, :, at:at + 4].rearrange("h p n -> p h n"), columns[:, :, m:m + 4])\
                    .then_inc(low_out, 16)
            pool.wait_ge(low_out, 96)

        @block.tensor
        def _(pe):
            pe.wait_ge(id_ok, 3)
            pe.wait_ge(rows_got, 48)
            pe.transpose(ps[:, 0:3 * HEADS1], rows[:], ident[0:3 * HEADS1, 0:3 * HEADS1]).then_inc(turned, 1)

        @block.vector
        def _(dve):
            dve.wait_ge(turned, 1)
            for m in range(3):
                dve.tensor_scalar(columns[:, :, m + m // 2 * 2], ps[:, m * HEADS1:(m + 1) * HEADS1], HD1 ** -0.5 if m == 0 else 1.0, None,
                                  ALU.mult).then_inc(columns_ok, 1)
            for n in range(4):
                dve.wait_ge(got[n], 80)
                dve.scalar_tensor_tensor(out=codes[n % 2][:], in0=codes[n % 2][:], scalar=HD1 ** -0.5 if n == 0 else 1.0,
                                         in1=scales[n % 2][:], op0=ALU.mult, op1=ALU.mult).then_inc(prod_ok, 1)
                dve.wait_ge(high_ok, n + 1)
                if n >= 1:
                    dve.wait_ge(low_out, 16 * n)
                if MATS[n] == "wo":
                    dve.tensor_tensor(low[:], codes[n % 2][:], high[n % 2][:].bitcast(F32), ALU.subtract).then_inc(low_ok, 1)
                else:
                    dve.tensor_tensor(low[:].rearrange("p (h c n) -> p c h n", c=DC, n=HD1),
                                      codes[n % 2][:].rearrange("p (c h n) -> p c h n", c=DC, n=HD1),
                                      high[n % 2][:].bitcast(F32).rearrange("p (h c n) -> p c h n", c=DC, n=HD1),
                                      ALU.subtract).then_inc(low_ok, 1)


def stage_attention(nc, dram):
    with ExitStack() as ctx:
        def sb(name, shape, dt=F32):
            return ctx.enter_context(nc.sbuf_tensor(name, shape, dt))

        def psum(name):
            return ctx.enter_context(nc.psum_tensor(name, [P, 512], F32))

        def sem(name):
            return ctx.enter_context(nc.semaphore(name))

        ident = sb("ident_a", [P, P])
        ones_f = sb("ones_fa", [1, P])
        ones_r = sb("ones_ra", [1, P], R32)
        raw_bo = sb("raw_bo", [1, 2, D])
        bo = [sb(f"bo{i}", [1, 2, D], R32) for i in range(2)]
        xT = [sb(f"xTa{i}", [P, DC, PAIR], R32) for i in range(2)]
        w_a = [sb(f"w_a{i}", [P, W_A], R32) for i in range(2)]
        w_b = [sb(f"w_b{i}", [P, W_B], R32) for i in range(2)]
        qT = [sb(f"qTa{i}", [P, PAIR], R32) for i in range(2)]
        kT = [sb(f"kTa{i}", [P, PAIR], R32) for i in range(2)]
        v = [[sb(f"v{i}_{a}", [P, TP, HD1], R32) for i in range(2)] for a in range(2)]
        probs = sb("probs_a", [P, 2, 2, SEQ])
        neg_max = sb("neg_max_a", [P, 2, 2])
        sums = sb("sums_a", [P, 2, 2])
        rinv = sb("rinv_a", [P, 2, 2])
        pT = [sb(f"pTa{i}", [P, 2, 512], R32) for i in range(2)]
        oT = [sb(f"oT{i}", [P, PAIR], R32) for i in range(2)]
        x1 = sb("x1a", [P, TP, D])
        x2 = sb("x2a", [P, TP, D])
        bank0, bank1 = psum("bank0"), psum("bank1")
        ps_s = [psum(f"ps_sa{i}") for i in range(2)]
        ps_t = [psum(f"ps_ta{i}") for i in range(2)]
        ps_y = [psum(f"ps_y{i}") for i in range(2)]

        H = HEADS1
        w_got = [sem(f"wa_got{a}") for a in range(2)]
        wb_got = [sem(f"wb_got{a}") for a in range(2)]
        x_got = Signal(sem("xa_got"), 48)
        x2_out = Signal(sem("x2_out"), 16, 1)
        prep = sem("prep_a")
        q_full, k_full, o_full = (Signal(sem(n), 1) for n in ("q_full", "k_full", "o_full"))
        v_full = Signal(sem("v_full"), 1, 2)
        y_done = Signal(sem("y_done"), 1, 2)
        q_high, k_high, v_high, o_high = (Signal(sem(n), 1) for n in ("q_high", "k_high", "v_high", "o_high"))
        q_done = Signal(sem("q_done"), 1)
        k_done = Signal(sem("k_done"), 1, 2)
        v_done, o_done = (Signal(sem(n), 1, 1) for n in ("v_done", "o_done"))
        s_full = Signal(sem("sa_full"), 2)
        max_ok = Signal(sem("maxa_ok"), 2)
        exp_ok = Signal(sem("exp_ok"), 2, 2)
        rinv_ok = Signal(sem("rinv_ok"), 2)
        p_ok = Signal(sem("pa_ok"), 2)
        t_full = Signal(sem("ta_full"), 2)
        t_high = Signal(sem("ta_high"), 2)
        t_low = Signal(sem("ta_low"), 2, 2)
        y_free = Signal(sem("y_free"), 1, 1)
        xo_ok = Signal(sem("xo_ok"), 2)

        block = ctx.enter_context(nc.Block())

        def walk(eng, step, start, end):
            with eng.Fori(0, TURNS) as u:
                start(u)
                for i in range(2):
                    step(u * H, i, i)
                with eng.Fori(0, (H - 2) // 2) as j:
                    for a in range(2):
                        step(u * H + j * 2, 2 + a, 2 + a)
                for i in range(H, H + 2):
                    step(u * H, i, i)
                end(u)


        def at(signal, base, i, n):
            return base * signal.per_turn + (signal.head + i * signal.per_turn + n)

        @block.sync
        def _(sp):
            for i in range(2):
                sp.dma_start(raw_bo[:, i, :], dram["bo"].rearrange("(a n) -> a n", a=1)).then_inc(prep, 16)
            with sp.Fori(0, TURNS) as u:
                sp.wait_ge(v_full.sem, at(v_full, u * H, 0, 0))
                for i in range(2):
                    sp.dma_start(xT[i][:].bitcast(F32).rearrange("p c n -> p (c n)"),
                                 dram["xn1T"][ds(2 * u + i, 1)].rearrange("o p n -> (o p) n")).then_inc(x_got.sem, 16)
                sp.wait_ge(x2_out.sem, x2_out.at(u, 0))
                sp.dma_start(x1[:].rearrange("p t n -> p (t n)"), dram["x1"][ds(u, 1)].rearrange("o p n -> (o p) n"))\
                    .then_inc(x_got.sem, 16)
                with sp.Fori(0, H // 2) as j:
                    for a in range(2):
                        base = u * H + j * 2
                        head = dram["w_head"][ds(j * 2 + a, 1)].rearrange("o p n -> (o p) n")
                        sp.wait_ge(v_full.sem, at(v_full, base, a - 2, 1))
                        sp.wait_ge(k_done.sem, at(k_done, base, a - 2, 1))
                        sp.dma_start(w_a[a][:].bitcast(F32), head[:, 0:W_A]).then_inc(w_got[a], 16)
                        sp.wait_ge(y_done.sem, at(y_done, base, a - 2, 1))
                        sp.dma_start(w_b[a][:].bitcast(F32), head[:, W_A:W_A + W_B]).then_inc(wb_got[a], 16)

        @block.gpsimd
        def _(pool):
            pool.memset(ident[:], 0.0).then_inc(prep, 1)
            pool.memset(ones_f[:], 1.0).then_inc(prep, 1)
            pool.wait_ge(prep, 34)
            pool.affine_select(out=ident[:], in_=ident[:], compare_op=ALU.not_equal, fill=1.0, base=0,
                               pattern=[[-1, P]], channel_multiplier=1).then_inc(prep, 1)

        @block.scalar
        def _(act):
            act.wait_ge(prep, 35)
            act.activation(ones_r[:], ones_f[:], ACT.Copy).then_inc(prep, 1)
            act.activation(bo[0][:], raw_bo[:], ACT.Copy).then_inc(prep, 1)
            act.sem_inc(exp_ok.sem, 2)

            def step(base, i, kind):
                a = i % 2
                now, back = kind < H, 1 <= kind <= H
                if now:
                    act.wait_ge(q_full.sem, at(q_full, base, i, 1))
                    act.activation(qT[0][:], bank0[:], ACT.Identity, bias=w_a[a][:, QKV_COLS:QKV_COLS + 1].bitcast(F32))\
                        .then_inc(q_high.sem, 1)
                    act.wait_ge(k_full.sem, at(k_full, base, i, 1))
                    act.activation(kT[0][:], bank1[:], ACT.Identity, bias=w_a[a][:, QKV_COLS + 1:QKV_COLS + 2].bitcast(F32))\
                        .then_inc(k_high.sem, 1)
                if back:
                    for s in range(2):
                        act.wait_ge(t_full.sem, at(t_full, base, i - 1, s + 1))
                        act.activation(pT[0][:, s, :], ps_t[s][:], ACT.Copy).then_inc(t_high.sem, 1)
                if now:
                    act.wait_ge(v_full.sem, at(v_full, base, i, 1))
                    act.activation(v[a][0][:].rearrange("p t n -> p (t n)"), bank0[:], ACT.Copy).then_inc(v_high.sem, 1)
                if back:
                    act.wait_ge(wb_got[1 - a], base * 8 + 16 * ((i - 1) // 2 + 1))
                    act.wait_ge(o_full.sem, at(o_full, base, i - 1, 1))
                    act.activation(oT[0][:], bank1[:], ACT.Identity, bias=w_b[1 - a][:, 2 * D:2 * D + 1].bitcast(F32))\
                        .then_inc(o_high.sem, 1)
                if now:
                    for s in range(2):
                        act.wait_ge(max_ok.sem, at(max_ok, base, i, s + 1))
                        for t in range(2):
                            last = act.activation(probs[:, s, t, :], ps_s[s][:, t * SEQ:(t + 1) * SEQ], ACT.Exp,
                                                  bias=neg_max[:, s, t:t + 1], scale=1.0, accum_out=sums[:, s, t:t + 1])
                        last.then_inc(exp_ok.sem, 1)

            def end(u):
                act.wait_ge(xo_ok.sem, xo_ok.at(u, 2))
                act.dma_start(dram["x1"][ds(u, 1)].rearrange("o p n -> (o p) n"), x2[:].rearrange("p t n -> p (t n)"))\
                    .then_inc(x2_out.sem, 16)

            act.sem_inc(x2_out.sem, 1)
            walk(act, step, lambda u: None, end)
            act.wait_ge(x2_out.sem, x2_out.at(TURNS, 0))

        @block.vector
        def _(dve):
            dve.wait_ge(prep, 37)
            dve.tensor_tensor(bo[1][:], raw_bo[:], bo[0][:].bitcast(F32), ALU.subtract).then_inc(prep, 1)
            dve.sem_inc(v_done.sem, 1)
            dve.sem_inc(k_done.sem, 2)
            dve.sem_inc(o_done.sem, 1)
            dve.sem_inc(t_low.sem, 2)
            dve.sem_inc(y_free.sem, 1)

            def low(dst, src, high, bias, signal):
                dve.scalar_tensor_tensor(out=dst, in0=src, scalar=bias, in1=high.bitcast(F32), op0=ALU.add,
                                         op1=ALU.subtract).then_inc(signal.sem, 1)

            def step(base, i, kind):
                a = i % 2
                now, back = kind < H, 1 <= kind <= H
                if now:
                    dve.wait_ge(q_high.sem, at(q_high, base, i, 1))
                    low(qT[1][:], bank0[:], qT[0][:], w_a[a][:, QKV_COLS:QKV_COLS + 1].bitcast(F32), q_done)
                    dve.wait_ge(k_high.sem, at(k_high, base, i, 1))
                    low(kT[1][:], bank1[:], kT[0][:], w_a[a][:, QKV_COLS + 1:QKV_COLS + 2].bitcast(F32), k_done)
                if back:
                    for s in range(2):
                        dve.wait_ge(t_high.sem, at(t_high, base, i - 1, s + 1))
                        dve.tensor_tensor(pT[1][:, s, :], ps_t[s][:], pT[0][:, s, :].bitcast(F32), ALU.subtract)\
                            .then_inc(t_low.sem, 1)
                if now:
                    dve.wait_ge(v_high.sem, at(v_high, base, i, 1))
                    dve.tensor_tensor(v[a][1][:].rearrange("p t n -> p (t n)"), bank0[:],
                                      v[a][0][:].bitcast(F32).rearrange("p t n -> p (t n)"), ALU.subtract).then_inc(v_done.sem, 1)
                if back:
                    dve.wait_ge(o_high.sem, at(o_high, base, i - 1, 1))
                    low(oT[1][:], bank1[:], oT[0][:], w_b[1 - a][:, 2 * D:2 * D + 1].bitcast(F32), o_done)
                if now:
                    for s in range(2):
                        dve.wait_ge(s_full.sem, at(s_full, base, i, s + 1))
                        dve.tensor_reduce(neg_max[:, s, :], ps_s[s][:].rearrange("p (t k) -> p t k", t=2), AX.X, ALU.max,
                                          negate=True).then_inc(max_ok.sem, 1)
                    for s in range(2):
                        dve.wait_ge(exp_ok.sem, at(exp_ok, base, i, s + 1))
                        dve.reciprocal(rinv[:, s, :], sums[:, s, :]).then_inc(rinv_ok.sem, 1)
                        dve.wait_ge(rinv_ok.sem, at(rinv_ok, base, i, s + 1))
                        for t in range(2):
                            last = dve.tensor_scalar(probs[:, s, t, :], probs[:, s, t, :], rinv[:, s, t:t + 1], None, ALU.mult)
                        last.then_inc(p_ok.sem, 1)

            def end(u):
                dve.wait_ge(y_done.sem, at(y_done, u * H, H, 0))
                dve.wait_ge(x_got.sem, x_got.at(u, 48))
                for b in range(2):
                    last = dve.tensor_tensor(x2[:, 2 * b:2 * b + 2, :].rearrange("p t n -> p (t n)"),
                                             x1[:, 2 * b:2 * b + 2, :].rearrange("p t n -> p (t n)"), ps_y[b][:], ALU.add)
                    last.then_inc(xo_ok.sem, 1)
                dve.wait_ge(xo_ok.sem, xo_ok.at(u, 2))
                dve.sem_inc(y_free.sem, 1)

            def start(u):
                dve.wait_ge(x2_out.sem, x2_out.at(u, 0))

            walk(dve, step, start, end)

        @block.tensor
        def _(pe):
            pe.wait_ge(prep, 38)
            pe.sem_inc(v_full.sem, 2)
            pe.sem_inc(y_done.sem, 2)

            def product3(out, lhs, rhs, start, stop):
                for n, (i, j) in enumerate(((0, 0), (0, 1), (1, 0))):
                    last = pe.matmul(out, lhs[i], rhs[j], start=start and n == 0, stop=stop and n == 2, skip_group_check=True)
                return last

            def w_part(a, m, c):
                return [w_a[a][:, (2 * m + i) * D + c * HD1:(2 * m + i) * D + (c + 1) * HD1] for i in range(2)]

            def project(out, a, m, signal):
                for c in range(DC):
                    last = product3(out[:], w_part(a, m, c), [x[:, c, :] for x in xT], c == 0, c == DC - 1)
                last.then_inc(signal.sem, 1)

            def step(base, i, kind):
                a = i % 2
                now, back, two_back = kind < H, 1 <= kind <= H, 2 <= kind
                if now:
                    pe.wait_ge(w_got[a], base * 8 + 16 * (i // 2 + 1))
                    pe.wait_ge(v_done.sem, at(v_done, base, i, 0))
                    project(bank0, a, 0, q_full)
                    if kind == 1:
                        pe.wait_ge(k_done.sem, at(k_done, base, i, 0))
                    else:
                        pe.wait_ge(o_done.sem, at(o_done, base, i, 0 if kind == 0 else -1))
                    project(bank1, a, 1, k_full)
                if back:
                    for s in range(2):
                        pe.wait_ge(p_ok.sem, at(p_ok, base, i - 1, s + 1))
                        pe.wait_ge(t_low.sem, at(t_low, base, i - 2, s + 1))
                        for k in range(2):
                            for t in range(2):
                                last = pe.transpose(ps_t[s][:, (2 * k + t) * P:(2 * k + t + 1) * P],
                                                    probs[:, s, t, k * P:(k + 1) * P], ident[:])
                        last.then_inc(t_full.sem, 1)
                if now:
                    pe.wait_ge(q_done.sem, at(q_done, base, i, 1))
                    for t in range(TP):
                        for c in range(DC):
                            last = product3(bank0[:, t * HD1:(t + 1) * HD1], [x[:, c, t * P:(t + 1) * P] for x in xT],
                                            w_part(a, 2, c), c == 0, c == DC - 1)
                    last.then_inc(v_full.sem, 1)
                if two_back:
                    pe.wait_ge(o_done.sem, at(o_done, base, i - 2, 1))
                    pe.wait_ge(wb_got[a], base * 8 + 16 * (i // 2))
                    for t in range(TP):
                        last = product3(ps_y[t // 2][:, (t % 2) * D:(t % 2 + 1) * D], [o[:, t * P:(t + 1) * P] for o in oT],
                                        [w_b[a][:, j * D:(j + 1) * D] for j in range(2)], False, kind == H + 1)
                    last.then_inc(y_done.sem, 1)
                if back:
                    if now:
                        pe.wait_ge(k_done.sem, at(k_done, base, i, 1))
                    else:
                        pe.wait_ge(o_done.sem, at(o_done, base, i - 1, 0))
                    pe.wait_ge(v_done.sem, at(v_done, base, i - 1, 1))
                    for s in range(2):
                        pe.wait_ge(t_low.sem, at(t_low, base, i - 1, s + 1))
                        for k in range(2):
                            last = product3(bank1[:, s * SEQ:(s + 1) * SEQ], [x[:, 2 * s + k, :] for x in v[1 - a]],
                                            [x[:, s, k * SEQ:(k + 1) * SEQ] for x in pT], k == 0, k == 1)
                    last.then_inc(o_full.sem, 1)
                if now:
                    pe.wait_ge(k_done.sem, at(k_done, base, i, 1))
                    for s in range(2):
                        pe.wait_ge(exp_ok.sem, at(exp_ok, base, i - 1, s + 1))
                        for t in range(2):
                            last = product3(ps_s[s][:, t * SEQ:(t + 1) * SEQ],
                                            [x[:, (2 * s + t) * P:(2 * s + t + 1) * P] for x in qT],
                                            [x[:, s * SEQ:(s + 1) * SEQ] for x in kT], True, True)
                        last.then_inc(s_full.sem, 1)

            def start(u):
                pe.wait_ge(x_got.sem, x_got.at(u, 48))
                pe.wait_ge(y_free.sem, y_free.at(u, 0))
                for b in range(2):
                    for n in range(2):
                        pe.matmul(ps_y[b][:], ones_r[:], bo[n][:].rearrange("a i n -> a (i n)"), start=(n == 0), stop=False,
                                  skip_group_check=True)

            walk(pe, step, start, lambda u: None)


TOP_K = 2
SLOT_TILES = -(-(TOP_K * TOKENS + EXPERTS * (P - 1)) // P)
SLOT_TILES += SLOT_TILES % 2
SLOTS = SLOT_TILES * P


def stage_routing(nc, dram, route):
    with ExitStack() as ctx:
        def sb(name, shape, dt=F32):
            return ctx.enter_context(nc.sbuf_tensor(name, shape, dt))

        def sem(name):
            return ctx.enter_context(nc.semaphore(name))

        lg = sb("lg_r", [P, TILES, EXPERTS])
        work = [sb(f"work{i}", [P, TILES, EXPERTS]) for i in range(2)]
        probs = sb("probs_r", [P, TILES, EXPERTS])
        masks = [sb(f"mask{i}", [P, TILES, EXPERTS]) for i in range(TOP_K)]
        chosen = sb("chosen", [P, TILES, EXPERTS], R32)
        rank = sb("rank", [P, TILES, EXPERTS])
        totals = [sb(f"totals{i}", [P, TILES, EXPERTS]) for i in range(2)]
        row = sb("row_r", [P, TILES])
        falling = sb("falling", [P, EXPERTS])
        place = sb("place", [P, TILES])
        counts_i = sb("counts_i", [P, EXPERTS], I32)
        tiles_i = sb("tiles_i", [P, EXPERTS], I32)
        tiles_f = sb("tiles_f", [P, EXPERTS])
        ends = [sb(f"ends{i}", [P, EXPERTS]) for i in range(2)]
        first = sb("first", [P, EXPERTS])
        tile_no = sb("tile_no", [1, SLOT_TILES])
        passed = sb("passed", [1, SLOT_TILES, EXPERTS])
        expert_f = sb("expert_f", [1, SLOT_TILES])
        before_f = sb("before_f", [P, P])
        before = sb("before", [P, P], R32)
        all_f = sb("all_f", [P, P])
        ones = sb("ones_r2", [P, P], R32)
        ps_rank = ctx.enter_context(nc.psum_tensor("ps_rank", [P, 512], F32))
        ps_total = ctx.enter_context(nc.psum_tensor("ps_total", [P, 512], F32))

        got = sem("lg_got")
        made = sem("made")
        cast = sem("cast")
        shifted = sem("shifted")
        exp_done = sem("exp_done")
        own = sem("own_r")
        chosen_ok = sem("chosen_ok")
        summed = sem("summed")
        block = ctx.enter_context(nc.Block())

        def flat(t):
            return t[:].rearrange("p t e -> p (t e)")

        @block.sync
        def _(sp):
            sp.dma_start(lg[:].rearrange("p (u t) e -> p u (t e)", u=TURNS), dram["logits"].rearrange("u p n -> p u n"))\
                .then_inc(got, 16)

        @block.gpsimd
        def _(pool):
            pool.memset(before_f[:], 1.0).then_inc(made, 1)
            pool.memset(all_f[:], 1.0).then_inc(made, 1)
            pool.iota(falling[:], [[-1, EXPERTS]], base=EXPERTS, channel_multiplier=0, allow_small_or_imprecise_dtypes=True)\
                .then_inc(made, 1)
            pool.iota(tile_no[:], [[1, SLOT_TILES]], base=0, channel_multiplier=0, allow_small_or_imprecise_dtypes=True)\
                .then_inc(made, 1)
            pool.wait_ge(made, 4)
            pool.affine_select(out=before_f[:], in_=before_f[:], compare_op=ALU.is_gt, fill=0.0, base=0,
                               pattern=[[1, P]], channel_multiplier=-1).then_inc(made, 1)

        @block.scalar
        def _(act):
            act.wait_ge(made, 5)
            act.activation(before[:], before_f[:], ACT.Copy).then_inc(cast, 1)
            act.activation(ones[:], all_f[:], ACT.Copy).then_inc(cast, 1)
            act.wait_ge(shifted, 1)
            act.activation(flat(work[1]), flat(work[0]), ACT.Exp).then_inc(exp_done, 1)

        @block.tensor
        def _(pe):
            pe.wait_ge(cast, 2)
            pe.wait_ge(chosen_ok, 1)
            n = TILES * EXPERTS
            pe.matmul(ps_rank[:, 0:n], before[:], flat(chosen), start=True, stop=True)
            pe.matmul(ps_total[:, 0:n], ones[:], flat(chosen), start=True, stop=True).then_inc(summed, 1)

        @block.vector
        def _(dve):
            steps = [0]

            def link(ins):
                steps[0] += 1
                ins.then_inc(own, 1)
                dve.wait_ge(own, steps[0])

            def wide(t):
                return t.unsqueeze(2).to_broadcast([P, TILES, EXPERTS])

            falling_w = falling[:].unsqueeze(1).to_broadcast([P, TILES, EXPERTS])
            dve.wait_ge(got, 16)
            dve.wait_ge(made, 5)
            link(dve.tensor_reduce(row[:], lg[:], AX.X, ALU.max))
            dve.tensor_tensor(work[0][:], lg[:], wide(row[:]), ALU.subtract).then_inc(shifted, 1)
            dve.wait_ge(exp_done, 1)
            link(dve.tensor_reduce(row[:], work[1][:], AX.X, ALU.add))
            link(dve.reciprocal(place[:], row[:]))
            link(dve.tensor_tensor(probs[:], work[1][:], wide(place[:]), ALU.mult))
            for k in range(TOP_K):
                weight = route.weight[k]
                link(dve.tensor_reduce(weight[:], probs[:], AX.X, ALU.max))
                link(dve.tensor_tensor(work[0][:], probs[:], wide(weight[:]), ALU.is_equal))
                link(dve.tensor_tensor(work[1][:], work[0][:], falling_w, ALU.mult))
                link(dve.tensor_reduce(row[:], work[1][:], AX.X, ALU.max))
                link(dve.tensor_tensor(masks[k][:], falling_w, wide(row[:]), ALU.is_equal))
                if k == 0:
                    link(dve.scalar_tensor_tensor(out=flat(probs), in0=flat(masks[0]), scalar=-2.0, in1=flat(probs),
                                                  op0=ALU.mult, op1=ALU.add))
            dve.tensor_tensor(chosen[:], masks[0][:], masks[1][:], ALU.add).then_inc(chosen_ok, 1)
            dve.wait_ge(summed, 1)
            n = TILES * EXPERTS
            link(dve.tensor_copy(flat(rank), ps_rank[:, 0:n]))
            link(dve.tensor_copy(flat(totals[0]), ps_total[:, 0:n]))
            link(dve.tensor_tensor(flat(rank), flat(rank), flat(totals[0]), ALU.subtract))
            src, dst, d = totals[0], totals[1], 1
            while d < TILES:
                link(dve.tensor_copy(dst[:, 0:d, :], src[:, 0:d, :]))
                link(dve.tensor_tensor(dst[:, d:, :], src[:, d:, :], src[:, 0:TILES - d, :], ALU.add))
                src, dst, d = dst, src, 2 * d
            link(dve.tensor_tensor(rank[:], rank[:], src[:], ALU.add))
            link(dve.tensor_scalar(counts_i[:], src[:, TILES - 1, :], float(P - 1), None, ALU.add))
            link(dve.tensor_scalar(tiles_i[:], counts_i[:], P.bit_length() - 1, None, ALU.arith_shift_right))
            link(dve.tensor_copy(tiles_f[:], tiles_i[:]))
            link(dve.tensor_copy(ends[0][:], tiles_f[:]))
            a, b, d = ends[0], ends[1], 1
            while d < EXPERTS:
                link(dve.tensor_copy(b[:, 0:d], a[:, 0:d]))
                link(dve.tensor_tensor(b[:, d:], a[:, d:], a[:, 0:EXPERTS - d], ALU.add))
                a, b, d = b, a, 2 * d
            link(dve.tensor_tensor(first[:], a[:], tiles_f[:], ALU.subtract))
            link(dve.tensor_scalar(first[:], first[:], float(P), None, ALU.mult))
            link(dve.tensor_tensor(rank[:], rank[:], first[:].unsqueeze(1).to_broadcast([P, TILES, EXPERTS]), ALU.add))
            for k in range(TOP_K):
                link(dve.tensor_tensor(work[0][:], masks[k][:], rank[:], ALU.mult))
                link(dve.tensor_reduce(place[:], work[0][:], AX.X, ALU.add))
                link(dve.tensor_copy(route.slot[k][:], place[:]))
            link(dve.tensor_tensor(passed[:], a[0:1, :].unsqueeze(1).to_broadcast([1, SLOT_TILES, EXPERTS]),
                                   tile_no[:].unsqueeze(2).to_broadcast([1, SLOT_TILES, EXPERTS]), ALU.is_le))
            link(dve.tensor_reduce(expert_f[:], passed[:], AX.X, ALU.add))
            link(dve.tensor_scalar(route.expert[:], expert_f[:], float(EXPERTS - 1), None, ALU.min))


def stage_scatter(nc, dram, route):
    with ExitStack() as ctx:
        rows = ctx.enter_context(nc.sbuf_tensor("rows_s", [P, TILES, D], F32))
        zeros = ctx.enter_context(nc.sbuf_tensor("zeros_s", [P, 8 * D], F32))
        got = ctx.enter_context(nc.semaphore("rows_s_got"))
        zero_ok = ctx.enter_context(nc.semaphore("zero_ok"))
        cleared = ctx.enter_context(nc.semaphore("cleared"))
        sent = ctx.enter_context(nc.semaphore("sent"))
        block = ctx.enter_context(nc.Block())

        @block.sync
        def _(sp):
            sp.dma_start(rows[:].rearrange("p (u t) n -> p u (t n)", u=TURNS), dram["xn1"].rearrange("u p n -> p u n"))\
                .then_inc(got, 16)
            sp.wait_ge(zero_ok, 1)
            for n in range(SLOT_TILES // 8):
                sp.dma_start(dram["xs"][n * 8 * P:(n + 1) * 8 * P, :].rearrange("(p t) n -> p (t n)", p=P), zeros[:])\
                    .then_inc(cleared, 16)

        @block.gpsimd
        def _(pool):
            pool.memset(zeros[:], 0.0).then_inc(zero_ok, 1)
            pool.wait_ge(got, 16)
            pool.wait_ge(cleared, 16 * (SLOT_TILES // 8))
            for t in range(TILES):
                for k in range(TOP_K):
                    pool.indirect_dma_start(dram["xs"], bass.IndirectOffsetOnAxis(ap=route.slot[k][:, t:t + 1], axis=0),
                                            rows[:, t, :], None).then_inc(sent, 16)
            pool.wait_ge(sent, 16 * TILES * TOP_K)


HALF = INTER // 2


def stage_experts(nc, dram, route):
    with ExitStack() as ctx:
        def sb(name, shape, dt=F32):
            return ctx.enter_context(nc.sbuf_tensor(name, shape, dt))

        def psum(name):
            return ctx.enter_context(nc.psum_tensor(name, [P, 512], F32))

        def sem(name):
            return ctx.enter_context(nc.semaphore(name))

        UP = DC * 2 * INTER
        DOWN = 2 * D
        PART = 2
        ident = sb("ident_e", [P, P])
        w_up = [sb(f"we_up{i}", [P, EXPERTS * UP], R32) for i in range(2)]
        w_down = [sb(f"we_down{i}", [HALF, EXPERTS * DOWN], R32) for i in range(2)]
        raw_up = sb("raw_up", [P, 2, PART, DC, 2, INTER])
        raw_down = sb("raw_down_e", [HALF, 2, PART * DOWN])
        xs = sb("xs_e", [P, 4, D])
        xT = [sb(f"xTe{i}", [P, 2, D], R32) for i in range(2)]
        tanh_g = sb("tanh_e", [P, 2, INTER])
        gated = sb("gated_e", [P, 2, INTER])
        h_f = sb("h_fe", [P, 2, INTER])
        hT = [sb(f"hTe{i}", [HALF, 2, 2 * P], R32) for i in range(2)]
        ys = sb("ys_e", [P, 2, D])
        ps_x = [psum(f"ps_x{i}") for i in range(2)]
        ps_u = [psum(f"ps_u{i}") for i in range(2)]
        ps_h = [psum(f"ps_h{i}") for i in range(2)]
        ps_d = [psum(f"ps_d{i}") for i in range(2)]

        id_ok = sem("ide_ok")
        raw_got = [sem(f"raw_got{i}") for i in range(2)]
        w_high = sem("w_high")
        w_low = sem("w_low")
        x_got = [Signal(sem(f"xs_got{i}"), 4) for i in range(4)]
        x_full = Signal(sem("xe_full"), 1, 4)
        x_high = Signal(sem("xe_high"), 1)
        x_low = Signal(sem("xe_low"), 1, 2)
        u_full = Signal(sem("ue_full"), 1)
        tanh_ok = Signal(sem("tanhe_ok"), 1)
        gate_ok = Signal(sem("gatee_ok"), 1)
        h_ok = Signal(sem("he_ok"), 1, 2)
        h_full = Signal(sem("he_full"), 1)
        h_high = Signal(sem("he_high"), 1)
        h_low = Signal(sem("he_low"), 1, 2)
        d_full = Signal(sem("de_full"), 1)
        y_ok = Signal(sem("ye_ok"), 1, 2)
        y_out = [Signal(sem(f"y_out{i}"), 8, 16) for i in range(2)]

        block = ctx.enter_context(nc.Block())

        def walk(step):
            return step

        def at(signal, base, i, n):
            return base * signal.per_turn + (signal.head + i * signal.per_turn + n)

        LAG = 3
        FILL = 4

        def steps(eng, step):
            for i in range(FILL):
                step(0, i, i)
            with eng.Fori(0, (SLOT_TILES - FILL) // 4) as j:
                for a in range(4):
                    step(j * 4, FILL + a, FILL)
            for i in range(LAG):
                step(SLOT_TILES, i, SLOT_TILES + i)

        @block.sync
        def _(sp):
            parts = EXPERTS // PART
            for n in range(parts):
                if n >= 2:
                    sp.wait_ge(w_low, 2 * (n - 1))
                e = n * PART
                for i, m in enumerate(("w1T", "w3T")):
                    for k in range(PART):
                        sp.dma_start(raw_up[:, n % 2, k, :, i, :], dram[m][e + k].rearrange("(c p) n -> p c n", p=P))\
                            .then_inc(raw_got[n % 2], 16)
                sp.dma_start(raw_down[:, n % 2, :].rearrange("p (a n) -> p a n", n=D),
                             dram["w2T"][e:e + PART].rearrange("e (c p) n -> p (e c) n", p=HALF)).then_inc(raw_got[n % 2], 16)
            with sp.Fori(0, SLOT_TILES // 4) as j:
                for a in range(4):
                    sp.wait_ge(x_full.sem, at(x_full, j * 4, a - 4, 1))
                    sp.dma_start(xs[:, a, :], dram["xs"].rearrange("(t p) n -> t p n", p=P)[ds(j * 4 + a, 1)]
                                 .rearrange("o p n -> (o p) n")).then_inc(x_got[a].sem, 16)

        @block.gpsimd
        def _(pool):
            pool.memset(ident[:], 0.0).then_inc(id_ok, 1)
            pool.wait_ge(id_ok, 1)
            pool.affine_select(out=ident[:], in_=ident[:], compare_op=ALU.not_equal, fill=1.0, base=0,
                               pattern=[[-1, P]], channel_multiplier=1).then_inc(id_ok, 1)

        def parts_of(n):
            e = n * PART
            return [(raw_up[:, n % 2].rearrange("p k c i n -> p (k c i n)"),
                     *[w[:, e * UP:(e + PART) * UP] for w in w_up]),
                    (raw_down[:, n % 2, :], *[w[:, e * DOWN:(e + PART) * DOWN] for w in w_down])]

        @block.scalar
        def _(act):
            for n in range(EXPERTS // PART):
                act.wait_ge(raw_got[n % 2], 16 * (2 * PART + 1) * (n // 2 + 1))
                for raw, high, _ in parts_of(n):
                    act.activation(high, raw, ACT.Copy).then_inc(w_high, 1)

            def step(base, i, kind):
                if kind < SLOT_TILES:
                    b = i % 2
                    act.wait_ge(x_full.sem, at(x_full, base, i, 1))
                    act.activation(xT[0][:, b, :], ps_x[b][:, 0:D], ACT.Copy).then_inc(x_high.sem, 1)
                if 1 <= kind < SLOT_TILES + 1:
                    b = (i - 1) % 2
                    act.wait_ge(u_full.sem, at(u_full, base, i - 1, 1))
                    act.activation(tanh_g[:, b, :], ps_u[b][:, 0:INTER], ACT.Tanh, scale=0.5).then_inc(tanh_ok.sem, 1)
                if 2 <= kind < SLOT_TILES + 2:
                    b = (i - 2) % 2
                    act.wait_ge(h_full.sem, at(h_full, base, i - 2, 1))
                    act.activation(hT[0][:, b, :], ps_h[b][0:HALF, 0:2 * P], ACT.Copy).then_inc(h_high.sem, 1)
                if 3 <= kind < SLOT_TILES + 3:
                    b = (i - 3) % 2
                    act.wait_ge(d_full.sem, at(d_full, base, i - 3, 1))
                    act.wait_ge(y_out[b].sem, base * 8 + 16 * ((i - 3) // 2 + 1))
                    act.activation(ys[:, b, :], ps_d[b][:, 0:D], ACT.Copy).then_inc(y_ok.sem, 1)
                    act.wait_ge(y_ok.sem, at(y_ok, base, i - 3, 1))
                    tiles = dram["ys"].rearrange("(t p) n -> t p n", p=P)
                    act.dma_start(tiles[ds(base + (i - 3), 1)].rearrange("o p n -> (o p) n"), ys[:, b, :])\
                        .then_inc(y_out[b].sem, 16)

            act.sem_inc(y_ok.sem, 2)
            for b in range(2):
                act.sem_inc(y_out[b].sem, 16)
            steps(act, step)
            for b in range(2):
                act.wait_ge(y_out[b].sem, 16 + 8 * SLOT_TILES)

        @block.vector
        def _(dve):
            for n in range(EXPERTS // PART):
                for m, (raw, high, low) in enumerate(parts_of(n)):
                    dve.wait_ge(w_high, 2 * n + m + 1)
                    dve.tensor_tensor(low, raw, high.bitcast(F32), ALU.subtract).then_inc(w_low, 1)
            dve.sem_inc(x_low.sem, 2)
            dve.sem_inc(h_ok.sem, 2)
            dve.sem_inc(h_low.sem, 2)

            def step(base, i, kind):
                if kind < SLOT_TILES:
                    b = i % 2
                    dve.wait_ge(x_high.sem, at(x_high, base, i, 1))
                    dve.tensor_tensor(xT[1][:, b, :], ps_x[b][:, 0:D], xT[0][:, b, :].bitcast(F32), ALU.subtract).then_inc(x_low.sem, 1)
                if 1 <= kind < SLOT_TILES + 1:
                    b = (i - 1) % 2
                    dve.wait_ge(tanh_ok.sem, at(tanh_ok, base, i - 1, 1))
                    dve.scalar_tensor_tensor(out=gated[:, b, :], in0=tanh_g[:, b, :], scalar=1.0, in1=ps_u[b][:, 0:INTER],
                                             op0=ALU.add, op1=ALU.mult).then_inc(gate_ok.sem, 1)
                    dve.wait_ge(gate_ok.sem, at(gate_ok, base, i - 1, 1))
                    dve.scalar_tensor_tensor(out=h_f[:, b, :], in0=ps_u[b][:, INTER:2 * INTER], scalar=0.5, in1=gated[:, b, :],
                                             op0=ALU.mult, op1=ALU.mult).then_inc(h_ok.sem, 1)
                if 2 <= kind < SLOT_TILES + 2:
                    b = (i - 2) % 2
                    dve.wait_ge(h_high.sem, at(h_high, base, i - 2, 1))
                    dve.tensor_tensor(hT[1][:, b, :], ps_h[b][0:HALF, 0:2 * P], hT[0][:, b, :].bitcast(F32), ALU.subtract)\
                        .then_inc(h_low.sem, 1)

            steps(dve, step)

        @block.tensor
        def _(pe):
            pe.wait_ge(id_ok, 2)
            pe.wait_ge(w_low, 2 * (EXPERTS // PART))
            pe.sem_inc(x_full.sem, 4)

            def expert(base, i):
                return pe.value_load(route.expert[0:1, ds(base + i, 1)], min_val=0, max_val=EXPERTS - 1)

            def step(base, i, kind):
                if 1 <= kind < SLOT_TILES + 1:
                    e_up = expert(base, i - 1)
                if 3 <= kind < SLOT_TILES + 3:
                    e_down = expert(base, i - 3)
                if kind < SLOT_TILES:
                    b = i % 2
                    pe.wait_ge(x_got[i % 4].sem, base * 4 + 16 * (i // 4 + 1))
                    pe.wait_ge(x_low.sem, at(x_low, base, i - 2, 1))
                    for c in range(DC):
                        last = pe.transpose(ps_x[b][:, c * P:(c + 1) * P], xs[:, i % 4, c * P:(c + 1) * P], ident[:])
                    last.then_inc(x_full.sem, 1)
                if 1 <= kind < SLOT_TILES + 1:
                    b = (i - 1) % 2
                    pe.wait_ge(x_low.sem, at(x_low, base, i - 1, 1))
                    pe.wait_ge(h_ok.sem, at(h_ok, base, i - 3, 1))
                    for c in range(DC):
                        for n, (x, w) in enumerate(((0, 0), (0, 1), (1, 0))):
                            last = pe.matmul(ps_u[b][:, 0:2 * INTER], xT[x][:, b, c * P:(c + 1) * P],
                                             w_up[w][:, ds(e_up * UP + c * 2 * INTER, 2 * INTER)],
                                             start=(c == 0 and n == 0), stop=(c == DC - 1 and n == 2), skip_group_check=True)
                    last.then_inc(u_full.sem, 1)
                if 2 <= kind < SLOT_TILES + 2:
                    b = (i - 2) % 2
                    pe.wait_ge(h_ok.sem, at(h_ok, base, i - 2, 1))
                    pe.wait_ge(h_low.sem, at(h_low, base, i - 4, 1))
                    for c in range(2):
                        last = pe.transpose(ps_h[b][0:HALF, c * P:(c + 1) * P], h_f[:, b, c * HALF:(c + 1) * HALF], ident[:])
                    last.then_inc(h_full.sem, 1)
                if 3 <= kind < SLOT_TILES + 3:
                    b = (i - 3) % 2
                    pe.wait_ge(h_low.sem, at(h_low, base, i - 3, 1))
                    pe.wait_ge(y_ok.sem, at(y_ok, base, i - 5, 1))
                    for c in range(2):
                        for n, (x, w) in enumerate(((0, 0), (0, 1), (1, 0))):
                            last = pe.matmul(ps_d[b][:, 0:D], hT[x][:, b, c * P:(c + 1) * P],
                                             w_down[w][:, ds(e_down * DOWN + c * D, D)],
                                             start=(c == 0 and n == 0), stop=(c == 1 and n == 2), skip_group_check=True)
                    last.then_inc(d_full.sem, 1)

            steps(pe, step)


def stage_combine(nc, dram, route):
    with ExitStack() as ctx:
        RING = 4
        x = ctx.enter_context(nc.sbuf_tensor("x_c", [P, TILES, D], F32))
        rows = [ctx.enter_context(nc.sbuf_tensor(f"rows_c{k}", [P, RING, D], F32)) for k in range(TOP_K)]
        got = [[ctx.enter_context(nc.semaphore(f"rows_c_got{k}_{i}")) for i in range(RING)] for k in range(TOP_K)]
        x_got = ctx.enter_context(nc.semaphore("x_c_got"))
        own = ctx.enter_context(nc.semaphore("own_c"))
        out = ctx.enter_context(nc.semaphore("out_c"))
        block = ctx.enter_context(nc.Block())

        @block.sync
        def _(sp):
            sp.dma_start(x[:].rearrange("p (u t) n -> p u (t n)", u=TURNS), dram["x1"].rearrange("u p n -> p u n")).then_inc(x_got, 16)
            for t in range(TILES):
                sp.wait_ge(own, TOP_K * (t + 1))
                sp.dma_start(dram["out"][t * P:(t + 1) * P, :], x[:, t, :]).then_inc(out, 16)
            sp.wait_ge(out, 16 * TILES)

        @block.gpsimd
        def _(pool):
            for t in range(TILES):
                if t >= RING:
                    pool.wait_ge(own, TOP_K * (t - RING + 1))
                for k in range(TOP_K):
                    pool.indirect_dma_start(rows[k][:, t % RING, :], None, dram["ys"],
                                            bass.IndirectOffsetOnAxis(ap=route.slot[k][:, t:t + 1], axis=0))\
                        .then_inc(got[k][t % RING], 16)

        @block.vector
        def _(dve):
            dve.wait_ge(x_got, 16)
            for t in range(TILES):
                for k in range(TOP_K):
                    dve.wait_ge(got[k][t % RING], 16 * (t // RING + 1))
                    if k:
                        dve.wait_ge(own, TOP_K * t + k)
                    dve.scalar_tensor_tensor(out=x[:, t, :], in0=rows[k][:, t % RING, :], scalar=route.weight[k][:, t:t + 1],
                                             in1=x[:, t, :], op0=ALU.mult, op1=ALU.add).then_inc(own, 1)


class Route:

    def __init__(self, nc, ctx):
        def sb(name, shape, dt):
            return ctx.enter_context(nc.sbuf_tensor(name, shape, dt))

        self.slot = [sb(f"slot{k}", [P, TILES], I32) for k in range(TOP_K)]
        self.weight = [sb(f"weight{k}", [P, TILES], F32) for k in range(TOP_K)]
        self.expert = sb("expert", [1, SLOT_TILES], I32)


def program(nc, dram):
    for name, shape, dt in (
        ("q_scr", [2, D, PAIR], F32),
        ("xn1", [TURNS, P, TP * D], F32),
        ("xn1T", [2 * TURNS, P, DC * PAIR], F32),
        ("x1", [TURNS, P, TP * D], F32),
        ("w_head", [HEADS1, P, W_A + W_B], F32),
        ("xs", [SLOTS, D], F32),
        ("ys", [SLOTS, D], F32),
        ("logits", [TURNS, P, TP * EXPERTS], F32),
    ):
        dram[name] = nc.dram_tensor("d_" + name, shape, dt, kind="Internal").ap()
    with ExitStack() as ctx:
        route = Route(nc, ctx)
        stage_layer0(nc, dram)
        stage_routing(nc, dram, route)
        stage_scatter(nc, dram, route)
        stage_experts(nc, dram, route)
        stage_attention_weights(nc, dram)
        stage_attention(nc, dram)
        stage_combine(nc, dram, route)


_OUTS = [((8, 256, 256), "float32")]


def kernel(**inputs):
    import numpy as _np
    import concourse.bacc as _bacc
    from concourse import mybir as _mybir
    from concourse.bass_utils import run_bass_kernel_spmd as _run

    g = lambda name: _np.asarray(inputs[name])
    laid = {
        "x": g("L0_attn_x").reshape(TOKENS, D),
        "WqkvT": g("L0_attn_Wqkv_w").T, "Wqkv_b": g("L0_attn_Wqkv_b"),
        "out_wT": g("L0_attn_out_w").T, "out_b": g("L0_attn_out_b"),
        "wgateT": g("L0_ffn_wq_gate").T, "s_gate": g("L0_ffn_s_gate"),
        "wupT": g("L0_ffn_wq_up").T, "s_up": g("L0_ffn_s_up"),
        "wdownT": g("L0_ffn_wq_down").T, "s_down": g("L0_ffn_s_down"),
        "wq_codes": g("L1_attn_wq_codes"), "wq_scales": g("L1_attn_wq_scales"), "bq": g("L1_attn_bq"),
        "wk_codes": g("L1_attn_wk_codes"), "wk_scales": g("L1_attn_wk_scales"), "bk": g("L1_attn_bk"),
        "wv_codes": g("L1_attn_wv_codes"), "wv_scales": g("L1_attn_wv_scales"), "bv": g("L1_attn_bv"),
        "wo_codes": g("L1_attn_wo_codes"), "wo_scales": g("L1_attn_wo_scales"), "bo": g("L1_attn_bo"),
        "w1T": g("L1_ffn_w1").transpose(0, 2, 1), "w3T": g("L1_ffn_w3").transpose(0, 2, 1), "w2T": g("L1_ffn_w2").transpose(0, 2, 1),
        "gate_wT": g("L1_ffn_gate_w").T,
        "sw1T": g("L1_ffn_sw1").T, "sw2T": g("L1_ffn_sw2").T, "sw3T": g("L1_ffn_sw3").T,
    }
    nc = _bacc.Bacc("TRN2", target_bir_lowering=False, num_devices=1)
    arrays, dram = {}, {}
    for name, a in laid.items():
        a = _np.ascontiguousarray(a)
        arrays[f"in_{name}"] = a
        dram[name] = nc.dram_tensor(f"in_{name}", a.shape, _mybir.dt.from_np(a.dtype), kind="ExternalInput").ap()
    shape, dtype = _OUTS[0]
    out = nc.dram_tensor("out_0", shape, _mybir.dt.from_np(_np.dtype(dtype)), kind="ExternalOutput").ap()
    dram["out"] = out.rearrange("b s d -> (b s) d")
    program(nc, dram)
    r = _run(nc, [arrays], core_ids=[0])
    return r.results[0]["out_0"]
```

```python
from contextlib import ExitStack

import numpy as np

import concourse.bass as bass
from concourse import mybir

F32 = mybir.dt.float32
R32 = mybir.dt.float32r
I32 = mybir.dt.int32
U32 = mybir.dt.uint32
ALU = mybir.AluOpType
ACT = mybir.ActivationFunctionType
AX = mybir.AxisListType
ds = bass.ds

P = 128
SEQS, SEQ, D = 8, 256, 256
TOKENS = SEQS * SEQ
DC = D // P
PAIR = 2 * SEQ
TURNS = TOKENS // PAIR
TP = PAIR // P
EPS = 1e-5
HEADS0, HD0 = 16, 16
QKV0 = D + 2 * HD0
HID = 704
ZERO_POINT = 128.0
HT = [min(m, HID - P) for m in range(0, HID, P)]
HEADS1, HD1 = 16, 128
FEAT = HEADS1 * HD1
BLOCK = 32
EXPERTS, INTER, SHARED = 16, 176, 352
ST = [min(m, SHARED - P) for m in range(0, SHARED, P)]
REP = P // HD0
TILES = TOKENS // P
MASKED = -1.0e30


class Signal:

    def __init__(self, sem, per_turn=0, head=0):
        self.sem, self.per_turn, self.head = sem, per_turn, head

    def at(self, turn, n):
        return turn * self.per_turn + (self.head + n)


def stage_layer0(nc, dram):
    QW = D + P + HD0
    DUP_H, DUP_S = 5 * P - HT[5], 2 * P - ST[2]
    with ExitStack() as ctx:
        def sb(name, shape, dt=F32):
            return ctx.enter_context(nc.sbuf_tensor(name, shape, dt))

        def psum(name):
            return ctx.enter_context(nc.psum_tensor(name, [P, 512], F32))

        def sem(name):
            return ctx.enter_context(nc.semaphore(name))

        ident = sb("ident", [P, P])
        ident_r = sb("ident_r", [P, P], R32)
        mask_r = sb("mask_r", [P, 4, P], R32)
        ones_r = sb("ones_r", [1, P], R32)
        w_qkv = [sb(f"w_qkv{i}", [P, DC, QW], R32) for i in range(2)]
        w_o = [sb(f"w_o{i}", [P, DC, D], R32) for i in range(2)]
        ob = [sb(f"ob{i}", [1, D], R32) for i in range(2)]
        w_gate = sb("w_gate", [P, DC, HID], R32)
        w_up = sb("w_up", [P, DC, HID], R32)
        w_down = sb("w_down", [P, len(HT), D], R32)
        w_s13 = [sb(f"w_s13{i}", [P, DC, 2 * SHARED], R32) for i in range(2)]
        w_s2 = [sb(f"w_s2{i}", [P, len(ST), D], R32) for i in range(2)]
        w_gw = [sb(f"w_gw{i}", [P, DC, EXPERTS], R32) for i in range(2)]
        bq = sb("bq", [P, DC])
        bk = sb("bk", [48, 1])
        bv = sb("bv", [P, 2, HD0])
        s_gate = sb("s_gate", [P, len(HT)])
        s_up = sb("s_up", [P, len(HT)])
        half_gate = sb("half_gate", [P, len(HT)])
        scale_h = sb("scale_h", [P, len(HT)])
        s_down = sb("s_down", [P, D])
        with ExitStack() as staging:
            def stage(name, shape, dt=F32):
                return staging.enter_context(nc.sbuf_tensor(name, shape, dt))

            def stage_sem(name):
                return staging.enter_context(nc.semaphore(name))

            mask_f = stage("mask_f", [P, 4, P])
            ones_f = stage("ones_f", [1, P])
            raw_qkv = stage("raw_qkv", [P, DC, QW])
            raw_o = stage("raw_o", [P, DC, D])
            raw_ob = stage("raw_ob", [1, D])
            raw_int = stage("raw_int", [P, DC, HID], I32)
            raw_down = stage("raw_down", [P, len(HT), D], I32)
            raw_s13 = raw_int[:].bitcast(F32)
            raw_s2 = stage("raw_s2", [P, len(ST), D])
            raw_gw = stage("raw_gw", [P, DC, EXPERTS])
            raw_in = stage_sem("raw_in")
            const_ok = stage_sem("const_ok")
            prep_act = stage_sem("prep_act")
            prep_dve = stage_sem("prep_dve")
            block = staging.enter_context(nc.Block())

            loads = [
                (raw_qkv[:, :, 0:D], dram["WqkvT"][:, 0:D].rearrange("(c p) n -> p c n", p=P)),
                *[(raw_qkv[:, :, D + HD0 * i:D + HD0 * (i + 1)], dram["WqkvT"][:, D:D + HD0].rearrange("(c p) n -> p c n", p=P))
                  for i in range(REP)],
                (raw_qkv[:, :, D + P:], dram["WqkvT"][:, D + HD0:].rearrange("(c p) n -> p c n", p=P)),
                (raw_o[:], dram["out_wT"].rearrange("(c p) n -> p c n", p=P)),
                (raw_ob[:], dram["out_b"].rearrange("(a n) -> a n", a=1)),
                *[(bq[:, c:c + 1], dram["Wqkv_b"][c * P:(c + 1) * P].rearrange("(p a) -> p a", a=1)) for c in range(DC)],
                *[(bk[HD0 * i:HD0 * (i + 1), :], dram["Wqkv_b"][D:D + HD0].rearrange("(p a) -> p a", a=1)) for i in range(3)],
                *[(bv[:, i, :], dram["Wqkv_b"][D + HD0:].rearrange("(a n) -> a n", a=1).partition_broadcast(P)) for i in range(2)],
                *[(t[:, m:m + 1], dram[n][at:at + P].rearrange("(p a) -> p a", a=1))
                  for t, n in ((s_gate, "s_gate"), (s_up, "s_up")) for m, at in enumerate(HT)],
                (s_down[:], dram["s_down"].rearrange("(a n) -> a n", a=1).partition_broadcast(P)),
                (raw_down[:, 0:5, :], dram["wdownT"][0:5 * P, :].rearrange("(m p) n -> p m n", p=P)),
                (raw_down[DUP_H:, 5, :], dram["wdownT"][5 * P:, :]),
                (raw_s2[:, 0:2, :], dram["sw2T"][0:2 * P, :].rearrange("(m p) n -> p m n", p=P)),
                (raw_s2[DUP_S:, 2, :], dram["sw2T"][2 * P:, :]),
                (raw_gw[:], dram["gate_wT"].rearrange("(c p) n -> p c n", p=P)),
                (raw_int[:], dram["wgateT"].rearrange("(c p) n -> p c n", p=P)),
            ]
            FIRST = 16 * len(loads)

            splits = [(raw_qkv[:], w_qkv[0][:], w_qkv[1][:]), (raw_o[:], w_o[0][:], w_o[1][:]), (raw_ob[:], ob[0][:], ob[1][:]),
                      (raw_s2[:], w_s2[0][:], w_s2[1][:]),
                      (raw_gw[:], w_gw[0][:], w_gw[1][:]),
                      (raw_s13, w_s13[0][:], w_s13[1][:])]

            @block.sync
            def _(sp):
                for dst, src in loads:
                    sp.dma_start(dst, src).then_inc(raw_in, 16)
                sp.wait_ge(prep_dve, 1)
                sp.dma_start(raw_int[:], dram["wupT"].rearrange("(c p) n -> p c n", p=P)).then_inc(raw_in, 16)
                sp.wait_ge(prep_dve, 2)
                for i, n in enumerate(("sw1T", "sw3T")):
                    sp.dma_start(raw_s13[:, :, SHARED * i:SHARED * (i + 1)],
                                 dram[n].rearrange("(c p) n -> p c n", p=P)).then_inc(raw_in, 16)

            @block.gpsimd
            def _(pool):
                pool.memset(ident[:], 0.0).then_inc(const_ok, 1)
                pool.memset(mask_f[:], 0.0).then_inc(const_ok, 1)
                pool.memset(ones_f[:], 1.0).then_inc(const_ok, 1)
                pool.wait_ge(const_ok, 3)
                pool.affine_select(out=ident[:], in_=ident[:], compare_op=ALU.not_equal, fill=1.0, base=0,
                                   pattern=[[-1, P]], channel_multiplier=1).then_inc(const_ok, 1)
                pool.memset(raw_down[0:DUP_H, 5, :], int(ZERO_POINT)).then_inc(const_ok, 1)
                pool.memset(raw_s2[0:DUP_S, 2, :], 0.0).then_inc(const_ok, 1)
                pool.affine_select(out=mask_f[:], in_=mask_f[:], compare_op=ALU.is_ge, fill=MASKED, base=0,
                                   pattern=[[0, 4], [-1, P]], channel_multiplier=1).then_inc(const_ok, 1)

            @block.scalar
            def _(act):
                act.wait_ge(const_ok, 7)
                act.activation(ident_r[:], ident[:], ACT.Copy).then_inc(prep_act, 1)
                act.activation(mask_r[:], mask_f[:], ACT.Copy).then_inc(prep_act, 1)
                act.activation(ones_r[:], ones_f[:], ACT.Copy).then_inc(prep_act, 1)
                act.wait_ge(prep_dve, 3)
                for n, (raw, high, _) in enumerate(splits):
                    if n == len(splits) - 1:
                        act.wait_ge(raw_in, FIRST + 48)
                    act.activation(high, raw, ACT.Copy).then_inc(prep_act, 1)

            @block.vector
            def _(dve):
                dve.wait_ge(raw_in, FIRST)
                dve.tensor_scalar(w_gate[:], raw_int[:], ZERO_POINT, None, ALU.subtract).then_inc(prep_dve, 1)
                dve.wait_ge(raw_in, FIRST + 16)
                dve.tensor_scalar(w_up[:], raw_int[:], ZERO_POINT, None, ALU.subtract).then_inc(prep_dve, 1)
                dve.tensor_scalar(raw_qkv[:, :, 0:D], raw_qkv[:, :, 0:D], HD0 ** -0.5, None, ALU.mult).then_inc(prep_dve, 1)
                dve.tensor_scalar(bq[:], bq[:], HD0 ** -0.5, None, ALU.mult).then_inc(prep_dve, 1)
                dve.wait_ge(const_ok, 7)
                dve.tensor_scalar(w_down[:], raw_down[:], ZERO_POINT, None, ALU.subtract).then_inc(prep_dve, 1)
                dve.tensor_scalar(half_gate[:], s_gate[:], 0.5, None, ALU.mult).then_inc(prep_dve, 1)
                dve.wait_ge(prep_dve, 6)
                dve.tensor_tensor(scale_h[:], half_gate[:], s_up[:], ALU.mult).then_inc(prep_dve, 1)
                for n, (raw, high, low) in enumerate(splits):
                    dve.wait_ge(prep_act, 4 + n)
                    dve.tensor_tensor(low, raw, high.bitcast(F32), ALU.subtract).then_inc(prep_dve, 1)

        x_in = sb("x_in", [P, TP, D])
        stats = sb("stats", [P, 2 * TP, 6])
        mv = sb("mv", [P, 2 * TP, 2])
        var_eps = sb("var_eps", [P, 2 * TP])
        rstd = sb("rstd", [P, 2 * TP])
        minus_half = sb("minus_half", [P, 2 * TP])
        xn = sb("xn", [P, TP, D])
        xnT = [sb(f"xnT{i}", [P, DC, PAIR], R32) for i in range(2)]
        qT = [sb(f"qT{i}", [P, DC, PAIR], R32) for i in range(2)]
        q3 = sb("q3", [48, HEADS0, PAIR], R32)
        k3 = sb("k3", [48, 2, SEQ], R32)
        vf = sb("vf", [P, 2, 2, HD0])
        vs = sb("vs", [P, TP, 2, HD0], R32)
        neg_max = sb("neg_max", [P, 2, 4])
        sums = sb("sums", [P, TP, HEADS0])
        probs = sb("probs", [P, 2, 512])
        pT = [sb(f"pT{i}", [P, 2, 512], R32) for i in range(2)]
        ctx_f = sb("ctx_f", [P, HEADS0, HD0])
        rinv = sb("rinv", [P, HEADS0])
        ctx_n = sb("ctx_n", [P, D])
        cT = [sb(f"cT{i}", [P, TP, DC, P], R32) for i in range(2)]
        tanh_g = sb("tanh_g", [P, 2, PAIR])
        gated = sb("gated", [P, 2, PAIR])
        h_f = sb("h_f", [P, 2, PAIR])
        hT = [sb(f"hT{i}", [P, len(HT), PAIR], R32) for i in range(2)]
        sT = [sb(f"sT{i}", [P, len(ST), PAIR], R32) for i in range(2)]
        down_f = sb("down_f", [P, D])
        both_f = sb("both_f", [P, D])
        x1 = sb("x1", [P, TP, D])
        xn1 = sb("xn1", [P, TP, D])
        xn1T = [sb(f"xn1T{i}", [P, DC, PAIR], R32) for i in range(2)]
        lg = sb("lg", [P, TP, EXPERTS])

        ps_m = [psum(f"ps_m{i}") for i in range(3)]
        ps_s = [psum(f"ps_s{i}") for i in range(2)]
        ps_t = psum("ps_t")
        ps_c = psum("ps_c")

        units = []
        for s in range(2):
            units += [(s, 0, h, 4) for h in range(0, HEADS0, 4)]
            units += [(s, 1, h, 2) for h in range(0, HEADS0, 2)]
        NU = len(units)
        last_unit = {(s, t): max(n for n, u in enumerate(units) if u[:2] == (s, t)) for s, t, _, _ in units}
        steps = [[] for _ in range(NU + 3)]
        for n in range(2 * len(HT)):
            steps[n].append(("ffn", n))
        for (s, t), n in last_unit.items():
            steps[n + 3].append(("ctx", 2 * s + t))
        for n, at in enumerate((15, 16, 20, NU + 2)):
            steps[at].append(("out", n))
        for n, at in enumerate((18, 19, 22, NU + 2)):
            steps[at].append(("norm", n))
        front = [("xT", 0), ("xT", 1), ("q", 0), ("q", 1), ("k", 0), ("v", 0), ("k", 1), ("v", 1)]
        back = [("ffs", n) for n in range(2 * len(ST))] + [("sum", n) for n in range(TP)]
        order = front + [i for step in steps for i in step] + back
        NI = len(order)
        assert NI % len(ps_m) == 0 and NU % 2 == 0
        number = {item: n for n, item in enumerate(order)}
        acted = [i for i in order if i[0] in ("xT", "q", "k", "ctx", "norm") or (i[0] in ("ffn", "ffs") and i[1] % 2 == 0)]
        act_number = {item: n for n, item in enumerate(acted)}
        NH = len(HT) + len(ST)
        LINKS = 4 + 8 * TP

        def bank(item):
            return ps_m[number[item] % len(ps_m)]

        own = Signal(sem("dve_own"), 0)
        x_got = Signal(sem("x_got"), 16)
        var_ok = Signal(sem("var_ok"), 1 + TP)
        half_ok = sem("half_ok")
        rstd_ok = Signal(sem("rstd_ok"), 1 + TP)
        ln_done = Signal(sem("ln_done"), TP)
        item_full = Signal(sem("item_full"), NI)
        item_act = Signal(sem("item_act"), len(acted))
        item_done = Signal(sem("item_done"), NI, len(ps_m))
        q_out = Signal(sem("q_out"), 32 * DC)
        q3_got = Signal(sem("q3_got"), 48)
        s_full = Signal(sem("s_full"), NU)
        max_ok = Signal(sem("max_ok"), NU)
        p_ok = Signal(sem("p_ok"), NU, 2)
        t_full = Signal(sem("t_full"), NU)
        t_high = Signal(sem("t_high"), NU)
        t_low = Signal(sem("t_low"), NU, 1)
        pv_ok = Signal(sem("pv_ok"), NU, 2)
        ctx_free = Signal(sem("ctx_free"), TP, 1)
        ctx_ok = Signal(sem("ctx_ok"), TP)
        norm1_ok = Signal(sem("norm1_ok"), TP)
        h_high = Signal(sem("h_high"), NH)
        h_low = Signal(sem("h_low"), NH, 2)
        stored = Signal(sem("stored"), 80, 1)

        block = ctx.enter_context(nc.Block())

        @block.sync
        def _(sp):
            sp.dma_start(x_in[:], dram["x"][0:PAIR, :].rearrange("(t p) n -> p t n", p=P)).then_inc(x_got.sem, 16)
            sp.sem_inc(stored.sem, 1)
            with sp.Fori(0, TURNS) as p:
                for c in range(DC):
                    sp.wait_ge(item_done.sem, item_done.at(p, number["q", c] + 1))
                    for i in range(2):
                        sp.dma_start(dram["q_scr"][i, c * P:(c + 1) * P, :], qT[i][:, c, :].bitcast(F32)).then_inc(q_out.sem, 16)
                sp.wait_ge(q_out.sem, q_out.at(p, 32 * DC))
                sp.wait_ge(p_ok.sem, p_ok.at(p, 0))
                for r, i in enumerate((0, 1, 0)):
                    sp.dma_start(q3[HD0 * r:HD0 * (r + 1), :, :].bitcast(F32),
                                 dram["q_scr"][i].rearrange("(h d) t -> d h t", d=HD0)).then_inc(q3_got.sem, 16)
                sp.wait_ge(item_done.sem, item_done.at(p, number["norm", TP - 1] + 1))
                sp.dma_start(x_in[:], dram["x"].rearrange("(u t p) n -> u p t n", t=TP, p=P)[ds((p + 1) % TURNS, 1)]
                             .rearrange("o p t n -> (o p) t n")).then_inc(x_got.sem, 16)
                sp.dma_start(dram["xn1"][ds(p, 1)].rearrange("o p n -> (o p) n"),
                             xn1[:].rearrange("p t n -> p (t n)")).then_inc(stored.sem, 16)
                for i in range(2):
                    sp.dma_start(dram["xn1T"][ds(2 * p + i, 1)].rearrange("o p n -> (o p) n"),
                                 xn1T[i][:].bitcast(F32).rearrange("p c n -> p (c n)")).then_inc(stored.sem, 16)
                sp.wait_ge(item_done.sem, item_done.at(p, NI))
                sp.dma_start(dram["x1"][ds(p, 1)].rearrange("o p n -> (o p) n"),
                             x1[:].rearrange("p t n -> p (t n)")).then_inc(stored.sem, 16)
                sp.dma_start(dram["logits"][ds(p, 1)].rearrange("o p n -> (o p) n"),
                             lg[:].rearrange("p t n -> p (t n)")).then_inc(stored.sem, 16)
            sp.wait_ge(stored.sem, stored.at(TURNS, 0))
            sp.wait_ge(x_got.sem, 16 * (TURNS + 1))

        @block.gpsimd
        def _(pool):
            pool.sem_inc(h_low.sem, 2)
            pool.memset(minus_half[:], -0.5).then_inc(half_ok, 1)
            pool.wait_ge(half_ok, 1)

            def inverse_root(p, n, k):
                pool.wait_ge(var_ok.sem, var_ok.at(p, n + 1))
                at = 0 if n == 0 else TP - 1 + n
                pool.tensor_tensor(rstd[:, at:at + k], var_eps[:, at:at + k], minus_half[:, at:at + k], ALU.pow).then_inc(rstd_ok.sem, 1)

            with pool.Fori(0, TURNS) as p:
                inverse_root(p, 0, TP)
                for n, ((high, low), m) in enumerate([(hT, m) for m in range(len(HT))] + [(sT, m) for m in range(len(ST))]):
                    if n == len(HT):
                        for i in range(TP):
                            inverse_root(p, 1 + i, 1)
                    pool.wait_ge(h_high.sem, h_high.at(p, n + 1))
                    pool.tensor_tensor(low[:, m, :], h_f[:, n % 2, :], high[:, m, :].bitcast(F32),
                                       ALU.subtract).then_inc(h_low.sem, 1)

        @block.scalar
        def _(act):
            act.sem_inc(p_ok.sem, 2)

            def exps(p, n):
                s, t, h0, nh = units[n]
                w = (t + 1) * P
                act.wait_ge(max_ok.sem, max_ok.at(p, n + 1))
                for h in range(nh):
                    last = act.activation(probs[:, n % 2, h * w:(h + 1) * w], ps_s[n % 2][:, h * w:(h + 1) * w], ACT.Exp,
                                          bias=neg_max[:, n % 2, h:h + 1], scale=1.0,
                                          accum_out=sums[:, 2 * s + t, h0 + h:h0 + h + 1])
                last.then_inc(p_ok.sem, 1)

            def high_probs(p, n):
                act.wait_ge(t_full.sem, t_full.at(p, n + 1))
                act.wait_ge(pv_ok.sem, pv_ok.at(p, n - 1))
                act.activation(pT[0][:, n % 2, :], ps_t[:], ACT.Copy).then_inc(t_high.sem, 1)

            def tanh_of(p, item, m, scale):
                act.wait_ge(item_full.sem, item_full.at(p, number[item] + 1))
                act.activation(tanh_g[:, m % 2, :], bank(item)[:], ACT.Tanh, scale=scale).then_inc(item_act.sem, 1)

            def high_hidden(p, item, m, n, dst):
                act.wait_ge(item_done.sem, item_done.at(p, number[item] + 1))
                act.activation(dst[:, m, :], h_f[:, n % 2, :], ACT.Copy).then_inc(h_high.sem, 1)

            def high_of(p, item, dst, src, bias=None):
                act.wait_ge(item_full.sem, item_full.at(p, number[item] + 1))
                if bias is None:
                    act.activation(dst, src, ACT.Copy).then_inc(item_act.sem, 1)
                else:
                    act.activation(dst, src, ACT.Identity, bias=bias).then_inc(item_act.sem, 1)

            with act.Fori(0, TURNS) as p:
                for c in range(DC):
                    high_of(p, ("xT", c), xnT[0][:, c, :], bank(("xT", c))[:])
                for c in range(DC):
                    high_of(p, ("q", c), qT[0][:, c, :], bank(("q", c))[:], bq[:, c:c + 1])
                for s in range(2):
                    high_of(p, ("k", s), k3[:, s, :], bank(("k", s))[0:48, 0:SEQ], bk[:])
                for n, step in enumerate(steps):
                    if n < NU:
                        exps(p, n)
                    if n >= 2 and n % 2 == 0 and n // 2 - 1 < len(HT):
                        m = n // 2 - 1
                        high_hidden(p, ("ffn", n - 1), m, m, hT[0])
                    for kind, i in step:
                        if kind == "ffn" and i % 2 == 0:
                            tanh_of(p, (kind, i), i // 2, half_gate[:, i // 2:i // 2 + 1])
                    if 1 <= n <= NU:
                        high_probs(p, n - 1)
                    for kind, i in step:
                        if kind == "ctx":
                            high_of(p, (kind, i), cT[0][:, i, :, :].rearrange("p c n -> p (c n)"), bank((kind, i))[:, 0:D])
                        if kind == "norm":
                            if i == 0:
                                act.wait_ge(stored.sem, stored.at(p, 0))
                            high_of(p, (kind, i), xn1T[0][:, :, i * P:(i + 1) * P],
                                    bank((kind, i))[:, 0:D].rearrange("p (c n) -> p c n", c=DC))
                for m in range(len(ST)):
                    if m >= 1:
                        high_hidden(p, ("ffs", 2 * m - 1), m - 1, len(HT) + m - 1, sT[0])
                    tanh_of(p, ("ffs", 2 * m), m, 0.5)
                high_hidden(p, ("ffs", 2 * len(ST) - 1), len(ST) - 1, NH - 1, sT[0])

        @block.vector
        def _(dve):
            dve.sem_inc(item_done.sem, len(ps_m))
            dve.sem_inc(t_low.sem, 1)
            dve.sem_inc(ctx_free.sem, 1)

            per_turn = [0]

            def link(p, ins):
                per_turn[0] += 1
                ins.then_inc(own.sem, 1)
                dve.wait_ge(own.sem, own.at(p, per_turn[0]))

            def count(ins):
                per_turn[0] += 1
                ins.then_inc(own.sem, 1)

            def settle(p):
                dve.wait_ge(own.sem, own.at(p, per_turn[0]))

            def norm(p, n, xs, outs, done):
                k = len(xs)
                at = 0 if n == 0 else TP - 1 + n
                for t in range(k):
                    count(dve.bn_stats(stats[:, at + t, :], xs[t]))
                settle(p)
                dve.memset(var_eps[:, at:at + k], 0.0)
                for t in range(k):
                    count(dve.bn_aggr(mv[:, at + t, :], stats[:, at + t, :]))
                settle(p)
                dve.tensor_scalar(var_eps[:, at:at + k], mv[:, at:at + k, 1], EPS, None, ALU.add).then_inc(var_ok.sem, 1)
                dve.wait_ge(rstd_ok.sem, rstd_ok.at(p, n + 1))
                for t in range(k):
                    dve.tensor_scalar(outs[t], xs[t], mv[:, at + t, 0:1], rstd[:, at + t:at + t + 1], ALU.subtract, ALU.mult)\
                        .then_inc(done.sem, 1)

            def low_of(p, item, dst, src, high, bias=None):
                dve.wait_ge(item_act.sem, item_act.at(p, act_number[item] + 1))
                if bias is None:
                    dve.tensor_tensor(dst, src, high.bitcast(F32), ALU.subtract).then_inc(item_done.sem, 1)
                else:
                    dve.scalar_tensor_tensor(out=dst, in0=src, scalar=bias, in1=high.bitcast(F32), op0=ALU.add,
                                             op1=ALU.subtract).then_inc(item_done.sem, 1)

            def gate_tile(p, item, m):
                dve.wait_ge(item_act.sem, item_act.at(p, act_number[item] + 1))
                dve.scalar_tensor_tensor(out=gated[:, m % 2, :], in0=tanh_g[:, m % 2, :], scalar=1.0, in1=bank(item)[:],
                                         op0=ALU.add, op1=ALU.mult).then_inc(item_done.sem, 1)

            def up_tile(p, item, n, scale):
                dve.wait_ge(item_full.sem, item_full.at(p, number[item] + 1))
                dve.wait_ge(item_done.sem, item_done.at(p, number[item[0], item[1] - 1] + 1))
                dve.wait_ge(h_low.sem, h_low.at(p, n - 1))
                dve.scalar_tensor_tensor(out=h_f[:, n % 2, :], in0=bank(item)[:], scalar=scale, in1=gated[:, item[1] // 2 % 2, :],
                                         op0=ALU.mult, op1=ALU.mult).then_inc(item_done.sem, 1)

            def context(p, s, t):
                n = last_unit[s, t]
                dve.wait_ge(pv_ok.sem, pv_ok.at(p, n + 1))
                dve.tensor_reduce(ctx_f[:], ps_c[:].rearrange("p (h i d) -> p h d i", i=2, d=HD0), AX.X, ALU.add)\
                    .then_inc(ctx_free.sem, 1)
                link(p, dve.reciprocal(rinv[:], sums[:, 2 * s + t, :]))
                dve.wait_ge(ctx_free.sem, ctx_free.at(p, 2 * s + t + 1))
                dve.tensor_tensor(ctx_n[:].rearrange("p (h d) -> p h d", h=HEADS0), ctx_f[:],
                                  rinv[:].unsqueeze(2).to_broadcast([P, HEADS0, HD0]), ALU.mult).then_inc(ctx_ok.sem, 1)

            def body(p):
                dve.wait_ge(x_got.sem, x_got.at(p, 16))
                norm(p, 0, [x_in[:, t, :] for t in range(TP)], [xn[:, t, :] for t in range(TP)], ln_done)
                for c in range(DC):
                    low_of(p, ("xT", c), xnT[1][:, c, :], bank(("xT", c))[:], xnT[0][:, c, :])
                for c in range(DC):
                    low_of(p, ("q", c), qT[1][:, c, :], bank(("q", c))[:], qT[0][:, c, :], bq[:, c:c + 1])
                for s in range(2):
                    low_of(p, ("k", s), k3[32:48, s, :], bank(("k", s))[32:48, 0:SEQ], k3[32:48, s, :], bk[32:48, :])
                    dve.wait_ge(item_full.sem, item_full.at(p, number["v", s] + 1))
                    link(p, dve.tensor_tensor(vf[:, s], bank(("v", s))[:, 0:2 * HD0].rearrange("p (t d) -> p t d", t=2), bv[:], ALU.add))
                    link(p, dve.tensor_copy(vs[:, 2 * s:2 * s + 2, 0, :], vf[:, s]))
                    dve.tensor_tensor(vs[:, 2 * s:2 * s + 2, 1, :], vf[:, s], vs[:, 2 * s:2 * s + 2, 0, :].bitcast(F32), ALU.subtract)\
                        .then_inc(item_done.sem, 1)
                for n, step in enumerate(steps):
                    if n < NU:
                        s, t, h0, nh = units[n]
                        dve.wait_ge(s_full.sem, s_full.at(p, n + 1))
                        dve.tensor_reduce(neg_max[:, n % 2, 0:nh], ps_s[n % 2][:].rearrange("p (h k) -> p h k", h=nh), AX.X,
                                          ALU.max, negate=True).then_inc(max_ok.sem, 1)
                    for item in step:
                        if item[0] == "ffn":
                            m = item[1] // 2
                            if item[1] % 2 == 0:
                                gate_tile(p, item, m)
                            else:
                                up_tile(p, item, m, scale_h[:, m:m + 1])
                    if 1 <= n <= NU:
                        dve.wait_ge(t_high.sem, t_high.at(p, n))
                        dve.tensor_tensor(pT[1][:, (n - 1) % 2, :], ps_t[:], pT[0][:, (n - 1) % 2, :].bitcast(F32), ALU.subtract)\
                            .then_inc(t_low.sem, 1)
                    if n >= 2:
                        for (s, t), last in last_unit.items():
                            if last == n - 2:
                                context(p, s, t)
                    for item in step:
                        kind, i = item
                        if kind == "ctx":
                            low_of(p, item, cT[1][:, i, :, :].rearrange("p c n -> p (c n)"), bank(item)[:, 0:D],
                                   cT[0][:, i, :, :].rearrange("p c n -> p (c n)"))
                        if kind == "out":
                            dve.wait_ge(item_full.sem, item_full.at(p, number[item] + 1))
                            link(p, dve.tensor_tensor(down_f[:], bank(item)[:, D:2 * D], s_down[:], ALU.mult))
                            dve.tensor_tensor(both_f[:], bank(item)[:, 0:D], down_f[:], ALU.add).then_inc(item_done.sem, 1)
                            dve.wait_ge(item_done.sem, item_done.at(p, number[item] + 1))
                            if i == 0:
                                dve.wait_ge(stored.sem, stored.at(p, 0))
                            link(p, dve.tensor_tensor(x1[:, i, :], x_in[:, i, :], both_f[:], ALU.add))
                            norm(p, 1 + i, [x1[:, i, :]], [xn1[:, i, :]], norm1_ok)
                        if kind == "norm":
                            low_of(p, item, xn1T[1][:, :, i * P:(i + 1) * P],
                                   bank(item)[:, 0:D].rearrange("p (c n) -> p c n", c=DC), xn1T[0][:, :, i * P:(i + 1) * P])
                for m in range(len(ST)):
                    gate_tile(p, ("ffs", 2 * m), m)
                    up_tile(p, ("ffs", 2 * m + 1), len(HT) + m, 0.5)
                for i in range(TP):
                    dve.wait_ge(item_full.sem, item_full.at(p, number["sum", i] + 1))
                    link(p, dve.tensor_copy(lg[:, i, :], bank(("sum", i))[:, D:D + EXPERTS]))
                    dve.tensor_tensor(x1[:, i, :], x1[:, i, :], bank(("sum", i))[:, 0:D], ALU.add).then_inc(item_done.sem, 1)

            own.per_turn = LINKS
            with dve.Fori(0, TURNS) as p:
                body(p)
            assert per_turn[0] == LINKS, per_turn[0]

        @block.tensor
        def _(pe):
            pe.sem_inc(pv_ok.sem, 2)

            def product3(out, lhs, rhs, start, stop):
                for n, (i, j) in enumerate(((0, 0), (0, 1), (1, 0))):
                    last = pe.matmul(out, lhs[i], rhs[j], start=start and n == 0, stop=stop and n == 2, skip_group_check=True)
                return last

            def body(p):
                def begin(item):
                    pe.wait_ge(item_done.sem, item_done.at(p, number[item] + 1 - len(ps_m)))
                    return bank(item)

                def full(last):
                    last.then_inc(item_full.sem, 1)

                def after(item):
                    pe.wait_ge(item_done.sem, item_done.at(p, number[item] + 1))

                for c in range(DC):
                    out = begin(("xT", c))
                    for t in range(TP):
                        if c == 0:
                            pe.wait_ge(ln_done.sem, ln_done.at(p, t + 1))
                        last = pe.transpose(out[:, t * P:(t + 1) * P], xn[:, t, c * P:(c + 1) * P], ident[:])
                    full(last)
                after(("xT", 1))
                for m in range(DC):
                    out = begin(("q", m))
                    for c in range(DC):
                        last = product3(out[:], [w[:, c, m * P:(m + 1) * P] for w in w_qkv], [x[:, c, :] for x in xnT],
                                        c == 0, c == DC - 1)
                    full(last)
                for s in range(2):
                    out = begin(("k", s))
                    for c in range(DC):
                        last = product3(out[:, 0:SEQ], [w[:, c, D:D + P] for w in w_qkv],
                                        [x[:, c, s * SEQ:(s + 1) * SEQ] for x in xnT], c == 0, c == DC - 1)
                    full(last)
                    out = begin(("v", s))
                    for t in range(2):
                        for c in range(DC):
                            last = product3(out[:, t * HD0:(t + 1) * HD0],
                                            [x[:, c, (2 * s + t) * P:(2 * s + t + 1) * P] for x in xnT],
                                            [w[:, c, D + P:] for w in w_qkv], c == 0, c == DC - 1)
                    full(last)

                def scores(n):
                    s, t, h0, nh = units[n]
                    w = (t + 1) * P
                    out = ps_s[n % 2]
                    pe.wait_ge(p_ok.sem, p_ok.at(p, n - 1))
                    by_head = out[:].rearrange("p (h k) -> p h k", h=nh)
                    pe.matmul(by_head[:, :, t * P:w], ident_r[:], mask_r[:, 0:nh, :], start=True, stop=False, skip_group_check=True)
                    for h in range(nh):
                        last = pe.matmul(out[:, h * w:(h + 1) * w], q3[:, h0 + h, (2 * s + t) * P:(2 * s + t + 1) * P],
                                         k3[:, s, 0:w], start=False, stop=(h == nh - 1), skip_group_check=True)
                    last.then_inc(s_full.sem, 1)

                def transposes(n):
                    pe.wait_ge(p_ok.sem, p_ok.at(p, n + 1))
                    pe.wait_ge(t_low.sem, t_low.at(p, n))
                    for b in range(4):
                        last = pe.transpose(ps_t[:, b * P:(b + 1) * P], probs[:, n % 2, b * P:(b + 1) * P], ident[:])
                    last.then_inc(t_full.sem, 1)

                def context(n):
                    s, t, h0, nh = units[n]
                    pe.wait_ge(t_low.sem, t_low.at(p, n + 1))
                    if h0 == 0:
                        pe.wait_ge(ctx_free.sem, ctx_free.at(p, 2 * s + t))
                    for h in range(nh):
                        at = (h0 + h) * 2 * HD0
                        for k in range(t + 1):
                            b = h * (t + 1) + k
                            v = vs[:, 2 * s + k, :, :].rearrange("p i d -> p (i d)")
                            pe.matmul(ps_c[:, at:at + 2 * HD0], pT[0][:, n % 2, b * P:(b + 1) * P], v,
                                      start=(h0 + h == 0 and k == 0), stop=False, skip_group_check=True)
                            last = pe.matmul(ps_c[:, at:at + HD0], pT[1][:, n % 2, b * P:(b + 1) * P], v[:, 0:HD0],
                                             start=False, stop=(h0 + h == HEADS0 - 1 and k == t), skip_group_check=True)
                    last.then_inc(pv_ok.sem, 1)

                def item_work(item):
                    kind, i = item
                    if kind == "norm":
                        pe.wait_ge(norm1_ok.sem, norm1_ok.at(p, i + 1))
                    if kind == "ctx":
                        pe.wait_ge(ctx_ok.sem, ctx_ok.at(p, i + 1))
                    if kind == "out":
                        after(("ctx", i))
                        if i == 0:
                            pe.wait_ge(h_low.sem, h_low.at(p, len(HT)))
                    out = begin(item)
                    if kind == "ffn":
                        w = w_gate if i % 2 == 0 else w_up
                        for c in range(DC):
                            for j in range(2):
                                last = pe.matmul(out[:], w[:, c, HT[i // 2]:HT[i // 2] + P], xnT[j][:, c, :],
                                                 start=(c == 0 and j == 0), stop=(c == DC - 1 and j == 1))
                    if kind in ("ctx", "norm"):
                        src = ctx_n[:] if kind == "ctx" else xn1[:, i, :]
                        for c in range(DC):
                            last = pe.transpose(out[:, c * P:(c + 1) * P], src[:, c * P:(c + 1) * P], ident[:])
                    if kind == "out":
                        pe.matmul(out[:, 0:D], ones_r[:], ob[0][:], start=True, stop=False, skip_group_check=True)
                        pe.matmul(out[:, 0:D], ones_r[:], ob[1][:], start=False, stop=False, skip_group_check=True)
                        for c in range(DC):
                            product3(out[:, 0:D], [x[:, i, c, :] for x in cT], [w[:, c, :] for w in w_o], False, False)
                        for m in range(len(HT)):
                            for j in range(2):
                                last = pe.matmul(out[:, D:2 * D], hT[j][:, m, i * P:(i + 1) * P], w_down[:, m, :],
                                                 start=False, stop=(m == len(HT) - 1 and j == 1), skip_group_check=True)
                    if kind == "ffs":
                        at = (i % 2) * SHARED + ST[i // 2]
                        for c in range(DC):
                            last = product3(out[:], [w[:, c, at:at + P] for w in w_s13], [x[:, c, :] for x in xn1T],
                                            c == 0, c == DC - 1)
                    if kind == "sum":
                        for m in range(len(ST)):
                            product3(out[:, 0:D], [x[:, m, i * P:(i + 1) * P] for x in sT], [w[:, m, :] for w in w_s2],
                                     m == 0, False)
                        for c in range(DC):
                            for a in range(2):
                                for b in range(2):
                                    last = pe.matmul(out[:, D:D + EXPERTS], xn1T[a][:, c, i * P:(i + 1) * P], w_gw[b][:, c, :],
                                                     start=False, stop=(c == DC - 1 and a + b == 2), skip_group_check=True)
                    full(last)

                pe.wait_ge(q3_got.sem, q3_got.at(p, 48))
                for n, step in enumerate(steps):
                    if n < NU:
                        scores(n)
                    for item in step:
                        if item[0] == "ffn":
                            item_work(item)
                    if 1 <= n <= NU:
                        transposes(n - 1)
                    if 2 <= n <= NU + 1:
                        context(n - 2)
                    for item in step:
                        if item[0] != "ffn":
                            item_work(item)
                after(("norm", TP - 1))
                for item in back:
                    if item == ("sum", 0):
                        pe.wait_ge(h_low.sem, h_low.at(p, NH))
                    item_work(item)

            with pe.Fori(0, TURNS) as p:
                body(p)

W_HEAD = 4 * D + 4
W_COLS = 4 * D


class AttentionWeights:

    def __init__(self, nc, ctx):
        self.v, self.o, self.bo = ([ctx.enter_context(nc.sbuf_tensor(f"{name}{i}", shape, R32)) for i in range(2)]
                                   for name, shape in (("w_v", [P, DC, FEAT]), ("w_out", [P, HEADS1 * D]), ("bo", [1, 2, D])))


def stage_attention_weights(nc, dram, kept):
    with ExitStack() as ctx:
        def sb(name, shape, dt=F32):
            return ctx.enter_context(nc.sbuf_tensor(name, shape, dt))

        def sem(name):
            return ctx.enter_context(nc.semaphore(name))

        units = [(m, half) for m in ("wo", "wv", "wq", "wk") for half in range(2)]
        N = FEAT
        RING = 3
        codes = [sb(f"codes{i}", [P, N]) for i in range(RING)]
        scales = [sb(f"scales{i}", [P, N]) for i in range(RING)]
        parts = [[sb(f"parts{a}_{i}", [P, N], R32) for i in range(2)] for a in range(2)]
        rows = sb("rows", [3 * HEADS1, HD1])
        columns = sb("columns", [P, HEADS1, 8])
        bv = [sb(f"bv_wide{i}", [P, HEADS1, P], R32) for i in range(2)]
        raw_bo = sb("raw_bo", [1, 2, D])
        ident = sb("ident_w", [P, P])
        ps = ctx.enter_context(nc.psum_tensor("ps_w", [P, 512], F32))
        ps_b = ctx.enter_context(nc.psum_tensor("ps_b", [P, 512], F32))

        got = [sem(f"w_got{i}") for i in range(RING)]
        rows_got = sem("rows_got")
        id_ok = sem("id_ok")
        turned = sem("turned")
        columns_ok = sem("columns_ok")
        bv_ok = sem("bv_ok")
        b_full = sem("b_full")
        bo_ok = sem("bo_ok")
        prod_ok = sem("prod_ok")
        high_ok = sem("high_ok")
        low_ok = sem("low_ok")
        high_out = [sem(f"high_out{i}") for i in range(2)]
        low_out = [sem(f"low_out{i}") for i in range(2)]
        out = sem("columns_out")
        block = ctx.enter_context(nc.Block())

        def home(n, i):
            m, half = units[n]
            if m == "wo":
                return kept.o[i][:, half * N:(half + 1) * N]
            return kept.v[i][:, half, :] if m == "wv" else parts[n % 2][i][:]

        def stored(n, i):
            m, half = units[n]
            at = (2 * ("wq", "wk").index(m) + i) * D + half * HD1
            return (dram["w_head"][:, :, at:at + HD1].rearrange("h p n -> p h n"),
                    parts[n % 2][i][:].bitcast(F32).rearrange("p (h n) -> p h n", n=HD1))

        @block.sync
        def _(sp):
            for m in range(3):
                sp.dma_start(rows[m * HEADS1:(m + 1) * HEADS1, :], dram["b" + "qkv"[m]].rearrange("(h p) -> h p", p=HD1))\
                    .then_inc(rows_got, 16)
            for i in range(2):
                sp.dma_start(raw_bo[:, i, :], dram["bo"].rearrange("(a n) -> a n", a=1)).then_inc(rows_got, 16)
            for n, (m, half) in enumerate(units):
                if n >= RING:
                    sp.wait_ge(low_ok, n - RING + 1)
                c, sc = dram[m + "_codes"], dram[m + "_scales"]
                to = codes[n % RING][:]
                if m == "wo":
                    c, to = c.rearrange("(a h p) n -> a p h n", a=2, p=P)[half], to.rearrange("p (h n) -> p h n", n=D)
                    sc = sc.rearrange("(a h b) n -> a b h n", a=2, b=P // BLOCK)[half]
                else:
                    c = c[half * P:(half + 1) * P, :]
                    sc = sc.rearrange("(a h b) n -> a b h n", a=2, b=P // BLOCK)[half]
                sp.dma_start(to, c).then_inc(got[n % RING], 16)
                for b in range(P // BLOCK):
                    sp.dma_start(scales[n % RING][b * BLOCK:(b + 1) * BLOCK, :].rearrange("p (c n) -> p c n", n=sc.shape[2]),
                                 sc[b:b + 1].partition_broadcast(BLOCK).rearrange("q o c n -> q (o c) n"))\
                        .then_inc(got[n % RING], 16)

        @block.scalar
        def _(act):
            act.wait_ge(columns_ok, 3)
            act.activation(bv[0][:], columns[:, :, 4:5].to_broadcast([P, HEADS1, P]), ACT.Copy).then_inc(bv_ok, 1)
            for n in range(len(units)):
                act.wait_ge(prod_ok, n + 1)
                if n >= 6:
                    act.wait_ge(high_out[n % 2], 16)
                act.activation(home(n, 0), codes[n % RING][:], ACT.Copy).then_inc(high_ok, 1)
                if n >= 4:
                    act.wait_ge(high_ok, n + 1)
                    act.dma_start(*stored(n, 0)).then_inc(high_out[n % 2], 16)
            act.wait_ge(bo_ok, 2)
            act.activation(kept.bo[0][:], raw_bo[:], ACT.Copy).then_inc(bo_ok, 1)
            for i in range(2):
                act.wait_ge(high_out[i], 32)

        @block.gpsimd
        def _(pool):
            pool.memset(ident[:], 0.0).then_inc(id_ok, 1)
            pool.memset(columns[:], 0.0).then_inc(id_ok, 1)
            pool.wait_ge(id_ok, 2)
            pool.affine_select(out=ident[:], in_=ident[:], compare_op=ALU.not_equal, fill=1.0, base=0,
                               pattern=[[-1, P]], channel_multiplier=1).then_inc(id_ok, 1)
            pool.wait_ge(columns_ok, 3)
            pool.dma_start(dram["w_head"][:, :, W_COLS:W_COLS + 4].rearrange("h p n -> p h n"), columns[:, :, 0:4]).then_inc(out, 16)
            for n in range(4, len(units)):
                pool.wait_ge(low_ok, n + 1)
                pool.dma_start(*stored(n, 1)).then_inc(low_out[n % 2], 16)
            for i in range(2):
                pool.wait_ge(low_out[i], 32)
            pool.wait_ge(out, 16)

        @block.tensor
        def _(pe):
            pe.wait_ge(id_ok, 3)
            pe.wait_ge(rows_got, 80)
            pe.transpose(ps[:, 0:3 * HEADS1], rows[:], ident[0:3 * HEADS1, 0:3 * HEADS1]).then_inc(turned, 1)
            pe.wait_ge(bv_ok, 2)
            pe.wait_ge(low_ok, 2)
            for h in range(HEADS1):
                for n, (i, j) in enumerate(((0, 0), (0, 1), (1, 0))):
                    last = pe.matmul(ps_b[:, 0:D], bv[i][:, h, :], kept.o[j][:, h * D:(h + 1) * D], start=h + n == 0,
                                     stop=h == HEADS1 - 1 and n == 2)
            last.then_inc(b_full, 1)

        @block.vector
        def _(dve):
            dve.wait_ge(turned, 1)
            for m in range(3):
                dve.tensor_scalar(columns[:, :, m + m // 2 * 2], ps[:, m * HEADS1:(m + 1) * HEADS1], HD1 ** -0.5 if m == 0 else 1.0, None,
                                  ALU.mult).then_inc(columns_ok, 1)
            dve.wait_ge(columns_ok, 3)
            dve.wait_ge(bv_ok, 1)
            dve.tensor_tensor(bv[1][:], columns[:, :, 4:5].to_broadcast([P, HEADS1, P]), bv[0][:].bitcast(F32), ALU.subtract)\
                .then_inc(bv_ok, 1)

            def low(n):
                dve.wait_ge(high_ok, n + 1)
                if n >= 6:
                    dve.wait_ge(low_out[n % 2], 16)
                dve.tensor_tensor(home(n, 1), codes[n % RING][:], home(n, 0).bitcast(F32), ALU.subtract).then_inc(low_ok, 1)

            for n, (m, _) in enumerate(units):
                dve.wait_ge(got[n % RING], 80 * (n // RING + 1))
                dve.scalar_tensor_tensor(out=codes[n % RING][:], in0=codes[n % RING][:], scalar=HD1 ** -0.5 if m == "wq" else 1.0,
                                         in1=scales[n % RING][:], op0=ALU.mult, op1=ALU.mult).then_inc(prod_ok, 1)
                if n:
                    low(n - 1)
            low(len(units) - 1)
            dve.wait_ge(b_full, 1)
            for i in range(2):
                dve.tensor_tensor(raw_bo[:, i, :], raw_bo[:, i, :], ps_b[0:1, 0:D], ALU.add).then_inc(bo_ok, 1)
            dve.wait_ge(bo_ok, 3)
            dve.tensor_tensor(kept.bo[1][:], raw_bo[:], kept.bo[0][:].bitcast(F32), ALU.subtract).then_inc(bo_ok, 1)


def stage_attention(nc, dram, route, kept):
    with ExitStack() as ctx:
        def sb(name, shape, dt=F32):
            return ctx.enter_context(nc.sbuf_tensor(name, shape, dt))

        def psum(name):
            return ctx.enter_context(nc.psum_tensor(name, [P, 512], F32))

        def sem(name):
            return ctx.enter_context(nc.semaphore(name))

        ident = sb("ident_a", [P, P])
        ones_f = sb("ones_fa", [1, P])
        ones_r = sb("ones_ra", [1, P], R32)
        xT = [sb(f"xTa{i}", [P, DC, PAIR], R32) for i in range(2)]
        w_qk = [sb(f"w_qk{a}", [P, W_HEAD], R32) for a in range(2)]
        qT = [sb(f"qTa{i}", [P, PAIR], R32) for i in range(2)]
        kT = [sb(f"kTa{i}", [P, PAIR], R32) for i in range(2)]
        v = [sb(f"v{i}", [P, TP, 2 * HD1], R32) for i in range(2)]
        probs = sb("probs_a", [P, 2, 2, SEQ])
        neg_max = sb("neg_max_a", [P, 2, 2])
        sums = sb("sums_a", [P, 2, 2])
        rinv = sb("rinv_a", [P, 2, 2])
        pT = [sb(f"pTa{i}", [P, 2, 512], R32) for i in range(2)]
        oT = [sb(f"oT{i}", [P, PAIR], R32) for i in range(2)]
        x2 = sb("x2a", [P, TP, D])
        RING = 4
        xe = sb("xe", [P, TILES, D])
        ex = [sb(f"ex{k}", [P, RING, D]) for k in range(TOP_K)]
        bank_q, bank_k = psum("bank_q"), psum("bank_k")
        ps_s = [psum(f"ps_sa{i}") for i in range(2)]
        ps_t = [psum(f"ps_ta{i}") for i in range(2)]
        ps_y = [psum(f"ps_y{i}") for i in range(2)]

        H = HEADS1
        w_got = [sem(f"wa_got{a}") for a in range(2)]
        x_got = Signal(sem("xa_got"), 32)
        x2_out = Signal(sem("x2_out"), 16, 1)
        prep = sem("prep_a")
        q_full, k_full, o_full, v_full, y_done = (Signal(sem(n), 1) for n in ("q_full", "k_full", "o_full", "v_full", "y_done"))
        q_high, k_high, v_high, o_high = (Signal(sem(n), 1) for n in ("q_high", "k_high", "v_high", "o_high"))
        q_done = Signal(sem("q_done"), 1)
        k_done = Signal(sem("k_done"), 1)
        o_done = Signal(sem("o_done"), 1, 1)
        v_done = Signal(sem("v_done"), 1, 2)
        s_full = Signal(sem("sa_full"), 2)
        max_ok = Signal(sem("maxa_ok"), 2)
        exp_ok = Signal(sem("exp_ok"), 2, 2)
        rinv_ok = Signal(sem("rinv_ok"), 2)
        p_ok = Signal(sem("pa_ok"), 2)
        t_full = Signal(sem("ta_full"), 2)
        t_high = Signal(sem("ta_high"), 2)
        t_low = Signal(sem("ta_low"), 2, 2)
        xo_ok = Signal(sem("xo_ok"), 2)
        xe_got = sem("xe_got")
        ex_got = [[sem(f"ex_got{k}_{i}") for i in range(RING)] for k in range(TOP_K)]
        weighted = sem("weighted")
        xe_ok = Signal(sem("xe_ok"), TP * TOP_K)

        block = ctx.enter_context(nc.Block())

        def walk(eng, step, end):
            def middle(u):
                with eng.Fori(0, (H - 2) // 2) as j:
                    for a in range(2):
                        step(u, j * 2, 2 + a, j * 2 + 2, j * 2 + a)

            step(0, 0, 0, 0, None)
            step(0, 0, 1, 0, None)
            with eng.Fori(0, TURNS - 1) as u:
                middle(u)
                for a in range(2):
                    step(u, 0, H + a, 0, H - 2 + a)
                end(u)
            middle(TURNS - 1)
            for a in range(2):
                step(TURNS - 1, 0, H + a, None, H - 2 + a)
            end(TURNS - 1)

        def at(signal, base, i, n):
            return base * signal.per_turn + (signal.head + i * signal.per_turn + n)

        def parts_of(i, pair, y_head):
            return pair is not None, (i >= 1 and (pair is not None or i == H)), y_head is not None

        @block.sync
        def _(sp):
            def weights(a, head):
                sp.dma_start(w_qk[a][:].bitcast(F32), head).then_inc(w_got[a], 16)

            for a in range(2):
                weights(a, dram["w_head"][a])
            sp.dma_start(xe[:].rearrange("p (u t) n -> p u (t n)", u=TURNS), dram["x1"].rearrange("u p n -> p u n")).then_inc(xe_got, 16)
            for i in range(2):
                sp.dma_start(xT[i][:].bitcast(F32).rearrange("p c n -> p (c n)"), dram["xn1T"][i]).then_inc(x_got.sem, 16)
            with sp.Fori(0, TURNS) as u:
                with sp.Fori(0, H // 2) as j:
                    for a in range(2):
                        sp.wait_ge(k_done.sem, at(k_done, u * H + j * 2, a, 1))
                        weights(a, dram["w_head"][ds((j * 2 + (2 + a)) % H, 1)].rearrange("o p n -> (o p) n"))
                sp.wait_ge(v_full.sem, at(v_full, u * H, H - 1, 1))
                for i in range(2):
                    sp.dma_start(xT[i][:].bitcast(F32).rearrange("p c n -> p (c n)"),
                                 dram["xn1T"][ds((u * 2 + (2 + i)) % (2 * TURNS), 1)].rearrange("o p n -> (o p) n"))\
                        .then_inc(x_got.sem, 16)
            sp.wait_ge(x_got.sem, 32 * (TURNS + 1))
            for a in range(2):
                sp.wait_ge(w_got[a], 16 * (TURNS * H // 2 + 1))

        @block.gpsimd
        def _(pool):
            pool.memset(ident[:], 0.0).then_inc(prep, 1)
            pool.memset(ones_f[:], 1.0).then_inc(prep, 1)
            pool.wait_ge(prep, 2)
            pool.affine_select(out=ident[:], in_=ident[:], compare_op=ALU.not_equal, fill=1.0, base=0,
                               pattern=[[-1, P]], channel_multiplier=1).then_inc(prep, 1)
            pool.wait_ge(xe_got, 16)

            def gather(t):
                for k in range(TOP_K):
                    pool.indirect_dma_start(ex[k][:, t % RING, :], None, dram["ys"],
                                            bass.IndirectOffsetOnAxis(ap=route.slot[k][:, t:t + 1], axis=0))\
                        .then_inc(ex_got[k][t % RING], 16)

            for t in range(RING - 1):
                gather(t)
            for t in range(TILES):
                for k in range(TOP_K):
                    pool.wait_ge(ex_got[k][t % RING], 16 * (t // RING + 1))
                    pool.tensor_tensor(ex[k][:, t % RING, :], ex[k][:, t % RING, :],
                                       route.weight[k][:, t:t + 1].to_broadcast([P, D]), ALU.mult).then_inc(weighted, 1)
                for k in range(TOP_K):
                    pool.wait_ge(weighted, TOP_K * t + k + 1)
                    if k:
                        pool.wait_ge(xe_ok.sem, TOP_K * t + k)
                    pool.tensor_tensor(xe[:, t, :], xe[:, t, :], ex[k][:, t % RING, :], ALU.add).then_inc(xe_ok.sem, 1)
                if t + RING - 1 < TILES:
                    if t:
                        pool.wait_ge(xe_ok.sem, TOP_K * t)
                    gather(t + RING - 1)

        @block.scalar
        def _(act):
            act.wait_ge(prep, 3)
            act.activation(ones_r[:], ones_f[:], ACT.Copy).then_inc(prep, 1)
            act.sem_inc(exp_ok.sem, 2)
            act.sem_inc(x2_out.sem, 1)

            def step(u, first, i, pair, y_head):
                base, a = u * H + first, i % 2
                now, back, _ = parts_of(i, pair, y_head)

                def take_v():
                    act.wait_ge(v_full.sem, at(v_full, base, i, 1))
                    act.activation(v[0][:, 2 * a:2 * a + 2, :].rearrange("p t n -> p (t n)"), (bank_k, bank_q)[a][:], ACT.Copy)\
                        .then_inc(v_high.sem, 1)

                if now:
                    act.wait_ge(q_full.sem, at(q_full, base, i, 1))
                    act.activation(qT[0][:], bank_q[:], ACT.Identity, bias=w_qk[a][:, W_COLS:W_COLS + 1].bitcast(F32))\
                        .then_inc(q_high.sem, 1)
                    act.wait_ge(k_full.sem, at(k_full, base, i, 1))
                    act.activation(kT[0][:], bank_k[:], ACT.Identity, bias=w_qk[a][:, W_COLS + 1:W_COLS + 2].bitcast(F32))\
                        .then_inc(k_high.sem, 1)
                if back:
                    for s in range(2):
                        act.wait_ge(t_full.sem, at(t_full, base, i - 1, s + 1))
                        act.activation(pT[0][:, s, :], ps_t[s][:], ACT.Copy).then_inc(t_high.sem, 1)
                if now and a:
                    take_v()
                if now:
                    for s in range(2):
                        act.wait_ge(max_ok.sem, at(max_ok, base, i, s + 1))
                        for t in range(2):
                            last = act.activation(probs[:, s, t, :], ps_s[s][:, t * SEQ:(t + 1) * SEQ], ACT.Exp,
                                                  bias=neg_max[:, s, t:t + 1], scale=1.0, accum_out=sums[:, s, t:t + 1])
                        last.then_inc(exp_ok.sem, 1)
                if back:
                    act.wait_ge(o_full.sem, at(o_full, base, i - 1, 1))
                    act.activation(oT[0][:], ps_t[0][:], ACT.Copy).then_inc(o_high.sem, 1)
                if now and not a:
                    take_v()

            def end(u):
                act.wait_ge(xo_ok.sem, xo_ok.at(u, 2))
                act.dma_start(dram["out"].rearrange("(u t p) n -> u p t n", t=TP, p=P)[ds(u, 1)].rearrange("o p t n -> (o p) t n"), x2[:])\
                    .then_inc(x2_out.sem, 16)

            walk(act, step, end)
            act.wait_ge(x2_out.sem, x2_out.at(TURNS, 0))

        @block.vector
        def _(dve):
            dve.sem_inc(v_done.sem, 2)
            dve.sem_inc(o_done.sem, 1)
            dve.sem_inc(t_low.sem, 2)

            def low(dst, src, high, bias, signal):
                dve.scalar_tensor_tensor(out=dst, in0=src, scalar=bias, in1=high.bitcast(F32), op0=ALU.add,
                                         op1=ALU.subtract).then_inc(signal.sem, 1)

            def step(u, first, i, pair, y_head):
                base, a = u * H + first, i % 2
                now, back, _ = parts_of(i, pair, y_head)

                def take_v():
                    dve.wait_ge(v_high.sem, at(v_high, base, i, 1))
                    dve.tensor_tensor(v[1][:, 2 * a:2 * a + 2, :].rearrange("p t n -> p (t n)"), (bank_k, bank_q)[a][:],
                                      v[0][:, 2 * a:2 * a + 2, :].rearrange("p t n -> p (t n)").bitcast(F32), ALU.subtract)\
                        .then_inc(v_done.sem, 1)

                if now:
                    dve.wait_ge(q_high.sem, at(q_high, base, i, 1))
                    low(qT[1][:], bank_q[:], qT[0][:], w_qk[a][:, W_COLS:W_COLS + 1].bitcast(F32), q_done)
                    dve.wait_ge(k_high.sem, at(k_high, base, i, 1))
                    low(kT[1][:], bank_k[:], kT[0][:], w_qk[a][:, W_COLS + 1:W_COLS + 2].bitcast(F32), k_done)
                if back:
                    for s in range(2):
                        dve.wait_ge(t_high.sem, at(t_high, base, i - 1, s + 1))
                        dve.tensor_tensor(pT[1][:, s, :], ps_t[s][:], pT[0][:, s, :].bitcast(F32), ALU.subtract)\
                            .then_inc(t_low.sem, 1)
                if now and a:
                    take_v()
                if i == H + 1:
                    dve.wait_ge(y_done.sem, at(y_done, u * H, H, 0))
                    dve.wait_ge(x2_out.sem, x2_out.at(u, 0))
                    dve.wait_ge(xe_ok.sem, xe_ok.at(u, TP * TOP_K))
                    tiles = xe[:, ds(u * TP, TP), :]
                    for b in range(2):
                        dve.tensor_tensor(x2[:, 2 * b:2 * b + 2, :].rearrange("p t n -> p (t n)"),
                                          tiles[:, 2 * b:2 * b + 2, :].rearrange("p t n -> p (t n)"), ps_y[b][:], ALU.add)\
                            .then_inc(xo_ok.sem, 1)
                if now:
                    for s in range(2):
                        dve.wait_ge(s_full.sem, at(s_full, base, i, s + 1))
                        dve.tensor_reduce(neg_max[:, s, :], ps_s[s][:].rearrange("p (t k) -> p t k", t=2), AX.X, ALU.max,
                                          negate=True).then_inc(max_ok.sem, 1)
                    for s in range(2):
                        dve.wait_ge(exp_ok.sem, at(exp_ok, base, i, s + 1))
                        dve.reciprocal(rinv[:, s, :], sums[:, s, :]).then_inc(rinv_ok.sem, 1)
                        dve.wait_ge(rinv_ok.sem, at(rinv_ok, base, i, s + 1))
                        for t in range(2):
                            last = dve.tensor_scalar(probs[:, s, t, :], probs[:, s, t, :], rinv[:, s, t:t + 1], None, ALU.mult)
                        last.then_inc(p_ok.sem, 1)
                if back:
                    dve.wait_ge(o_high.sem, at(o_high, base, i - 1, 1))
                    dve.tensor_tensor(oT[1][:], ps_t[0][:], oT[0][:].bitcast(F32), ALU.subtract).then_inc(o_done.sem, 1)
                if now and not a:
                    take_v()

            walk(dve, step, lambda u: None)

        @block.tensor
        def _(pe):
            def product3(out, lhs, rhs, start, stop):
                for n, (i, j) in enumerate(((0, 0), (0, 1), (1, 0))):
                    last = pe.matmul(out, lhs[i], rhs[j], start=start and n == 0, stop=stop and n == 2, skip_group_check=True)
                return last

            def start_sums():
                for b in range(2):
                    for n in range(2):
                        pe.matmul(ps_y[b][:], ones_r[:], kept.bo[n][:].rearrange("a i n -> a (i n)"), start=(n == 0), stop=False,
                                  skip_group_check=True)

            def project(out, a, m, signal):
                for c in range(DC):
                    w = [w_qk[a][:, (2 * m + i) * D + c * HD1:(2 * m + i) * D + (c + 1) * HD1] for i in range(2)]
                    last = product3(out[:], w, [x[:, c, :] for x in xT], c == 0, c == DC - 1)
                last.then_inc(signal.sem, 1)

            def project_v(base, i, pair):
                a = i % 2
                if a:
                    pe.wait_ge(q_done.sem, at(q_done, base, i, 1))
                else:
                    pe.wait_ge(k_done.sem, at(k_done, base, i, 1))
                for n in range(2):
                    t = 2 * a + n
                    for c in range(DC):
                        last = product3((bank_k, bank_q)[a][:, n * 2 * HD1:(n + 1) * 2 * HD1], [x[:, c, t * P:(t + 1) * P] for x in xT],
                                        [w[:, c, ds(pair * HD1, 2 * HD1)] for w in kept.v], c == 0, c == DC - 1)
                last.then_inc(v_full.sem, 1)

            def step(u, first, i, pair, y_head):
                base, a = u * H + first, i % 2
                now, back, two_back = parts_of(i, pair, y_head)
                if now:
                    if i % H == 0:
                        pe.wait_ge(x_got.sem, x_got.at(u, 32 * (i // H + 1)))
                    pe.wait_ge(w_got[a], base * 8 + 16 * (i // 2 + 1))
                    pe.wait_ge(v_done.sem, at(v_done, base, i - 1 - a, 1))
                    project(bank_q, a, 0, q_full)
                    pe.wait_ge(v_done.sem, at(v_done, base, i - 2 + a, 1))
                    project(bank_k, a, 1, k_full)
                if back:
                    for s in range(2):
                        pe.wait_ge(p_ok.sem, at(p_ok, base, i - 1, s + 1))
                        pe.wait_ge(t_low.sem, at(t_low, base, i - 2, s + 1))
                        if s == 0:
                            pe.wait_ge(o_done.sem, at(o_done, base, i - 2, 1))
                        for k in range(2):
                            for t in range(2):
                                last = pe.transpose(ps_t[s][:, (2 * k + t) * P:(2 * k + t + 1) * P],
                                                    probs[:, s, t, k * P:(k + 1) * P], ident[:])
                        last.then_inc(t_full.sem, 1)
                if now and a:
                    project_v(base, i, pair)
                if two_back:
                    pe.wait_ge(o_done.sem, at(o_done, base, i - 2, 1))
                    for t in range(TP):
                        last = product3(ps_y[t // 2][:, (t % 2) * D:(t % 2 + 1) * D], [o[:, t * P:(t + 1) * P] for o in oT],
                                        [w[:, ds(y_head * D, D)] for w in kept.o], False, i == H + 1)
                    last.then_inc(y_done.sem, 1)
                if now:
                    pe.wait_ge(k_done.sem, at(k_done, base, i, 1))
                    for s in range(2):
                        pe.wait_ge(exp_ok.sem, at(exp_ok, base, i - 1, s + 1))
                        for t in range(2):
                            last = product3(ps_s[s][:, t * SEQ:(t + 1) * SEQ],
                                            [x[:, (2 * s + t) * P:(2 * s + t + 1) * P] for x in qT],
                                            [x[:, s * SEQ:(s + 1) * SEQ] for x in kT], True, True)
                        last.then_inc(s_full.sem, 1)
                if back:
                    pe.wait_ge(v_done.sem, at(v_done, base, i - 1 + a, 1))
                    b = 1 - a
                    for s in range(2):
                        pe.wait_ge(t_low.sem, at(t_low, base, i - 1, s + 1))
                        for k in range(2):
                            last = product3(ps_t[0][:, s * SEQ:(s + 1) * SEQ], [x[:, 2 * s + k, b * HD1:(b + 1) * HD1] for x in v],
                                            [x[:, s, k * SEQ:(k + 1) * SEQ] for x in pT], k == 0, k == 1)
                    last.then_inc(o_full.sem, 1)
                if now and not a:
                    project_v(base, i, pair)
                if now and i == H + 1:
                    pe.wait_ge(xo_ok.sem, xo_ok.at(u, 2))
                    start_sums()

            pe.wait_ge(prep, 4)
            start_sums()
            walk(pe, step, lambda u: None)


TOP_K = 2
SLOT_TILES = -(-(TOP_K * TOKENS + EXPERTS * (P - 1)) // P)
SLOT_TILES += SLOT_TILES % 2
SLOTS = SLOT_TILES * P


def stage_routing(nc, dram, route):
    with ExitStack() as ctx:
        def sb(name, shape, dt=F32):
            return ctx.enter_context(nc.sbuf_tensor(name, shape, dt))

        def sem(name):
            return ctx.enter_context(nc.semaphore(name))

        lg = sb("lg_r", [P, TILES, EXPERTS])
        work = [sb(f"work{i}", [P, TILES, EXPERTS]) for i in range(2)]
        probs = sb("probs_r", [P, TILES, EXPERTS])
        masks = [sb(f"mask{i}", [P, TILES, EXPERTS]) for i in range(TOP_K)]
        chosen = sb("chosen", [P, TILES, EXPERTS], R32)
        rank = sb("rank", [P, TILES, EXPERTS])
        totals = [sb(f"totals{i}", [P, TILES, EXPERTS]) for i in range(2)]
        row = sb("row_r", [P, TILES])
        falling = sb("falling", [P, EXPERTS])
        place = sb("place", [P, TILES])
        counts_i = sb("counts_i", [P, EXPERTS], I32)
        tiles_i = sb("tiles_i", [P, EXPERTS], I32)
        tiles_f = sb("tiles_f", [P, EXPERTS])
        ends = [sb(f"ends{i}", [P, EXPERTS]) for i in range(2)]
        first = sb("first", [P, EXPERTS])
        tile_no = sb("tile_no", [1, SLOT_TILES])
        passed = sb("passed", [1, SLOT_TILES, EXPERTS])
        expert_f = sb("expert_f", [1, SLOT_TILES])
        before_f = sb("before_f", [P, P])
        before = sb("before", [P, P], R32)
        all_f = sb("all_f", [P, P])
        ones = sb("ones_r2", [P, P], R32)
        ps_rank = ctx.enter_context(nc.psum_tensor("ps_rank", [P, 512], F32))
        ps_total = ctx.enter_context(nc.psum_tensor("ps_total", [P, 512], F32))

        got = sem("lg_got")
        made = sem("made")
        cast = sem("cast")
        shifted = sem("shifted")
        exp_done = sem("exp_done")
        own = sem("own_r")
        chosen_ok = sem("chosen_ok")
        summed = sem("summed")
        block = ctx.enter_context(nc.Block())

        def flat(t):
            return t[:].rearrange("p t e -> p (t e)")

        @block.sync
        def _(sp):
            sp.dma_start(lg[:].rearrange("p (u t) e -> p u (t e)", u=TURNS), dram["logits"].rearrange("u p n -> p u n"))\
                .then_inc(got, 16)

        @block.gpsimd
        def _(pool):
            pool.memset(before_f[:], 1.0).then_inc(made, 1)
            pool.memset(all_f[:], 1.0).then_inc(made, 1)
            pool.iota(falling[:], [[-1, EXPERTS]], base=EXPERTS, channel_multiplier=0, allow_small_or_imprecise_dtypes=True)\
                .then_inc(made, 1)
            pool.iota(tile_no[:], [[1, SLOT_TILES]], base=0, channel_multiplier=0, allow_small_or_imprecise_dtypes=True)\
                .then_inc(made, 1)
            pool.wait_ge(made, 4)
            pool.affine_select(out=before_f[:], in_=before_f[:], compare_op=ALU.is_gt, fill=0.0, base=0,
                               pattern=[[1, P]], channel_multiplier=-1).then_inc(made, 1)

        @block.scalar
        def _(act):
            act.wait_ge(made, 5)
            act.activation(before[:], before_f[:], ACT.Copy).then_inc(cast, 1)
            act.activation(ones[:], all_f[:], ACT.Copy).then_inc(cast, 1)
            act.wait_ge(shifted, 1)
            act.activation(flat(work[1]), flat(work[0]), ACT.Exp).then_inc(exp_done, 1)

        @block.tensor
        def _(pe):
            pe.wait_ge(cast, 2)
            pe.wait_ge(chosen_ok, 1)
            n = TILES * EXPERTS
            pe.matmul(ps_rank[:, 0:n], before[:], flat(chosen), start=True, stop=True)
            pe.matmul(ps_total[:, 0:n], ones[:], flat(chosen), start=True, stop=True).then_inc(summed, 1)

        @block.vector
        def _(dve):
            steps = [0]

            def link(ins):
                steps[0] += 1
                ins.then_inc(own, 1)
                dve.wait_ge(own, steps[0])

            def wide(t):
                return t.unsqueeze(2).to_broadcast([P, TILES, EXPERTS])

            falling_w = falling[:].unsqueeze(1).to_broadcast([P, TILES, EXPERTS])
            dve.wait_ge(got, 16)
            dve.wait_ge(made, 5)
            link(dve.tensor_reduce(row[:], lg[:], AX.X, ALU.max))
            dve.tensor_tensor(work[0][:], lg[:], wide(row[:]), ALU.subtract).then_inc(shifted, 1)
            dve.wait_ge(exp_done, 1)
            link(dve.tensor_reduce(row[:], work[1][:], AX.X, ALU.add))
            link(dve.reciprocal(place[:], row[:]))
            link(dve.tensor_tensor(probs[:], work[1][:], wide(place[:]), ALU.mult))
            for k in range(TOP_K):
                weight = route.weight[k]
                link(dve.tensor_reduce(weight[:], probs[:], AX.X, ALU.max))
                link(dve.tensor_tensor(work[0][:], probs[:], wide(weight[:]), ALU.is_equal))
                link(dve.tensor_tensor(work[1][:], work[0][:], falling_w, ALU.mult))
                link(dve.tensor_reduce(row[:], work[1][:], AX.X, ALU.max))
                link(dve.tensor_tensor(masks[k][:], falling_w, wide(row[:]), ALU.is_equal))
                if k == 0:
                    link(dve.scalar_tensor_tensor(out=flat(probs), in0=flat(masks[0]), scalar=-2.0, in1=flat(probs),
                                                  op0=ALU.mult, op1=ALU.add))
            dve.tensor_tensor(chosen[:], masks[0][:], masks[1][:], ALU.add).then_inc(chosen_ok, 1)
            dve.wait_ge(summed, 1)
            n = TILES * EXPERTS
            link(dve.tensor_copy(flat(rank), ps_rank[:, 0:n]))
            link(dve.tensor_copy(flat(totals[0]), ps_total[:, 0:n]))
            link(dve.tensor_tensor(flat(rank), flat(rank), flat(totals[0]), ALU.subtract))
            src, dst, d = totals[0], totals[1], 1
            while d < TILES:
                link(dve.tensor_copy(dst[:, 0:d, :], src[:, 0:d, :]))
                link(dve.tensor_tensor(dst[:, d:, :], src[:, d:, :], src[:, 0:TILES - d, :], ALU.add))
                src, dst, d = dst, src, 2 * d
            link(dve.tensor_tensor(rank[:], rank[:], src[:], ALU.add))
            link(dve.tensor_scalar(counts_i[:], src[:, TILES - 1, :], float(P - 1), None, ALU.add))
            link(dve.tensor_scalar(tiles_i[:], counts_i[:], P.bit_length() - 1, None, ALU.arith_shift_right))
            link(dve.tensor_copy(tiles_f[:], tiles_i[:]))
            link(dve.tensor_copy(ends[0][:], tiles_f[:]))
            a, b, d = ends[0], ends[1], 1
            while d < EXPERTS:
                link(dve.tensor_copy(b[:, 0:d], a[:, 0:d]))
                link(dve.tensor_tensor(b[:, d:], a[:, d:], a[:, 0:EXPERTS - d], ALU.add))
                a, b, d = b, a, 2 * d
            link(dve.tensor_tensor(first[:], a[:], tiles_f[:], ALU.subtract))
            link(dve.tensor_scalar(first[:], first[:], float(P), None, ALU.mult))
            link(dve.tensor_tensor(rank[:], rank[:], first[:].unsqueeze(1).to_broadcast([P, TILES, EXPERTS]), ALU.add))
            for k in range(TOP_K):
                link(dve.tensor_tensor(work[0][:], masks[k][:], rank[:], ALU.mult))
                link(dve.tensor_reduce(place[:], work[0][:], AX.X, ALU.add))
                link(dve.tensor_copy(route.slot[k][:], place[:]))
            link(dve.tensor_tensor(passed[:], a[0:1, :].unsqueeze(1).to_broadcast([1, SLOT_TILES, EXPERTS]),
                                   tile_no[:].unsqueeze(2).to_broadcast([1, SLOT_TILES, EXPERTS]), ALU.is_le))
            link(dve.tensor_reduce(expert_f[:], passed[:], AX.X, ALU.add))
            link(dve.tensor_scalar(route.expert[:], expert_f[:], float(EXPERTS - 1), None, ALU.min))


def stage_scatter(nc, dram, route):
    with ExitStack() as ctx:
        rows = ctx.enter_context(nc.sbuf_tensor("rows_s", [P, TILES, D], F32))
        zeros = ctx.enter_context(nc.sbuf_tensor("zeros_s", [P, 8 * D], F32))
        got = ctx.enter_context(nc.semaphore("rows_s_got"))
        zero_ok = ctx.enter_context(nc.semaphore("zero_ok"))
        cleared = ctx.enter_context(nc.semaphore("cleared"))
        sent = ctx.enter_context(nc.semaphore("sent"))
        block = ctx.enter_context(nc.Block())

        @block.sync
        def _(sp):
            sp.dma_start(rows[:].rearrange("p (u t) n -> p u (t n)", u=TURNS), dram["xn1"].rearrange("u p n -> p u n"))\
                .then_inc(got, 16)
            sp.wait_ge(zero_ok, 1)
            for n in range(SLOT_TILES // 8):
                sp.dma_start(dram["xs"][n * 8 * P:(n + 1) * 8 * P, :].rearrange("(p t) n -> p (t n)", p=P), zeros[:])\
                    .then_inc(cleared, 16)

        @block.gpsimd
        def _(pool):
            pool.memset(zeros[:], 0.0).then_inc(zero_ok, 1)
            pool.wait_ge(got, 16)
            pool.wait_ge(cleared, 16 * (SLOT_TILES // 8))
            for t in range(TILES):
                for k in range(TOP_K):
                    pool.indirect_dma_start(dram["xs"], bass.IndirectOffsetOnAxis(ap=route.slot[k][:, t:t + 1], axis=0),
                                            rows[:, t, :], None).then_inc(sent, 16)
            pool.wait_ge(sent, 16 * TILES * TOP_K)


HALF = INTER // 2


def stage_experts(nc, dram, route):
    with ExitStack() as ctx:
        def sb(name, shape, dt=F32):
            return ctx.enter_context(nc.sbuf_tensor(name, shape, dt))

        def psum(name):
            return ctx.enter_context(nc.psum_tensor(name, [P, 512], F32))

        def sem(name):
            return ctx.enter_context(nc.semaphore(name))

        UP = DC * 2 * INTER
        DOWN = 2 * D
        PART = 2
        ident = sb("ident_e", [P, P])
        w_up = [sb(f"we_up{i}", [P, EXPERTS * UP], R32) for i in range(2)]
        w_down = [sb(f"we_down{i}", [HALF, EXPERTS * DOWN], R32) for i in range(2)]
        raw_up = sb("raw_up", [P, 2, PART, DC, 2, INTER])
        raw_down = sb("raw_down_e", [HALF, 2, PART * DOWN])
        xs = sb("xs_e", [P, 4, D])
        xT = [sb(f"xTe{i}", [P, 2, D], R32) for i in range(2)]
        tanh_g = sb("tanh_e", [P, 2, INTER])
        gated = sb("gated_e", [P, 2, INTER])
        h_f = sb("h_fe", [P, 2, INTER])
        hT = [sb(f"hTe{i}", [HALF, 2, 2 * P], R32) for i in range(2)]
        ys = sb("ys_e", [P, 2, D])
        ps_x = [psum(f"ps_x{i}") for i in range(2)]
        ps_u = [psum(f"ps_u{i}") for i in range(2)]
        ps_h = [psum(f"ps_h{i}") for i in range(2)]
        ps_d = [psum(f"ps_d{i}") for i in range(2)]

        id_ok = sem("ide_ok")
        raw_got = [sem(f"raw_got{i}") for i in range(2)]
        w_high = sem("w_high")
        w_low = sem("w_low")
        x_got = [Signal(sem(f"xs_got{i}"), 4) for i in range(4)]
        x_full = Signal(sem("xe_full"), 1, 4)
        x_high = Signal(sem("xe_high"), 1)
        x_low = Signal(sem("xe_low"), 1, 2)
        u_full = Signal(sem("ue_full"), 1)
        tanh_ok = Signal(sem("tanhe_ok"), 1)
        gate_ok = Signal(sem("gatee_ok"), 1)
        h_ok = Signal(sem("he_ok"), 1, 2)
        h_full = Signal(sem("he_full"), 1)
        h_high = Signal(sem("he_high"), 1)
        h_low = Signal(sem("he_low"), 1, 2)
        d_full = Signal(sem("de_full"), 1)
        y_ok = Signal(sem("ye_ok"), 1, 2)
        y_out = [Signal(sem(f"y_out{i}"), 8, 16) for i in range(2)]

        block = ctx.enter_context(nc.Block())

        def walk(step):
            return step

        def at(signal, base, i, n):
            return base * signal.per_turn + (signal.head + i * signal.per_turn + n)

        LAG = 3
        FILL = 4

        def steps(eng, step):
            for i in range(FILL):
                step(0, i, i)
            with eng.Fori(0, (SLOT_TILES - FILL) // 4) as j:
                for a in range(4):
                    step(j * 4, FILL + a, FILL)
            for i in range(LAG):
                step(SLOT_TILES, i, SLOT_TILES + i)

        @block.sync
        def _(sp):
            parts = EXPERTS // PART
            for n in range(parts):
                if n >= 2:
                    sp.wait_ge(w_low, 2 * (n - 1))
                e = n * PART
                for i, m in enumerate(("w1T", "w3T")):
                    for k in range(PART):
                        sp.dma_start(raw_up[:, n % 2, k, :, i, :], dram[m][e + k].rearrange("(c p) n -> p c n", p=P))\
                            .then_inc(raw_got[n % 2], 16)
                sp.dma_start(raw_down[:, n % 2, :].rearrange("p (a n) -> p a n", n=D),
                             dram["w2T"][e:e + PART].rearrange("e (c p) n -> p (e c) n", p=HALF)).then_inc(raw_got[n % 2], 16)
            with sp.Fori(0, SLOT_TILES // 4) as j:
                for a in range(4):
                    sp.wait_ge(x_full.sem, at(x_full, j * 4, a - 4, 1))
                    sp.dma_start(xs[:, a, :], dram["xs"].rearrange("(t p) n -> t p n", p=P)[ds(j * 4 + a, 1)]
                                 .rearrange("o p n -> (o p) n")).then_inc(x_got[a].sem, 16)

        @block.gpsimd
        def _(pool):
            pool.memset(ident[:], 0.0).then_inc(id_ok, 1)
            pool.wait_ge(id_ok, 1)
            pool.affine_select(out=ident[:], in_=ident[:], compare_op=ALU.not_equal, fill=1.0, base=0,
                               pattern=[[-1, P]], channel_multiplier=1).then_inc(id_ok, 1)

        def parts_of(n):
            e = n * PART
            return [(raw_up[:, n % 2].rearrange("p k c i n -> p (k c i n)"),
                     *[w[:, e * UP:(e + PART) * UP] for w in w_up]),
                    (raw_down[:, n % 2, :], *[w[:, e * DOWN:(e + PART) * DOWN] for w in w_down])]

        @block.scalar
        def _(act):
            for n in range(EXPERTS // PART):
                act.wait_ge(raw_got[n % 2], 16 * (2 * PART + 1) * (n // 2 + 1))
                for raw, high, _ in parts_of(n):
                    act.activation(high, raw, ACT.Copy).then_inc(w_high, 1)

            def step(base, i, kind):
                if kind < SLOT_TILES:
                    b = i % 2
                    act.wait_ge(x_full.sem, at(x_full, base, i, 1))
                    act.activation(xT[0][:, b, :], ps_x[b][:, 0:D], ACT.Copy).then_inc(x_high.sem, 1)
                if 1 <= kind < SLOT_TILES + 1:
                    b = (i - 1) % 2
                    act.wait_ge(u_full.sem, at(u_full, base, i - 1, 1))
                    act.activation(tanh_g[:, b, :], ps_u[b][:, 0:INTER], ACT.Tanh, scale=0.5).then_inc(tanh_ok.sem, 1)
                if 2 <= kind < SLOT_TILES + 2:
                    b = (i - 2) % 2
                    act.wait_ge(h_full.sem, at(h_full, base, i - 2, 1))
                    act.activation(hT[0][:, b, :], ps_h[b][0:HALF, 0:2 * P], ACT.Copy).then_inc(h_high.sem, 1)
                if 3 <= kind < SLOT_TILES + 3:
                    b = (i - 3) % 2
                    act.wait_ge(d_full.sem, at(d_full, base, i - 3, 1))
                    act.wait_ge(y_out[b].sem, base * 8 + 16 * ((i - 3) // 2 + 1))
                    act.activation(ys[:, b, :], ps_d[b][:, 0:D], ACT.Copy).then_inc(y_ok.sem, 1)
                    act.wait_ge(y_ok.sem, at(y_ok, base, i - 3, 1))
                    tiles = dram["ys"].rearrange("(t p) n -> t p n", p=P)
                    act.dma_start(tiles[ds(base + (i - 3), 1)].rearrange("o p n -> (o p) n"), ys[:, b, :])\
                        .then_inc(y_out[b].sem, 16)

            act.sem_inc(y_ok.sem, 2)
            for b in range(2):
                act.sem_inc(y_out[b].sem, 16)
            steps(act, step)
            for b in range(2):
                act.wait_ge(y_out[b].sem, 16 + 8 * SLOT_TILES)

        @block.vector
        def _(dve):
            for n in range(EXPERTS // PART):
                for m, (raw, high, low) in enumerate(parts_of(n)):
                    dve.wait_ge(w_high, 2 * n + m + 1)
                    dve.tensor_tensor(low, raw, high.bitcast(F32), ALU.subtract).then_inc(w_low, 1)
            dve.sem_inc(x_low.sem, 2)
            dve.sem_inc(h_ok.sem, 2)
            dve.sem_inc(h_low.sem, 2)

            def step(base, i, kind):
                if kind < SLOT_TILES:
                    b = i % 2
                    dve.wait_ge(x_high.sem, at(x_high, base, i, 1))
                    dve.tensor_tensor(xT[1][:, b, :], ps_x[b][:, 0:D], xT[0][:, b, :].bitcast(F32), ALU.subtract).then_inc(x_low.sem, 1)
                if 1 <= kind < SLOT_TILES + 1:
                    b = (i - 1) % 2
                    dve.wait_ge(tanh_ok.sem, at(tanh_ok, base, i - 1, 1))
                    dve.scalar_tensor_tensor(out=gated[:, b, :], in0=tanh_g[:, b, :], scalar=1.0, in1=ps_u[b][:, 0:INTER],
                                             op0=ALU.add, op1=ALU.mult).then_inc(gate_ok.sem, 1)
                    dve.wait_ge(gate_ok.sem, at(gate_ok, base, i - 1, 1))
                    dve.scalar_tensor_tensor(out=h_f[:, b, :], in0=ps_u[b][:, INTER:2 * INTER], scalar=0.5, in1=gated[:, b, :],
                                             op0=ALU.mult, op1=ALU.mult).then_inc(h_ok.sem, 1)
                if 2 <= kind < SLOT_TILES + 2:
                    b = (i - 2) % 2
                    dve.wait_ge(h_high.sem, at(h_high, base, i - 2, 1))
                    dve.tensor_tensor(hT[1][:, b, :], ps_h[b][0:HALF, 0:2 * P], hT[0][:, b, :].bitcast(F32), ALU.subtract)\
                        .then_inc(h_low.sem, 1)

            steps(dve, step)

        @block.tensor
        def _(pe):
            pe.wait_ge(id_ok, 2)
            pe.wait_ge(w_low, 2 * (EXPERTS // PART))
            pe.sem_inc(x_full.sem, 4)

            def expert(base, i):
                return pe.value_load(route.expert[0:1, ds(base + i, 1)], min_val=0, max_val=EXPERTS - 1)

            def step(base, i, kind):
                if 1 <= kind < SLOT_TILES + 1:
                    e_up = expert(base, i - 1)
                if 3 <= kind < SLOT_TILES + 3:
                    e_down = expert(base, i - 3)
                if kind < SLOT_TILES:
                    b = i % 2
                    pe.wait_ge(x_got[i % 4].sem, base * 4 + 16 * (i // 4 + 1))
                    pe.wait_ge(x_low.sem, at(x_low, base, i - 2, 1))
                    for c in range(DC):
                        last = pe.transpose(ps_x[b][:, c * P:(c + 1) * P], xs[:, i % 4, c * P:(c + 1) * P], ident[:])
                    last.then_inc(x_full.sem, 1)
                if 1 <= kind < SLOT_TILES + 1:
                    b = (i - 1) % 2
                    pe.wait_ge(x_low.sem, at(x_low, base, i - 1, 1))
                    pe.wait_ge(h_ok.sem, at(h_ok, base, i - 3, 1))
                    for c in range(DC):
                        for n, (x, w) in enumerate(((0, 0), (0, 1), (1, 0))):
                            last = pe.matmul(ps_u[b][:, 0:2 * INTER], xT[x][:, b, c * P:(c + 1) * P],
                                             w_up[w][:, ds(e_up * UP + c * 2 * INTER, 2 * INTER)],
                                             start=(c == 0 and n == 0), stop=(c == DC - 1 and n == 2), skip_group_check=True)
                    last.then_inc(u_full.sem, 1)
                if 2 <= kind < SLOT_TILES + 2:
                    b = (i - 2) % 2
                    pe.wait_ge(h_ok.sem, at(h_ok, base, i - 2, 1))
                    pe.wait_ge(h_low.sem, at(h_low, base, i - 4, 1))
                    for c in range(2):
                        last = pe.transpose(ps_h[b][0:HALF, c * P:(c + 1) * P], h_f[:, b, c * HALF:(c + 1) * HALF], ident[:])
                    last.then_inc(h_full.sem, 1)
                if 3 <= kind < SLOT_TILES + 3:
                    b = (i - 3) % 2
                    pe.wait_ge(h_low.sem, at(h_low, base, i - 3, 1))
                    pe.wait_ge(y_ok.sem, at(y_ok, base, i - 5, 1))
                    for c in range(2):
                        for n, (x, w) in enumerate(((0, 0), (0, 1), (1, 0))):
                            last = pe.matmul(ps_d[b][:, 0:D], hT[x][:, b, c * P:(c + 1) * P],
                                             w_down[w][:, ds(e_down * DOWN + c * D, D)],
                                             start=(c == 0 and n == 0), stop=(c == 1 and n == 2), skip_group_check=True)
                    last.then_inc(d_full.sem, 1)

            steps(pe, step)


class Route:

    def __init__(self, nc, ctx):
        def sb(name, shape, dt):
            return ctx.enter_context(nc.sbuf_tensor(name, shape, dt))

        self.slot = [sb(f"slot{k}", [P, TILES], I32) for k in range(TOP_K)]
        self.weight = [sb(f"weight{k}", [P, TILES], F32) for k in range(TOP_K)]
        self.expert = sb("expert", [1, SLOT_TILES], I32)


def program(nc, dram):
    for name, shape, dt in (
        ("q_scr", [2, D, PAIR], F32),
        ("xn1", [TURNS, P, TP * D], F32),
        ("xn1T", [2 * TURNS, P, DC * PAIR], F32),
        ("x1", [TURNS, P, TP * D], F32),
        ("w_head", [HEADS1, P, W_HEAD], F32),
        ("xs", [SLOTS, D], F32),
        ("ys", [SLOTS, D], F32),
        ("logits", [TURNS, P, TP * EXPERTS], F32),
    ):
        dram[name] = nc.dram_tensor("d_" + name, shape, dt, kind="Internal").ap()
    with ExitStack() as ctx:
        route = Route(nc, ctx)
        stage_layer0(nc, dram)
        stage_routing(nc, dram, route)
        stage_scatter(nc, dram, route)
        stage_experts(nc, dram, route)
        kept = AttentionWeights(nc, ctx)
        stage_attention_weights(nc, dram, kept)
        stage_attention(nc, dram, route, kept)


_OUTS = [((8, 256, 256), "float32")]


def kernel(**inputs):
    import numpy as _np
    import concourse.bacc as _bacc
    from concourse import mybir as _mybir
    from concourse.bass_utils import run_bass_kernel_spmd as _run

    g = lambda name: _np.asarray(inputs[name])
    laid = {
        "x": g("L0_attn_x").reshape(TOKENS, D),
        "WqkvT": g("L0_attn_Wqkv_w").T, "Wqkv_b": g("L0_attn_Wqkv_b"),
        "out_wT": g("L0_attn_out_w").T, "out_b": g("L0_attn_out_b"),
        "wgateT": g("L0_ffn_wq_gate").T, "s_gate": g("L0_ffn_s_gate"),
        "wupT": g("L0_ffn_wq_up").T, "s_up": g("L0_ffn_s_up"),
        "wdownT": g("L0_ffn_wq_down").T, "s_down": g("L0_ffn_s_down"),
        "wq_codes": g("L1_attn_wq_codes"), "wq_scales": g("L1_attn_wq_scales"), "bq": g("L1_attn_bq"),
        "wk_codes": g("L1_attn_wk_codes"), "wk_scales": g("L1_attn_wk_scales"), "bk": g("L1_attn_bk"),
        "wv_codes": g("L1_attn_wv_codes"), "wv_scales": g("L1_attn_wv_scales"), "bv": g("L1_attn_bv"),
        "wo_codes": g("L1_attn_wo_codes"), "wo_scales": g("L1_attn_wo_scales"), "bo": g("L1_attn_bo"),
        "w1T": g("L1_ffn_w1").transpose(0, 2, 1), "w3T": g("L1_ffn_w3").transpose(0, 2, 1), "w2T": g("L1_ffn_w2").transpose(0, 2, 1),
        "gate_wT": g("L1_ffn_gate_w").T,
        "sw1T": g("L1_ffn_sw1").T, "sw2T": g("L1_ffn_sw2").T, "sw3T": g("L1_ffn_sw3").T,
    }
    nc = _bacc.Bacc("TRN2", target_bir_lowering=False, num_devices=1)
    arrays, dram = {}, {}
    for name, a in laid.items():
        a = _np.ascontiguousarray(a)
        arrays[f"in_{name}"] = a
        dram[name] = nc.dram_tensor(f"in_{name}", a.shape, _mybir.dt.from_np(a.dtype), kind="ExternalInput").ap()
    shape, dtype = _OUTS[0]
    out = nc.dram_tensor("out_0", shape, _mybir.dt.from_np(_np.dtype(dtype)), kind="ExternalOutput").ap()
    dram["out"] = out.rearrange("b s d -> (b s) d")
    program(nc, dram)
    r = _run(nc, [arrays], core_ids=[0])
    return r.results[0]["out_0"]
```

```python
from contextlib import ExitStack

import concourse.bass as bass
from concourse import mybir

F32 = mybir.dt.float32
R32 = mybir.dt.float32r
I32 = mybir.dt.int32
U32 = mybir.dt.uint32
ALU = mybir.AluOpType
ACT = mybir.ActivationFunctionType
AX = mybir.AxisListType
ds = bass.ds

P = 128
SEQS, SEQ, D = 8, 256, 256
TOKENS = SEQS * SEQ
DC = D // P
PAIR = 2 * SEQ
TURNS = TOKENS // PAIR
TP = PAIR // P
EPS = 1e-5
HEADS0, HD0 = 16, 16
QKV0 = D + 2 * HD0
HID = 704
ZERO_POINT = 128.0
HT = [min(m, HID - P) for m in range(0, HID, P)]
HEADS1, HD1 = 16, 128
FEAT = HEADS1 * HD1
BLOCK = 32
EXPERTS, INTER, SHARED = 16, 176, 352
ST = [min(m, SHARED - P) for m in range(0, SHARED, P)]
REP = P // HD0
TILES = TOKENS // P
MASKED = -1.0e30


class Signal:

    def __init__(self, sem, per_turn=0, head=0):
        self.sem, self.per_turn, self.head = sem, per_turn, head

    def at(self, turn, n):
        return turn * self.per_turn + (self.head + n)


def stage_layer0(nc, dram):
    QW = D + P + HD0
    DUP_H, DUP_S = 5 * P - HT[5], 2 * P - ST[2]
    with ExitStack() as ctx:
        def sb(name, shape, dt=F32):
            return ctx.enter_context(nc.sbuf_tensor(name, shape, dt))

        def psum(name):
            return ctx.enter_context(nc.psum_tensor(name, [P, 512], F32))

        def sem(name):
            return ctx.enter_context(nc.semaphore(name))

        ident = sb("ident", [P, P])
        ident_r = sb("ident_r", [P, P], R32)
        mask_r = sb("mask_r", [P, P], R32)
        ones_r = sb("ones_r", [1, P], R32)
        w_qkv = [sb(f"w_qkv{i}", [P, DC, D + P], R32) for i in range(2)]
        w_o = [sb(f"w_o{i}", [P, DC, D], R32) for i in range(2)]
        ob = [sb(f"ob{i}", [1, D], R32) for i in range(2)]
        w_gate = sb("w_gate", [P, DC, HID], R32)
        w_up = sb("w_up", [P, DC, HID], R32)
        w_down = sb("w_down", [P, len(HT), D], R32)
        w_s13 = [sb(f"w_s13{i}", [P, DC, 2 * SHARED], R32) for i in range(2)]
        w_s2 = [sb(f"w_s2{i}", [P, len(ST), D], R32) for i in range(2)]
        w_gate1 = sb("w_gate1", [P, DC, P], R32)
        w_v = sb("w_v_l0", [P, DC, 2, HD0], R32)
        bq = sb("bq", [P, DC])
        bk = sb("bk", [48, 1])
        bv = sb("bv", [P, 2, HD0])
        s_gate = sb("s_gate", [P, len(HT)])
        s_up = sb("s_up", [P, len(HT)])
        half_gate = sb("half_gate", [P, len(HT)])
        scale_h = sb("scale_h", [P, len(HT)])
        s_down = sb("s_down", [P, D])
        x_in = sb("x_in", [P, TP, D])
        x_got = Signal(sem("x_got"), 32)
        with ExitStack() as staging:
            def stage(name, shape, dt=F32):
                return staging.enter_context(nc.sbuf_tensor(name, shape, dt))

            def stage_sem(name):
                return staging.enter_context(nc.semaphore(name))

            mask_f = stage("mask_f", [P, P])
            ones_f = stage("ones_f", [1, P])
            raw_qkv = stage("raw_qkv", [P, DC, QW])
            raw_o = stage("raw_o", [P, DC, D])
            raw_ob = stage("raw_ob", [1, D])
            raw_int = stage("raw_int", [P, DC, HID], I32)
            raw_down = stage("raw_down", [P, len(HT), D], I32)
            raw_s13 = raw_int[:].bitcast(F32)
            raw_s2 = stage("raw_s2", [P, len(ST), D])
            raw_gw = stage("raw_gw", [P, DC, EXPERTS])
            block_scales = stage("block_scales", [4 * D // BLOCK, FEAT])
            scales_in = stage_sem("scales_in")
            scaled = stage_sem("scaled")
            scales_out = stage_sem("scales_out")
            raw_in = stage_sem("raw_in")
            gate_zero = stage_sem("gate_zero")
            columns_in = stage_sem("columns_in")
            const_ok = stage_sem("const_ok")
            prep_act = stage_sem("prep_act")
            prep_dve = stage_sem("prep_dve")
            block = staging.enter_context(nc.Block())

            loads = [
                (raw_qkv[:, :, 0:D], dram["WqkvT"][:, 0:D].rearrange("(c p) n -> p c n", p=P)),
                *[(raw_qkv[:, c, D:D + P].rearrange("p (r n) -> p r n", r=REP),
                   dram["WqkvT"][c * P:(c + 1) * P, D:D + HD0].unsqueeze(1).to_broadcast([P, REP, HD0])) for c in range(DC)],
                (raw_qkv[:, :, D + P:], dram["WqkvT"][:, D + HD0:].rearrange("(c p) n -> p c n", p=P)),
                (raw_o[:], dram["out_wT"].rearrange("(c p) n -> p c n", p=P)),
                (raw_ob[:], dram["out_b"].rearrange("(a n) -> a n", a=1)),
                *[(bv[:, i, :], dram["Wqkv_b"][D + HD0:].rearrange("(a n) -> a n", a=1).partition_broadcast(P)) for i in range(2)],
                (s_down[:], dram["s_down"].rearrange("(a n) -> a n", a=1).partition_broadcast(P)),
                (raw_down[:, 0:5, :], dram["wdownT"][0:5 * P, :].rearrange("(m p) n -> p m n", p=P)),
                (raw_down[DUP_H:, 5, :], dram["wdownT"][5 * P:, :]),
                (raw_s2[:, 0:2, :], dram["sw2T"][0:2 * P, :].rearrange("(m p) n -> p m n", p=P)),
                (raw_s2[DUP_S:, 2, :], dram["sw2T"][2 * P:, :]),
                (raw_gw[:], dram["gate_wT"].rearrange("(c p) n -> p c n", p=P)),
                (raw_int[:], dram["wgateT"].rearrange("(c p) n -> p c n", p=P)),
            ]
            FIRST = 16 * len(loads)
            column_loads = [
                *[(bq[:, c:c + 1], dram["Wqkv_b"][c * P:(c + 1) * P].rearrange("(p a) -> p a", a=1)) for c in range(DC)],
                *[(bk[HD0 * i:HD0 * (i + 1), :], dram["Wqkv_b"][D:D + HD0].rearrange("(p a) -> p a", a=1)) for i in range(3)],
                *[(t[:, m:m + 1], dram[n][at:at + P].rearrange("(p a) -> p a", a=1))
                  for t, n in ((s_gate, "s_gate"), (s_up, "s_up")) for m, at in enumerate(HT)],
            ]

            splits = [(raw_qkv[:, :, 0:D + P], w_qkv[0][:], w_qkv[1][:]), (raw_o[:], w_o[0][:], w_o[1][:]), (raw_ob[:], ob[0][:], ob[1][:]),
                      (raw_s2[:], w_s2[0][:], w_s2[1][:]),
                      (raw_gw[:], *[w_gate1[:, :, i * EXPERTS:(i + 1) * EXPERTS] for i in range(2)]),
                      (raw_qkv[:, :, D + P:], w_v[:, :, 0, :], w_v[:, :, 1, :]),
                      (raw_s13, w_s13[0][:], w_s13[1][:])]

            @block.sync
            def _(sp):
                sp.dma_start(block_scales[:], dram["w_scales"].rearrange("m a b n -> (m a b) n")).then_inc(scales_in, 16)
                for dst, src in loads:
                    sp.dma_start(dst, src).then_inc(raw_in, 16)
                for half in range(2):
                    a = half * TP // 2
                    sp.dma_start(x_in[:, a:a + TP // 2, :], dram["x"][a * P:(a + TP // 2) * P, :].rearrange("(t p) n -> p t n", p=P))\
                        .then_inc(x_got.sem, 16)
                sp.wait_ge(scaled, 1)
                sp.dma_start(dram["scales"].rearrange("m a b n -> (m a b) n"), block_scales[:]).then_inc(scales_out, 16)
                sp.wait_ge(prep_dve, 1)
                sp.dma_start(raw_int[:], dram["wupT"].rearrange("(c p) n -> p c n", p=P)).then_inc(raw_in, 16)
                sp.wait_ge(prep_dve, 2)
                for i, n in enumerate(("sw1T", "sw3T")):
                    sp.dma_start(raw_s13[:, :, SHARED * i:SHARED * (i + 1)],
                                 dram[n].rearrange("(c p) n -> p c n", p=P)).then_inc(raw_in, 16)
                sp.wait_ge(scales_out, 16)

            @block.gpsimd
            def _(pool):
                for dst, src in column_loads:
                    pool.dma_start(dst, src).then_inc(columns_in, 16)
                pool.memset(ident[:], 0.0).then_inc(const_ok, 1)
                pool.memset(mask_f[:], 0.0).then_inc(const_ok, 1)
                pool.memset(ones_f[:], 1.0).then_inc(const_ok, 1)
                pool.memset(w_gate1[:].bitcast(F32), 0.0).then_inc(gate_zero, 1)
                pool.wait_ge(const_ok, 3)
                pool.affine_select(out=ident[:], in_=ident[:], compare_op=ALU.not_equal, fill=1.0, base=0,
                                   pattern=[[-1, P]], channel_multiplier=1).then_inc(const_ok, 1)
                pool.memset(raw_down[0:DUP_H, 5, :], int(ZERO_POINT)).then_inc(const_ok, 1)
                pool.memset(raw_s2[0:DUP_S, 2, :], 0.0).then_inc(const_ok, 1)
                pool.affine_select(out=mask_f[:], in_=mask_f[:], compare_op=ALU.is_ge, fill=MASKED, base=0,
                                   pattern=[[-1, P]], channel_multiplier=1).then_inc(const_ok, 1)

            @block.scalar
            def _(act):
                act.wait_ge(const_ok, 7)
                act.activation(ident_r[:], ident[:], ACT.Copy).then_inc(prep_act, 1)
                act.activation(mask_r[:], mask_f[:], ACT.Copy).then_inc(prep_act, 1)
                act.activation(ones_r[:], ones_f[:], ACT.Copy).then_inc(prep_act, 1)
                act.wait_ge(gate_zero, 1)
                act.wait_ge(prep_dve, 3)
                for n, (raw, high, _) in enumerate(splits):
                    if n == len(splits) - 1:
                        act.wait_ge(raw_in, FIRST + 48)
                    act.activation(high, raw, ACT.Copy).then_inc(prep_act, 1)

            @block.vector
            def _(dve):
                dve.wait_ge(scales_in, 16)
                dve.tensor_scalar(block_scales[0:D // BLOCK, :], block_scales[0:D // BLOCK, :], HD1 ** -0.5, None, ALU.mult)\
                    .then_inc(scaled, 1)
                dve.wait_ge(raw_in, FIRST)
                dve.tensor_scalar(w_gate[:], raw_int[:], ZERO_POINT, None, ALU.subtract).then_inc(prep_dve, 1)
                dve.wait_ge(raw_in, FIRST + 16)
                dve.tensor_scalar(w_up[:], raw_int[:], ZERO_POINT, None, ALU.subtract).then_inc(prep_dve, 1)
                dve.tensor_scalar(raw_qkv[:, :, 0:D], raw_qkv[:, :, 0:D], HD0 ** -0.5, None, ALU.mult).then_inc(prep_dve, 1)
                dve.wait_ge(columns_in, 16 * len(column_loads))
                dve.tensor_scalar(bq[:], bq[:], HD0 ** -0.5, None, ALU.mult).then_inc(prep_dve, 1)
                dve.wait_ge(const_ok, 7)
                dve.tensor_scalar(w_down[:], raw_down[:], ZERO_POINT, None, ALU.subtract).then_inc(prep_dve, 1)
                dve.tensor_scalar(half_gate[:], s_gate[:], 0.5, None, ALU.mult).then_inc(prep_dve, 1)
                dve.wait_ge(prep_dve, 6)
                dve.tensor_tensor(scale_h[:], half_gate[:], s_up[:], ALU.mult).then_inc(prep_dve, 1)
                for n, (raw, high, low) in enumerate(splits):
                    dve.wait_ge(prep_act, 4 + n)
                    dve.tensor_tensor(low, raw, high.bitcast(F32), ALU.subtract).then_inc(prep_dve, 1)

        zeros = sb("zeros", [P, D])
        PC = 256
        CHUNKS = DC * FEAT // PC
        codes = sb("codes", [P, 2, PC])
        scales = sb("scales", [P, 2, PC])
        parts = [sb(f"parts{i}", [P, 2, PC], R32) for i in range(2)]
        stats = sb("stats", [P, 2 * TP, 6])
        mv = sb("mv", [P, 2 * TP, 2])
        var_eps = sb("var_eps", [P, 2 * TP])
        rstd = sb("rstd", [P, 2 * TP])
        minus_half = sb("minus_half", [P, 2 * TP])
        xn = xn1 = sb("xn", [P, TP, D])
        xnT = [sb(f"xnT{i}", [P, DC, PAIR], R32) for i in range(2)]
        qT = [sb(f"qT{i}", [P, DC, PAIR], R32) for i in range(2)]
        q3 = sb("q3", [48, HEADS0, PAIR], R32)
        k3 = sb("k3", [48, 2, SEQ], R32)
        vf = sb("vf", [P, 2, 2, HD0])
        vs = sb("vs", [P, TP, 2, HD0], R32)
        neg_max = sb("neg_max", [P, 2, 4])
        sums = sb("sums", [P, TP, HEADS0])
        probs = sb("probs", [P, 3, 512])
        pT = [sb(f"pT{i}", [P, 2, 512], R32) for i in range(2)]
        ctx_f = sb("ctx_f", [P, HEADS0, HD0])
        rinv = sb("rinv", [P, HEADS0])
        ctx_n = sb("ctx_n", [P, D])
        cT = [sb(f"cT{i}", [P, TP, DC, P], R32) for i in range(2)]
        tanh_g = sb("tanh_g", [P, 2, PAIR])
        gated = sb("gated", [P, 2, PAIR])
        h_f = sb("h_f", [P, 2, PAIR])
        hT = [sb(f"hT{i}", [P, len(HT), PAIR], R32) for i in range(2)]
        sT = [sb(f"sT{i}", [P, len(ST), PAIR], R32) for i in range(2)]
        down_f = sb("down_f", [P, D])
        both_f = sb("both_f", [P, D])
        x1 = sb("x1", [P, TP, D])
        xn1T = [sb(f"xn1T{i}", [P, DC, PAIR], R32) for i in range(2)]
        lgT = sb("lgT", [2 * EXPERTS, PAIR])

        ps_m = [psum(f"ps_m{i}") for i in range(3)]
        ps_s = [psum(f"ps_s{i}") for i in range(2)]
        ps_t = psum("ps_t")
        ps_c = psum("ps_c")
        ps_b = psum("ps_b0")

        units = []
        for s in range(2):
            units += [(s, 0, h, 4) for h in range(0, HEADS0, 4)]
            units += [(s, 1, h, 2) for h in range(0, HEADS0, 2)]
        NU = len(units)
        last_unit = {(s, t): max(n for n, u in enumerate(units) if u[:2] == (s, t)) for s, t, _, _ in units}
        steps = [[] for _ in range(NU + 4)]
        EARLY = 8
        for n in range(EARLY, 2 * len(HT)):
            steps[n - EARLY].append(("ffn", n))
        for (s, t), n in last_unit.items():
            steps[n + 4].append(("ctx", 2 * s + t))
        for n, at in enumerate((17, 18, 20, NU + 3)):
            steps[at].append(("out", n))
        for n, at in enumerate((20, 21, 23, NU + 3)):
            steps[at].append(("norm", n))
        front = [("xT", 0), ("xT", 1), ("q", 0), ("q", 1), ("kv", 0), ("kv", 1)] + [("ffn", n) for n in range(EARLY)]
        order = front + [i for step in steps for i in step]
        back = [("ffs", n) for n in range(2 * len(ST))] + [("logit", 0)] + [("sum", n) for n in range(TP)]
        back_at = dict(zip(range(4, 15), range(len(back))))
        STORE_AT = 15
        NI = len(order)
        assert NI % len(ps_m) == 0 and NU % 2 == 0
        number = {item: n for n, item in enumerate(order)}
        acted = [i for i in order if i[0] in ("xT", "q", "kv", "ctx", "norm") or (i[0] == "ffn" and i[1] % 2 == 0)]
        act_number = {item: n for n, item in enumerate(acted)}
        LINKS = 6 + 6 * TP

        def bank(item):
            return ps_m[number[item] % len(ps_m)]

        own = Signal(sem("dve_own"), 0)
        var_ok = Signal(sem("var_ok"), 1 + TP)
        half_ok = sem("half_ok")
        zero_ok = sem("zero_ok")
        cleared = sem("cleared")
        rstd_ok = Signal(sem("rstd_ok"), 1 + TP)
        ln_done = Signal(sem("ln_done"), TP)
        item_full = Signal(sem("item_full"), NI)
        item_act = Signal(sem("item_act"), len(acted))
        item_done = Signal(sem("item_done"), NI, len(ps_m))
        q_out = Signal(sem("q_out"), 32 * DC)
        q3_got = Signal(sem("q3_got"), 48)
        s_full = Signal(sem("s_full"), NU)
        max_ok = Signal(sem("max_ok"), NU)
        p_ok = Signal(sem("p_ok"), NU, 2)
        t_full = Signal(sem("t_full"), NU)
        t_high = Signal(sem("t_high"), NU)
        t_low = Signal(sem("t_low"), NU, 1)
        pv_ok = Signal(sem("pv_ok"), NU, 2)
        ctx_free = Signal(sem("ctx_free"), TP, 1)
        ctx_ok = Signal(sem("ctx_ok"), TP)
        norm1_ok = Signal(sem("norm1_ok"), TP)
        h_high = Signal(sem("h_high"), len(HT))
        h_low = Signal(sem("h_low"), len(HT))
        b_full = Signal(sem("back_full"), len(back))
        b_act = Signal(sem("back_act"), len(ST))
        b_done = Signal(sem("back_done"), len(back), 1)
        hs_high = Signal(sem("hs_high"), len(ST))
        hs_low = Signal(sem("hs_low"), len(ST), 2 * len(ST))
        xn1_out = Signal(sem("xn1_out"), 16, 1)
        x1_ok = Signal(sem("x1_ok"), TP)
        xT_out = Signal(sem("xT_out"), 32, 1)
        x1_out = Signal(sem("x1_out"), 32, 1)

        def overlapped(eng, body):
            body(0, None)
            with eng.Fori(0, TURNS - 1) as u:
                body(u + 1, u)
            body(None, TURNS - 1)

        w_in = [Signal(sem(f"w_in{i}"), 16 * 5 * CHUNKS // 2) for i in range(2)]
        w_own = Signal(sem("w_own"), 2 * CHUNKS)
        w_done = Signal(sem("w_done"), CHUNKS)
        w_out = [Signal(sem(f"w_out{i}"), 16 * CHUNKS, 32) for i in range(2)]

        block = ctx.enter_context(nc.Block())

        @block.sync
        def _(sp):
            def load_chunk(m, n):
                half, at = n // (CHUNKS // 2), n % (CHUNKS // 2) * PC
                sp.dma_start(codes[:, n % 2, :], dram["w_codes"][ds(m, 1), half, :, at:at + PC].rearrange("o p n -> (o p) n"))\
                    .then_inc(w_in[n % 2].sem, 16)
                for b in range(P // BLOCK):
                    sp.dma_start(scales[b * BLOCK:(b + 1) * BLOCK, n % 2, :],
                                 dram["scales"][ds(m, 1), half, b, at:at + PC].partition_broadcast(BLOCK).rearrange("q o n -> q (o n)"))\
                        .then_inc(w_in[n % 2].sem, 16)

            sp.sem_inc(xT_out.sem, 1)
            sp.sem_inc(xn1_out.sem, 1)
            for i in range(2):
                sp.sem_inc(w_out[i].sem, 32)
            sp.wait_ge(zero_ok, 1)
            for n in range(2):
                load_chunk(0, n)
            with sp.Fori(0, TURNS) as p:
                for c in range(DC):
                    sp.wait_ge(item_done.sem, item_done.at(p, number["q", c] + 1))
                    for i in range(2):
                        sp.dma_start(dram["q_scr"][i, c * P:(c + 1) * P, :], qT[i][:, c, :].bitcast(F32)).then_inc(q_out.sem, 16)
                sp.wait_ge(q_out.sem, q_out.at(p, 32 * DC))
                sp.wait_ge(p_ok.sem, p_ok.at(p, 0))
                for r, i in enumerate((0, 1, 0)):
                    sp.dma_start(q3[HD0 * r:HD0 * (r + 1), :, :].bitcast(F32),
                                 dram["q_scr"][i].rearrange("(h d) t -> d h t", d=HD0)).then_inc(q3_got.sem, 16)
                for n in range(CHUNKS):
                    if n % 4 == 0:
                        sp.dma_start(dram["xs"].rearrange("(u t p) n -> u p t n", u=4 * TURNS, p=P)[ds(4 * p + n // 4, 1)]
                                     .rearrange("o p t n -> (o p) t n"),
                                     zeros[:].unsqueeze(1).to_broadcast([P, SLOT_TILES // (4 * TURNS), D])).then_inc(cleared, 16)
                    sp.wait_ge(w_done.sem, w_done.at(p, n + 1))
                    half, h = n // (CHUNKS // 2), n % (CHUNKS // 2) * (PC // HD1)
                    for i in range(2):
                        sp.dma_start(dram["w_head"][ds(p, 1), h:h + PC // HD1, :, i * D + half * HD1:i * D + (half + 1) * HD1]
                                     .rearrange("o h p n -> p (o h) n"),
                                     parts[i][:, n % 2, :].bitcast(F32).rearrange("p (h n) -> p h n", n=HD1)).then_inc(w_out[n % 2].sem, 16)
                    load_chunk((p + (n + 2) // CHUNKS) % TURNS, (n + 2) % CHUNKS)
                x_next = dram["x"].rearrange("(u t p) n -> u p t n", t=TP, p=P)[ds((p + 1) % TURNS, 1)].rearrange("o p t n -> (o p) t n")
                for a, b in ((0, TP - 1), (TP - 1, TP)):
                    sp.wait_ge(x1_ok.sem, x1_ok.at(p, b))
                    sp.dma_start(x_in[:, a:b, :], x_next[:, a:b, :]).then_inc(x_got.sem, 16)
                sp.wait_ge(item_done.sem, item_done.at(p, number["norm", TP - 1] + 1))
                sp.dma_start(dram["xn1"][ds(p, 1)].rearrange("o p n -> (o p) n"),
                             xn1[:].rearrange("p t n -> p (t n)")).then_inc(xn1_out.sem, 16)
                for i in range(2):
                    sp.dma_start(dram["xn1T"][ds(2 * p + i, 1)].rearrange("o p n -> (o p) n"),
                                 xn1T[i][:].bitcast(F32).rearrange("p c n -> p (c n)")).then_inc(xT_out.sem, 16)
            sp.wait_ge(xT_out.sem, xT_out.at(TURNS, 0))
            sp.wait_ge(xn1_out.sem, xn1_out.at(TURNS, 0))
            sp.wait_ge(x_got.sem, 32 * (TURNS + 1))
            sp.wait_ge(cleared, 64 * TURNS)
            for i in range(2):
                sp.wait_ge(w_out[i].sem, w_out[i].at(TURNS, 0))
                sp.wait_ge(w_in[i].sem, w_in[i].at(TURNS, 80))

        @block.gpsimd
        def _(pool):
            pool.memset(zeros[:], 0.0).then_inc(zero_ok, 1)
            pool.memset(minus_half[:], -0.5).then_inc(half_ok, 1)
            pool.wait_ge(half_ok, 1)

            def inverse_root(p, n, k):
                pool.wait_ge(var_ok.sem, var_ok.at(p, n + 1))
                at = 0 if n == 0 else TP - 1 + n
                pool.tensor_tensor(rstd[:, at:at + k], var_eps[:, at:at + k], minus_half[:, at:at + k], ALU.pow).then_inc(rstd_ok.sem, 1)

            def split(p, n):
                b = n % 2
                pool.wait_ge(w_in[b].sem, w_in[b].at(p, 80 * (n // 2 + 1)))
                pool.wait_ge(w_out[b].sem, w_out[b].at(p, 32 * (n // 2)))
                pool.tensor_tensor(parts[0][:, b, :], codes[:, b, :], scales[:, b, :], ALU.mult).then_inc(w_own.sem, 1)
                pool.wait_ge(w_own.sem, w_own.at(p, 2 * n + 1))
                pool.tensor_tensor(codes[:, b, :], codes[:, b, :], scales[:, b, :], ALU.mult).then_inc(w_own.sem, 1)
                pool.wait_ge(w_own.sem, w_own.at(p, 2 * n + 2))
                pool.tensor_tensor(parts[1][:, b, :], codes[:, b, :], parts[0][:, b, :].bitcast(F32), ALU.subtract).then_inc(w_done.sem, 1)

            with pool.Fori(0, TURNS) as p:
                for n in range(1 + TP):
                    if n == 0:
                        inverse_root(p, 0, TP)
                    else:
                        inverse_root(p, n, 1)
                    for i in range(CHUNKS if n == 0 else 0):
                        split(p, i)

        @block.scalar
        def _(act):
            act.sem_inc(p_ok.sem, 2)

            def exps(p, n):
                s, t, h0, nh = units[n]
                w = (t + 1) * P
                act.wait_ge(max_ok.sem, max_ok.at(p, n + 1))
                for h in range(nh):
                    last = act.activation(probs[:, n % 3, h * w:(h + 1) * w], ps_s[n % 2][:, h * w:(h + 1) * w], ACT.Exp,
                                          bias=neg_max[:, n % 2, h:h + 1], scale=1.0,
                                          accum_out=sums[:, 2 * s + t, h0 + h:h0 + h + 1])
                last.then_inc(p_ok.sem, 1)

            def high_probs(p, n):
                act.wait_ge(t_full.sem, t_full.at(p, n + 1))
                act.wait_ge(pv_ok.sem, pv_ok.at(p, n - 1))
                act.activation(pT[0][:, n % 2, :], ps_t[:], ACT.Copy).then_inc(t_high.sem, 1)

            def gate_tanh(full, acted, turn, number, bank, m, scale):
                act.wait_ge(full.sem, full.at(turn, number + 1))
                act.activation(tanh_g[:, m % 2, :], bank[:], ACT.Tanh, scale=scale).then_inc(acted.sem, 1)

            def high_hidden(done, high, turn, number, m, dst):
                act.wait_ge(done.sem, done.at(turn, number + 1))
                act.activation(dst[:, m, :], h_f[:, m % 2, :], ACT.Copy).then_inc(high.sem, 1)

            def high_of(p, item, dst, src, bias=None):
                act.wait_ge(item_full.sem, item_full.at(p, number[item] + 1))
                if bias is None:
                    act.activation(dst, src, ACT.Copy).then_inc(item_act.sem, 1)
                else:
                    act.activation(dst, src, ACT.Identity, bias=bias).then_inc(item_act.sem, 1)

            def shared(q, n):
                kind, i = back[n]
                if (kind == "ffs" and i % 2 == 0 and i) or n == 2 * len(ST):
                    high_hidden(b_done, hs_high, q, n - 1, (n - 2) // 2, sT[0])
                if kind == "ffs" and i % 2 == 0:
                    gate_tanh(b_full, b_act, q, n, ps_b, i // 2, 0.5)

            def store(q):
                act.wait_ge(b_done.sem, b_done.at(q, len(back)))
                act.dma_start(dram["x1"][ds(q, 1)].rearrange("o p n -> (o p) n"),
                              x1[:].rearrange("p t n -> p (t n)")).then_inc(x1_out.sem, 16)
                act.dma_start(dram["logits"][ds(q, 1)].rearrange("o p n -> (o p) n"),
                              lgT[:]).then_inc(x1_out.sem, 16)

            def ffn_parts(p, i):
                if i % 2 == 0:
                    if i >= 2:
                        high_hidden(item_done, h_high, p, number["ffn", i - 1], i // 2 - 1, hT[0])
                    if i < 2 * len(HT):
                        gate_tanh(item_full, item_act, p, number["ffn", i], bank(("ffn", i)), i // 2, half_gate[:, i // 2:i // 2 + 1])

            def body(p, q):
                if p is None:
                    for n in range(len(back)):
                        shared(q, n)
                    store(q)
                    return
                for c in range(DC):
                    high_of(p, ("xT", c), xnT[0][:, c, :], bank(("xT", c))[:])
                for c in range(DC):
                    high_of(p, ("q", c), qT[0][:, c, :], bank(("q", c))[:], bq[:, c:c + 1])
                for s in range(2):
                    high_of(p, ("kv", s), k3[:, s, :], bank(("kv", s))[0:48, 0:SEQ], bk[:])
                for i in range(EARLY):
                    ffn_parts(p, i)
                for n, step in enumerate(steps):
                    if 2 <= n <= NU + 1:
                        high_probs(p, n - 2)
                    if n < NU:
                        exps(p, n)
                    if n + EARLY <= 2 * len(HT):
                        ffn_parts(p, n + EARLY)
                    if q is not None and n in back_at:
                        shared(q, back_at[n])
                    if q is not None and n == STORE_AT:
                        store(q)
                    for kind, i in step:
                        if kind == "ctx":
                            high_of(p, (kind, i), cT[0][:, i, :, :].rearrange("p c n -> p (c n)"), bank((kind, i))[:, 0:D])
                        if kind == "norm":
                            if i == 0:
                                act.wait_ge(xT_out.sem, xT_out.at(p, 0))
                                if q is not None:
                                    act.wait_ge(b_done.sem, b_done.at(q, len(back)))
                            high_of(p, (kind, i), xn1T[0][:, :, i * P:(i + 1) * P],
                                    bank((kind, i))[:, 0:D].rearrange("p (c n) -> p c n", c=DC))

            act.sem_inc(x1_out.sem, 1)
            overlapped(act, body)
            act.wait_ge(x1_out.sem, x1_out.at(TURNS, 0))

        @block.vector
        def _(dve):
            dve.sem_inc(item_done.sem, len(ps_m))
            dve.sem_inc(t_low.sem, 1)
            dve.sem_inc(ctx_free.sem, 1)
            dve.sem_inc(b_done.sem, 1)
            dve.sem_inc(hs_low.sem, 2 * len(ST))

            per_turn = [0]

            def link(p, ins):
                per_turn[0] += 1
                ins.then_inc(own.sem, 1)
                dve.wait_ge(own.sem, own.at(p, per_turn[0]))

            def count(ins):
                per_turn[0] += 1
                ins.then_inc(own.sem, 1)

            def settle(p):
                dve.wait_ge(own.sem, own.at(p, per_turn[0]))

            def norm(p, n, xs, outs, done):
                k = len(xs)
                at = 0 if n == 0 else TP - 1 + n
                for t in range(k):
                    count(dve.bn_stats(stats[:, at + t, :], xs[t]))
                settle(p)
                dve.memset(var_eps[:, at:at + k], 0.0)
                for t in range(k):
                    count(dve.bn_aggr(mv[:, at + t, :], stats[:, at + t, :]))
                settle(p)
                dve.tensor_scalar(var_eps[:, at:at + k], mv[:, at:at + k, 1], EPS, None, ALU.add).then_inc(var_ok.sem, 1)
                dve.wait_ge(rstd_ok.sem, rstd_ok.at(p, n + 1))
                if n == 0:
                    dve.wait_ge(xn1_out.sem, xn1_out.at(p, 0))
                for t in range(k):
                    dve.tensor_scalar(outs[t], xs[t], mv[:, at + t, 0:1], rstd[:, at + t:at + t + 1], ALU.subtract, ALU.mult)\
                        .then_inc(done.sem, 1)

            def low_of(p, item, dst, src, high, bias=None):
                dve.wait_ge(item_act.sem, item_act.at(p, act_number[item] + 1))
                if bias is None:
                    dve.tensor_tensor(dst, src, high.bitcast(F32), ALU.subtract).then_inc(item_done.sem, 1)
                else:
                    dve.scalar_tensor_tensor(out=dst, in0=src, scalar=bias, in1=high.bitcast(F32), op0=ALU.add,
                                             op1=ALU.subtract).then_inc(item_done.sem, 1)

            def gate_tile(acted, done, turn, act_number, bank, m):
                dve.wait_ge(acted.sem, acted.at(turn, act_number + 1))
                dve.scalar_tensor_tensor(out=gated[:, m % 2, :], in0=tanh_g[:, m % 2, :], scalar=1.0, in1=bank[:],
                                         op0=ALU.add, op1=ALU.mult).then_inc(done.sem, 1)

            def up_tile(full, done, turn, number, bank, m, scale):
                dve.wait_ge(full.sem, full.at(turn, number + 1))
                dve.wait_ge(done.sem, done.at(turn, number))
                dve.scalar_tensor_tensor(out=h_f[:, m % 2, :], in0=bank[:], scalar=scale, in1=gated[:, m % 2, :],
                                         op0=ALU.mult, op1=ALU.mult).then_inc(done.sem, 1)

            def low_hidden(high, low, turn, m, dst):
                dve.wait_ge(high.sem, high.at(turn, m + 1))
                dve.tensor_tensor(dst[1][:, m, :], h_f[:, m % 2, :], dst[0][:, m, :].bitcast(F32), ALU.subtract).then_inc(low.sem, 1)

            def ffn_tile(p, i):
                m, item = i // 2, ("ffn", i)
                if i % 2 == 0 and m:
                    low_hidden(h_high, h_low, p, m - 1, hT)
                if m == len(HT):
                    return
                if i % 2 == 0:
                    gate_tile(item_act, item_done, p, act_number[item], bank(item), m)
                else:
                    if m >= 2:
                        dve.wait_ge(h_low.sem, h_low.at(p, m - 1))
                    else:
                        dve.wait_ge(hs_low.sem, hs_low.at(p, -len(ST)))
                    up_tile(item_full, item_done, p, number[item], bank(item), m, scale_h[:, m:m + 1])

            def shared(p, q, n):
                kind, i = back[n]
                if (kind == "ffs" and i % 2 == 0 and i) or n == 2 * len(ST):
                    low_hidden(hs_high, hs_low, q, (n - 2) // 2, sT)
                if kind == "ffs" and i % 2 == 0:
                    gate_tile(b_act, b_done, q, i // 2, ps_b, i // 2)
                if kind == "ffs" and i % 2 == 1:
                    if i // 2 < 2:
                        dve.wait_ge(h_low.sem, h_low.at(q if p is None else p, len(HT) - 1 + i // 2))
                    else:
                        dve.wait_ge(hs_low.sem, hs_low.at(q, i // 2 - 1))
                    up_tile(b_full, b_done, q, n, ps_b, i // 2, 0.5)
                if kind == "logit":
                    dve.wait_ge(b_full.sem, b_full.at(q, n + 1))
                    dve.tensor_copy(lgT[:], ps_b[0:2 * EXPERTS, :]).then_inc(b_done.sem, 1)
                if kind == "sum":
                    dve.wait_ge(b_full.sem, b_full.at(q, n + 1))
                    dve.tensor_tensor(x1[:, i, :], x1[:, i, :], ps_b[:, 0:D], ALU.add).then_inc(b_done.sem, 1)

            def context(p, s, t):
                n = last_unit[s, t]
                dve.wait_ge(pv_ok.sem, pv_ok.at(p, n + 1))
                dve.tensor_reduce(ctx_f[:], ps_c[:].rearrange("p (h i d) -> p h d i", i=2, d=HD0), AX.X, ALU.add)\
                    .then_inc(ctx_free.sem, 1)
                link(p, dve.reciprocal(rinv[:], sums[:, 2 * s + t, :]))
                dve.wait_ge(ctx_free.sem, ctx_free.at(p, 2 * s + t + 1))
                dve.tensor_tensor(ctx_n[:].rearrange("p (h d) -> p h d", h=HEADS0), ctx_f[:],
                                  rinv[:].unsqueeze(2).to_broadcast([P, HEADS0, HD0]), ALU.mult).then_inc(ctx_ok.sem, 1)

            def body(p, q):
                if p is None:
                    for n in range(len(back)):
                        shared(p, q, n)
                    return
                per_turn[0] = 0
                dve.wait_ge(x_got.sem, x_got.at(p, 32))
                norm(p, 0, [x_in[:, t, :] for t in range(TP)], [xn[:, t, :] for t in range(TP)], ln_done)
                for c in range(DC):
                    low_of(p, ("xT", c), xnT[1][:, c, :], bank(("xT", c))[:], xnT[0][:, c, :])
                for c in range(DC):
                    low_of(p, ("q", c), qT[1][:, c, :], bank(("q", c))[:], qT[0][:, c, :], bq[:, c:c + 1])
                for s in range(2):
                    out = bank(("kv", s))
                    dve.wait_ge(item_act.sem, item_act.at(p, act_number["kv", s] + 1))
                    dve.scalar_tensor_tensor(out=k3[32:48, s, :], in0=out[32:48, 0:SEQ], scalar=bk[32:48, :],
                                             in1=k3[32:48, s, :].bitcast(F32), op0=ALU.add, op1=ALU.subtract)
                    by_part = out[:, SEQ:SEQ + 4 * HD0].rearrange("p (t i d) -> p i t d", t=2, i=2)
                    link(p, dve.tensor_tensor(vf[:, s], by_part[:, 0], bv[:], ALU.add))
                    link(p, dve.tensor_tensor(vf[:, s], vf[:, s], by_part[:, 1], ALU.add))
                    link(p, dve.tensor_copy(vs[:, 2 * s:2 * s + 2, 0, :], vf[:, s]))
                    dve.tensor_tensor(vs[:, 2 * s:2 * s + 2, 1, :], vf[:, s], vs[:, 2 * s:2 * s + 2, 0, :].bitcast(F32), ALU.subtract)\
                        .then_inc(item_done.sem, 1)

                for i in range(EARLY):
                    ffn_tile(p, i)
                for n, step in enumerate(steps):
                    if n < NU:
                        s, t, h0, nh = units[n]
                        dve.wait_ge(s_full.sem, s_full.at(p, n + 1))
                        dve.tensor_reduce(neg_max[:, n % 2, 0:nh], ps_s[n % 2][:].rearrange("p (h k) -> p h k", h=nh), AX.X,
                                          ALU.max, negate=True).then_inc(max_ok.sem, 1)
                    if 2 <= n <= NU + 1:
                        dve.wait_ge(t_high.sem, t_high.at(p, n - 1))
                        dve.tensor_tensor(pT[1][:, n % 2, :], ps_t[:], pT[0][:, n % 2, :].bitcast(F32), ALU.subtract)\
                            .then_inc(t_low.sem, 1)
                    if n + EARLY <= 2 * len(HT):
                        ffn_tile(p, n + EARLY)
                    if q is not None and n in back_at:
                        shared(p, q, back_at[n])
                    if n >= 3:
                        for (s, t), last in last_unit.items():
                            if last == n - 3:
                                context(p, s, t)
                    for item in step:
                        kind, i = item
                        if kind == "ctx":
                            low_of(p, item, cT[1][:, i, :, :].rearrange("p c n -> p (c n)"), bank(item)[:, 0:D],
                                   cT[0][:, i, :, :].rearrange("p c n -> p (c n)"))
                        if kind == "out":
                            dve.wait_ge(item_full.sem, item_full.at(p, number[item] + 1))
                            link(p, dve.tensor_tensor(down_f[:], bank(item)[:, D:2 * D], s_down[:], ALU.mult))
                            dve.tensor_tensor(both_f[:], bank(item)[:, 0:D], down_f[:], ALU.add).then_inc(item_done.sem, 1)
                            dve.wait_ge(item_done.sem, item_done.at(p, number[item] + 1))
                            if i == 0:
                                dve.wait_ge(x1_out.sem, x1_out.at(p, 0))
                            dve.tensor_tensor(x1[:, i, :], x_in[:, i, :], both_f[:], ALU.add).then_inc(x1_ok.sem, 1)
                            dve.wait_ge(x1_ok.sem, x1_ok.at(p, i + 1))
                            norm(p, 1 + i, [x1[:, i, :]], [xn1[:, i, :]], norm1_ok)
                        if kind == "norm":
                            low_of(p, item, xn1T[1][:, :, i * P:(i + 1) * P],
                                   bank(item)[:, 0:D].rearrange("p (c n) -> p c n", c=DC), xn1T[0][:, :, i * P:(i + 1) * P])
                assert per_turn[0] == LINKS, per_turn[0]

            own.per_turn = LINKS
            overlapped(dve, body)

        @block.tensor
        def _(pe):
            pe.sem_inc(pv_ok.sem, 2)

            def product3(out, lhs, rhs, start, stop):
                for n, (i, j) in enumerate(((0, 0), (0, 1), (1, 0))):
                    last = pe.matmul(out, lhs[i], rhs[j], start=start and n == 0, stop=stop and n == 2, skip_group_check=True)
                return last

            def shared(q, n):
                kind, i = back[n]
                if n == 0:
                    pe.wait_ge(item_done.sem, item_done.at(q, number["norm", TP - 1] + 1))
                if back[n] == ("sum", 0):
                    pe.wait_ge(hs_low.sem, hs_low.at(q, len(ST)))
                pe.wait_ge(b_done.sem, b_done.at(q, n))
                if kind == "ffs":
                    at = (i % 2) * SHARED + ST[i // 2]
                    for c in range(DC):
                        last = product3(ps_b[:], [w[:, c, at:at + P] for w in w_s13], [x[:, c, :] for x in xn1T],
                                        c == 0, c == DC - 1)
                elif kind == "logit":
                    for c in range(DC):
                        for a in range(2):
                            last = pe.matmul(ps_b[:], w_gate1[:, c, :], xn1T[a][:, c, :], start=(c + a == 0), stop=(c + a == DC))
                else:
                    for m in range(len(ST)):
                        last = product3(ps_b[:, 0:D], [x[:, m, i * P:(i + 1) * P] for x in sT], [w[:, m, :] for w in w_s2],
                                        m == 0, m == len(ST) - 1)
                last.then_inc(b_full.sem, 1)

            def body(p, q):
                if p is None:
                    for n in range(len(back)):
                        shared(q, n)
                    return

                def begin(item):
                    pe.wait_ge(item_done.sem, item_done.at(p, number[item] + 1 - len(ps_m)))
                    return bank(item)

                def full(last):
                    last.then_inc(item_full.sem, 1)

                def after(item):
                    pe.wait_ge(item_done.sem, item_done.at(p, number[item] + 1))

                for c in range(DC):
                    out = begin(("xT", c))
                    for t in range(TP):
                        if c == 0:
                            pe.wait_ge(ln_done.sem, ln_done.at(p, t + 1))
                        last = pe.transpose(out[:, t * P:(t + 1) * P], xn[:, t, c * P:(c + 1) * P], ident[:])
                    full(last)
                after(("xT", 1))
                for m in range(DC):
                    out = begin(("q", m))
                    for c in range(DC):
                        last = product3(out[:], [w[:, c, m * P:(m + 1) * P] for w in w_qkv], [x[:, c, :] for x in xnT],
                                        c == 0, c == DC - 1)
                    full(last)
                for s in range(2):
                    out = begin(("kv", s))
                    for c in range(DC):
                        product3(out[:, 0:SEQ], [w[:, c, D:D + P] for w in w_qkv],
                                 [x[:, c, s * SEQ:(s + 1) * SEQ] for x in xnT], c == 0, False)
                    for t in range(2):
                        for c in range(DC):
                            for a in range(2):
                                last = pe.matmul(out[:, SEQ + t * 2 * HD0:SEQ + (t + 1) * 2 * HD0],
                                                 xnT[a][:, c, (2 * s + t) * P:(2 * s + t + 1) * P],
                                                 w_v[:, c, :, :].rearrange("p i d -> p (i d)"),
                                                 start=False, stop=(a == 1 and c == DC - 1 and t == 1), skip_group_check=True)
                    full(last)

                def scores(n):
                    s, t, h0, nh = units[n]
                    w = (t + 1) * P
                    out = ps_s[n % 2]
                    pe.wait_ge(p_ok.sem, p_ok.at(p, n - 1))
                    by_head = out[:].rearrange("p (h k) -> p h k", h=nh)
                    pe.matmul(by_head[:, :, t * P:w], ident_r[:], mask_r[:].unsqueeze(1).to_broadcast([P, nh, P]), start=True, stop=False, skip_group_check=True)
                    for h in range(nh):
                        last = pe.matmul(out[:, h * w:(h + 1) * w], q3[:, h0 + h, (2 * s + t) * P:(2 * s + t + 1) * P],
                                         k3[:, s, 0:w], start=False, stop=(h == nh - 1), skip_group_check=True)
                    last.then_inc(s_full.sem, 1)

                def transposes(n):
                    pe.wait_ge(p_ok.sem, p_ok.at(p, n + 1))
                    pe.wait_ge(t_low.sem, t_low.at(p, n))
                    for b in range(4):
                        last = pe.transpose(ps_t[:, b * P:(b + 1) * P], probs[:, n % 3, b * P:(b + 1) * P], ident[:])
                    last.then_inc(t_full.sem, 1)

                def context(n):
                    s, t, h0, nh = units[n]
                    pe.wait_ge(t_low.sem, t_low.at(p, n + 1))
                    if h0 == 0:
                        pe.wait_ge(ctx_free.sem, ctx_free.at(p, 2 * s + t))
                    for h in range(nh):
                        at = (h0 + h) * 2 * HD0
                        for k in range(t + 1):
                            b = h * (t + 1) + k
                            v = vs[:, 2 * s + k, :, :].rearrange("p i d -> p (i d)")
                            pe.matmul(ps_c[:, at:at + 2 * HD0], pT[0][:, n % 2, b * P:(b + 1) * P], v,
                                      start=(h0 + h == 0 and k == 0), stop=False, skip_group_check=True)
                            last = pe.matmul(ps_c[:, at:at + HD0], pT[1][:, n % 2, b * P:(b + 1) * P], v[:, 0:HD0],
                                             start=False, stop=(h0 + h == HEADS0 - 1 and k == t), skip_group_check=True)
                    last.then_inc(pv_ok.sem, 1)

                def item_work(item):
                    kind, i = item
                    if kind == "norm":
                        pe.wait_ge(norm1_ok.sem, norm1_ok.at(p, i + 1))
                    if kind == "ctx":
                        pe.wait_ge(ctx_ok.sem, ctx_ok.at(p, i + 1))
                    if kind == "out":
                        after(("ctx", i))
                        if i == 0:
                            pe.wait_ge(h_low.sem, h_low.at(p, len(HT)))
                    out = begin(item)
                    if kind == "ffn":
                        w = w_gate if i % 2 == 0 else w_up
                        for c in range(DC):
                            for j in range(2):
                                last = pe.matmul(out[:], w[:, c, HT[i // 2]:HT[i // 2] + P], xnT[j][:, c, :],
                                                 start=(c == 0 and j == 0), stop=(c == DC - 1 and j == 1))
                    if kind in ("ctx", "norm"):
                        src = ctx_n[:] if kind == "ctx" else xn1[:, i, :]
                        for c in range(DC):
                            last = pe.transpose(out[:, c * P:(c + 1) * P], src[:, c * P:(c + 1) * P], ident[:])
                    if kind == "out":
                        pe.matmul(out[:, 0:D], ones_r[:], ob[0][:], start=True, stop=False, skip_group_check=True)
                        pe.matmul(out[:, 0:D], ones_r[:], ob[1][:], start=False, stop=False, skip_group_check=True)
                        for c in range(DC):
                            product3(out[:, 0:D], [x[:, i, c, :] for x in cT], [w[:, c, :] for w in w_o], False, False)
                        for m in range(len(HT)):
                            for j in range(2):
                                last = pe.matmul(out[:, D:2 * D], hT[j][:, m, i * P:(i + 1) * P], w_down[:, m, :],
                                                 start=False, stop=(m == len(HT) - 1 and j == 1), skip_group_check=True)
                    full(last)

                for i in range(EARLY):
                    item_work(("ffn", i))
                pe.wait_ge(q3_got.sem, q3_got.at(p, 48))
                for n, step in enumerate(steps):
                    if n < NU:
                        scores(n)
                    if 2 <= n <= NU + 1:
                        transposes(n - 2)
                    for item in step:
                        if item[0] == "ffn":
                            item_work(item)
                    if q is not None and n in back_at:
                        shared(q, back_at[n])
                    if 3 <= n <= NU + 2:
                        context(n - 3)
                    for item in step:
                        if item[0] != "ffn":
                            item_work(item)

            overlapped(pe, body)


W_BIAS = 2 * D
W_HEAD = W_BIAS + 4


def stage_attention(nc, dram, route):
    with ExitStack() as ctx:
        def sb(name, shape, dt=F32):
            return ctx.enter_context(nc.sbuf_tensor(name, shape, dt))

        def psum(name):
            return ctx.enter_context(nc.psum_tensor(name, [P, 512], F32))

        def sem(name):
            return ctx.enter_context(nc.semaphore(name))

        ident = sb("ident_a", [P, P])
        ones_f = sb("ones_fa", [1, P])
        ones_r = sb("ones_ra", [1, P], R32)
        xT = [sb(f"xTa{i}", [P, DC, PAIR], R32) for i in range(2)]
        w_v = [sb(f"w_v{i}", [P, DC, FEAT], R32) for i in range(2)]
        w_out = [sb(f"w_out{i}", [P, 2, HEADS1 // 2 * D], R32) for i in range(2)]
        bv = [sb(f"bv_wide{i}", [P, HEADS1, P], R32) for i in range(2)]
        raw_bo = sb("raw_bo", [1, 2, D])
        bo = [sb(f"bo{i}", [1, 2, D], R32) for i in range(2)]
        w_qk = [sb(f"w_qk{a}", [P, 2, W_HEAD], R32) for a in range(2)]
        qT = [sb(f"qTa{i}", [P, PAIR], R32) for i in range(2)]
        kT = [sb(f"kTa{i}", [P, PAIR], R32) for i in range(2)]
        v = [sb(f"v{i}", [P, TP, 2 * HD1], R32) for i in range(2)]
        probs = sb("probs_a", [P, 2, 2, SEQ])
        neg_max = sb("neg_max_a", [P, 2, 2])
        sums = sb("sums_a", [P, 2, 2])
        rinv = sb("rinv_a", [P, 2, 2])
        pT = [sb(f"pTa{i}", [P, 2, 512], R32) for i in range(2)]
        oT = [sb(f"oT{i}", [P, PAIR], R32) for i in range(2)]
        x2 = sb("x2a", [P, TP, D])
        RING = 4
        xe = sb("xe", [P, TILES, D])
        ex = [sb(f"ex{k}", [P, RING, D]) for k in range(TOP_K)]
        bank_q, bank_k = psum("bank_q"), psum("bank_k")
        ps_s = [psum(f"ps_sa{i}") for i in range(2)]
        ps_t = [psum(f"ps_ta{i}") for i in range(2)]
        ps_y = [psum(f"ps_y{i}") for i in range(2)]

        H = HEADS1
        w_got = [sem(f"wa_got{a}") for a in range(2)]
        v_first, v_rest, o_got = sem("v_first"), sem("v_rest"), sem("o_got")
        raw_bo_got = sem("raw_bo_got")
        bv_ok = sem("bv_ok")
        b_full = sem("b_full")
        bo_ok = sem("bo_ok")
        x_got = Signal(sem("xa_got"), 32)
        x2_out = Signal(sem("x2_out"), 16, 1)
        prep = sem("prep_a")
        q_full, k_full, o_full, v_full, y_done = (Signal(sem(n), 1) for n in ("q_full", "k_full", "o_full", "v_full", "y_done"))
        q_high, k_high, v_high, o_high = (Signal(sem(n), 1) for n in ("q_high", "k_high", "v_high", "o_high"))
        q_done = Signal(sem("q_done"), 1)
        k_done = Signal(sem("k_done"), 1)
        o_done = Signal(sem("o_done"), 1, 1)
        v_done = Signal(sem("v_done"), 1, 2)
        s_full = Signal(sem("sa_full"), 2)
        max_ok = Signal(sem("maxa_ok"), 2)
        exp_ok = Signal(sem("exp_ok"), 2, 2)
        rinv_ok = Signal(sem("rinv_ok"), 2)
        p_ok = Signal(sem("pa_ok"), 2)
        t_full = Signal(sem("ta_full"), 2)
        t_high = Signal(sem("ta_high"), 2)
        t_low = Signal(sem("ta_low"), 2, 2)
        xo_ok = Signal(sem("xo_ok"), 2)
        xe_got = sem("xe_got")
        ex_got = [[sem(f"ex_got{k}_{i}") for i in range(RING)] for k in range(TOP_K)]
        weighted = sem("weighted")
        xe_ok = Signal(sem("xe_ok"), TP * TOP_K)

        block = ctx.enter_context(nc.Block())

        def walk(eng, step, end, between=lambda: None):
            def middle(u):
                with eng.Fori(0, (H - 2) // 2) as j:
                    for a in range(2):
                        step(u, j * 2, 2 + a, j * 2 + 2, j * 2 + a)

            step(0, 0, 0, 0, None)
            step(0, 0, 1, 0, None)
            between()
            with eng.Fori(0, TURNS - 1) as u:
                middle(u)
                for a in range(2):
                    step(u, 0, H + a, 0, H - 2 + a)
                end(u)
            middle(TURNS - 1)
            for a in range(2):
                step(TURNS - 1, 0, H + a, None, H - 2 + a)
            end(TURNS - 1)

        def at(signal, base, i, n):
            return base * signal.per_turn + (signal.head + i * signal.per_turn + n)

        def parts_of(i, pair, y_head):
            return pair is not None, (i >= 1 and (pair is not None or i == H)), y_head is not None

        @block.sync
        def _(sp):
            def weights(a, head):
                sp.dma_start(w_qk[a][:].bitcast(F32), head.rearrange("m p n -> p m n")).then_inc(w_got[a], 16)

            def resident(to, m, h0, h1, got):
                for i in range(2):
                    for c in range(DC):
                        at = i * D + c * HD1
                        sp.dma_start(to[i][:, c, h0 * HD1:h1 * HD1].bitcast(F32).rearrange("p (h n) -> p h n", n=HD1),
                                     dram["w_head"][m, h0:h1, :, at:at + HD1].rearrange("h p n -> p h n")).then_inc(got, 16)

            weights(0, dram["w_head"][0:2, 0])
            for i in range(2):
                sp.dma_start(xT[i][:].bitcast(F32).rearrange("p c n -> p (c n)"), dram["xn1T"][i]).then_inc(x_got.sem, 16)
            resident(w_v, 2, 0, 2, v_first)
            weights(1, dram["w_head"][0:2, 1])
            resident(w_v, 2, 2, H, v_rest)
            resident(w_out, 3, 0, H, o_got)
            for i in range(2):
                sp.dma_start(raw_bo[:, i, :], dram["bo"].rearrange("(a n) -> a n", a=1)).then_inc(raw_bo_got, 16)
            sp.dma_start(xe[:].rearrange("p (u t) n -> p u (t n)", u=TURNS), dram["x1"].rearrange("u p n -> p u n")).then_inc(xe_got, 16)
            with sp.Fori(0, TURNS) as u:
                with sp.Fori(0, H // 2) as j:
                    for a in range(2):
                        sp.wait_ge(k_done.sem, at(k_done, u * H + j * 2, a, 1))
                        weights(a, dram["w_head"][0:2, ds((j * 2 + (2 + a)) % H, 1)].rearrange("m o p n -> m (o p) n"))
                sp.wait_ge(v_full.sem, at(v_full, u * H, H - 1, 1))
                for i in range(2):
                    sp.dma_start(xT[i][:].bitcast(F32).rearrange("p c n -> p (c n)"),
                                 dram["xn1T"][ds((u * 2 + (2 + i)) % (2 * TURNS), 1)].rearrange("o p n -> (o p) n"))\
                        .then_inc(x_got.sem, 16)
            sp.wait_ge(x_got.sem, 32 * (TURNS + 1))
            for a in range(2):
                sp.wait_ge(w_got[a], 16 * (TURNS * H // 2 + 1))

        @block.gpsimd
        def _(pool):
            pool.memset(ident[:], 0.0).then_inc(prep, 1)
            pool.memset(ones_f[:], 1.0).then_inc(prep, 1)
            pool.wait_ge(prep, 2)
            pool.affine_select(out=ident[:], in_=ident[:], compare_op=ALU.not_equal, fill=1.0, base=0,
                               pattern=[[-1, P]], channel_multiplier=1).then_inc(prep, 1)
            pool.wait_ge(xe_got, 16)

            def gather(t):
                for k in range(TOP_K):
                    pool.indirect_dma_start(ex[k][:, t % RING, :], None, dram["ys"],
                                            bass.IndirectOffsetOnAxis(ap=route.slot[k][:, t:t + 1], axis=0))\
                        .then_inc(ex_got[k][t % RING], 16)

            for t in range(RING - 1):
                gather(t)
            for t in range(TILES):
                for k in range(TOP_K):
                    pool.wait_ge(ex_got[k][t % RING], 16 * (t // RING + 1))
                    pool.tensor_tensor(ex[k][:, t % RING, :], ex[k][:, t % RING, :],
                                       route.weight[k][:, t:t + 1].to_broadcast([P, D]), ALU.mult).then_inc(weighted, 1)
                for k in range(TOP_K):
                    pool.wait_ge(weighted, TOP_K * t + k + 1)
                    if k:
                        pool.wait_ge(xe_ok.sem, TOP_K * t + k)
                    pool.tensor_tensor(xe[:, t, :], xe[:, t, :], ex[k][:, t % RING, :], ALU.add).then_inc(xe_ok.sem, 1)
                if t + RING - 1 < TILES:
                    if t:
                        pool.wait_ge(xe_ok.sem, TOP_K * t)
                    gather(t + RING - 1)

        @block.scalar
        def _(act):
            act.wait_ge(prep, 3)
            act.activation(ones_r[:], ones_f[:], ACT.Copy).then_inc(prep, 1)
            act.sem_inc(exp_ok.sem, 2)
            act.sem_inc(x2_out.sem, 1)
            v_bias = route.columns[:, 2, :, 0:1].to_broadcast([P, HEADS1, P])
            act.activation(bv[0][:], v_bias, ACT.Copy).then_inc(bv_ok, 1)

            def between():
                act.wait_ge(bo_ok, 2)
                act.activation(bo[0][:], raw_bo[:], ACT.Copy).then_inc(bo_ok, 1)

            def step(u, first, i, pair, y_head):
                base, a = u * H + first, i % 2
                now, back, _ = parts_of(i, pair, y_head)

                def take_v():
                    act.wait_ge(v_full.sem, at(v_full, base, i, 1))
                    act.activation(v[0][:, 2 * a:2 * a + 2, :].rearrange("p t n -> p (t n)"), (bank_k, bank_q)[a][:], ACT.Copy)\
                        .then_inc(v_high.sem, 1)

                if now:
                    act.wait_ge(q_full.sem, at(q_full, base, i, 1))
                    act.activation(qT[0][:], bank_q[:], ACT.Identity, bias=w_qk[a][:, 0, W_BIAS:W_BIAS + 1].bitcast(F32))\
                        .then_inc(q_high.sem, 1)
                    act.wait_ge(k_full.sem, at(k_full, base, i, 1))
                    act.activation(kT[0][:], bank_k[:], ACT.Identity, bias=w_qk[a][:, 1, W_BIAS:W_BIAS + 1].bitcast(F32))\
                        .then_inc(k_high.sem, 1)
                if back:
                    for s in range(2):
                        act.wait_ge(t_full.sem, at(t_full, base, i - 1, s + 1))
                        act.activation(pT[0][:, s, :], ps_t[s][:], ACT.Copy).then_inc(t_high.sem, 1)
                if now and a:
                    take_v()
                if now:
                    for s in range(2):
                        act.wait_ge(max_ok.sem, at(max_ok, base, i, s + 1))
                        for t in range(2):
                            last = act.activation(probs[:, s, t, :], ps_s[s][:, t * SEQ:(t + 1) * SEQ], ACT.Exp,
                                                  bias=neg_max[:, s, t:t + 1], scale=1.0, accum_out=sums[:, s, t:t + 1])
                        last.then_inc(exp_ok.sem, 1)
                if back:
                    act.wait_ge(o_full.sem, at(o_full, base, i - 1, 1))
                    act.activation(oT[0][:], ps_t[0][:], ACT.Copy).then_inc(o_high.sem, 1)
                if now and not a:
                    take_v()

            def end(u):
                act.wait_ge(xo_ok.sem, xo_ok.at(u, 2))
                act.dma_start(dram["out"].rearrange("(u t p) n -> u p t n", t=TP, p=P)[ds(u, 1)].rearrange("o p t n -> (o p) t n"), x2[:])\
                    .then_inc(x2_out.sem, 16)

            walk(act, step, end, between)
            act.wait_ge(x2_out.sem, x2_out.at(TURNS, 0))

        @block.vector
        def _(dve):
            dve.wait_ge(bv_ok, 1)
            v_bias = route.columns[:, 2, :, 0:1].to_broadcast([P, HEADS1, P])
            dve.tensor_tensor(bv[1][:], v_bias, bv[0][:].bitcast(F32), ALU.subtract).then_inc(bv_ok, 1)

            def between():
                dve.wait_ge(raw_bo_got, 32)
                dve.wait_ge(b_full, 1)
                for i in range(2):
                    dve.tensor_tensor(raw_bo[:, i, :], raw_bo[:, i, :], ps_y[0][0:1, 0:D], ALU.add).then_inc(bo_ok, 1)
                dve.wait_ge(bo_ok, 3)
                dve.tensor_tensor(bo[1][:], raw_bo[:], bo[0][:].bitcast(F32), ALU.subtract).then_inc(bo_ok, 1)

            dve.sem_inc(v_done.sem, 2)
            dve.sem_inc(o_done.sem, 1)
            dve.sem_inc(t_low.sem, 2)

            def low(dst, src, high, bias, signal):
                dve.scalar_tensor_tensor(out=dst, in0=src, scalar=bias, in1=high.bitcast(F32), op0=ALU.add,
                                         op1=ALU.subtract).then_inc(signal.sem, 1)

            def step(u, first, i, pair, y_head):
                base, a = u * H + first, i % 2
                now, back, _ = parts_of(i, pair, y_head)

                def take_v():
                    dve.wait_ge(v_high.sem, at(v_high, base, i, 1))
                    dve.tensor_tensor(v[1][:, 2 * a:2 * a + 2, :].rearrange("p t n -> p (t n)"), (bank_k, bank_q)[a][:],
                                      v[0][:, 2 * a:2 * a + 2, :].rearrange("p t n -> p (t n)").bitcast(F32), ALU.subtract)\
                        .then_inc(v_done.sem, 1)

                if now:
                    dve.wait_ge(q_high.sem, at(q_high, base, i, 1))
                    low(qT[1][:], bank_q[:], qT[0][:], w_qk[a][:, 0, W_BIAS:W_BIAS + 1].bitcast(F32), q_done)
                    dve.wait_ge(k_high.sem, at(k_high, base, i, 1))
                    low(kT[1][:], bank_k[:], kT[0][:], w_qk[a][:, 1, W_BIAS:W_BIAS + 1].bitcast(F32), k_done)
                if back:
                    for s in range(2):
                        dve.wait_ge(t_high.sem, at(t_high, base, i - 1, s + 1))
                        dve.tensor_tensor(pT[1][:, s, :], ps_t[s][:], pT[0][:, s, :].bitcast(F32), ALU.subtract)\
                            .then_inc(t_low.sem, 1)
                if now and a:
                    take_v()
                if i == H + 1:
                    dve.wait_ge(y_done.sem, at(y_done, u * H, H, 0))
                    dve.wait_ge(x2_out.sem, x2_out.at(u, 0))
                    dve.wait_ge(xe_ok.sem, xe_ok.at(u, TP * TOP_K))
                    tiles = xe[:, ds(u * TP, TP), :]
                    for b in range(2):
                        dve.tensor_tensor(x2[:, 2 * b:2 * b + 2, :].rearrange("p t n -> p (t n)"),
                                          tiles[:, 2 * b:2 * b + 2, :].rearrange("p t n -> p (t n)"), ps_y[b][:], ALU.add)\
                            .then_inc(xo_ok.sem, 1)
                if now:
                    for s in range(2):
                        dve.wait_ge(s_full.sem, at(s_full, base, i, s + 1))
                        dve.tensor_reduce(neg_max[:, s, :], ps_s[s][:].rearrange("p (t k) -> p t k", t=2), AX.X, ALU.max,
                                          negate=True).then_inc(max_ok.sem, 1)
                    for s in range(2):
                        dve.wait_ge(exp_ok.sem, at(exp_ok, base, i, s + 1))
                        dve.reciprocal(rinv[:, s, :], sums[:, s, :]).then_inc(rinv_ok.sem, 1)
                        dve.wait_ge(rinv_ok.sem, at(rinv_ok, base, i, s + 1))
                        for t in range(2):
                            last = dve.tensor_scalar(probs[:, s, t, :], probs[:, s, t, :], rinv[:, s, t:t + 1], None, ALU.mult)
                        last.then_inc(p_ok.sem, 1)
                if back:
                    dve.wait_ge(o_high.sem, at(o_high, base, i - 1, 1))
                    dve.tensor_tensor(oT[1][:], ps_t[0][:], oT[0][:].bitcast(F32), ALU.subtract).then_inc(o_done.sem, 1)
                if now and not a:
                    take_v()

            walk(dve, step, lambda u: None, between)

        @block.tensor
        def _(pe):
            def product3(out, lhs, rhs, start, stop):
                for n, (i, j) in enumerate(((0, 0), (0, 1), (1, 0))):
                    last = pe.matmul(out, lhs[i], rhs[j], start=start and n == 0, stop=stop and n == 2, skip_group_check=True)
                return last

            def start_sums():
                for b in range(2):
                    for n in range(2):
                        pe.matmul(ps_y[b][:], ones_r[:], bo[n][:].rearrange("a i n -> a (i n)"), start=(n == 0), stop=False,
                                  skip_group_check=True)

            def project(out, a, m, signal):
                for c in range(DC):
                    w = [w_qk[a][:, m, i * D + c * HD1:i * D + (c + 1) * HD1] for i in range(2)]
                    last = product3(out[:], w, [x[:, c, :] for x in xT], c == 0, c == DC - 1)
                last.then_inc(signal.sem, 1)

            def project_v(u, base, i, pair):
                a = i % 2
                if a:
                    pe.wait_ge(q_done.sem, at(q_done, base, i, 1))
                else:
                    pe.wait_ge(k_done.sem, at(k_done, base, i, 1))
                if isinstance(u, int) and i == 0:
                    pe.wait_ge(v_first, 64)
                for n in range(2):
                    t = 2 * a + n
                    for c in range(DC):
                        last = product3((bank_k, bank_q)[a][:, n * 2 * HD1:(n + 1) * 2 * HD1], [x[:, c, t * P:(t + 1) * P] for x in xT],
                                        [w[:, c, ds(pair * HD1, 2 * HD1)] for w in w_v], c == 0, c == DC - 1)
                last.then_inc(v_full.sem, 1)

            def step(u, first, i, pair, y_head):
                base, a = u * H + first, i % 2
                now, back, two_back = parts_of(i, pair, y_head)
                if now:
                    if i % H == 0:
                        pe.wait_ge(x_got.sem, x_got.at(u, 32 * (i // H + 1)))
                    pe.wait_ge(w_got[a], base * 8 + 16 * (i // 2 + 1))
                    pe.wait_ge(v_done.sem, at(v_done, base, i - 1 - a, 1))
                    project(bank_q, a, 0, q_full)
                    pe.wait_ge(v_done.sem, at(v_done, base, i - 2 + a, 1))
                    project(bank_k, a, 1, k_full)
                if back:
                    for s in range(2):
                        pe.wait_ge(p_ok.sem, at(p_ok, base, i - 1, s + 1))
                        pe.wait_ge(t_low.sem, at(t_low, base, i - 2, s + 1))
                        if s == 0:
                            pe.wait_ge(o_done.sem, at(o_done, base, i - 2, 1))
                        for k in range(2):
                            for t in range(2):
                                last = pe.transpose(ps_t[s][:, (2 * k + t) * P:(2 * k + t + 1) * P],
                                                    probs[:, s, t, k * P:(k + 1) * P], ident[:])
                        last.then_inc(t_full.sem, 1)
                if now and a:
                    project_v(u, base, i, pair)
                if two_back:
                    pe.wait_ge(o_done.sem, at(o_done, base, i - 2, 1))
                    for t in range(TP):
                        last = product3(ps_y[t // 2][:, (t % 2) * D:(t % 2 + 1) * D], [o[:, t * P:(t + 1) * P] for o in oT],
                                        [w[:].rearrange("p c n -> p (c n)")[:, ds(y_head * D, D)] for w in w_out], False, i == H + 1)
                    last.then_inc(y_done.sem, 1)
                if now:
                    pe.wait_ge(k_done.sem, at(k_done, base, i, 1))
                    for s in range(2):
                        pe.wait_ge(exp_ok.sem, at(exp_ok, base, i - 1, s + 1))
                        for t in range(2):
                            last = product3(ps_s[s][:, t * SEQ:(t + 1) * SEQ],
                                            [x[:, (2 * s + t) * P:(2 * s + t + 1) * P] for x in qT],
                                            [x[:, s * SEQ:(s + 1) * SEQ] for x in kT], True, True)
                        last.then_inc(s_full.sem, 1)
                if back:
                    pe.wait_ge(v_done.sem, at(v_done, base, i - 1 + a, 1))
                    b = 1 - a
                    for s in range(2):
                        pe.wait_ge(t_low.sem, at(t_low, base, i - 1, s + 1))
                        for k in range(2):
                            last = product3(ps_t[0][:, s * SEQ:(s + 1) * SEQ], [x[:, 2 * s + k, b * HD1:(b + 1) * HD1] for x in v],
                                            [x[:, s, k * SEQ:(k + 1) * SEQ] for x in pT], k == 0, k == 1)
                    last.then_inc(o_full.sem, 1)
                if now and not a:
                    project_v(u, base, i, pair)
                if now and i == H + 1:
                    pe.wait_ge(xo_ok.sem, xo_ok.at(u, 2))
                    start_sums()

            def between():
                pe.wait_ge(v_rest, 64)
                pe.wait_ge(o_got, 64)
                pe.wait_ge(bv_ok, 2)
                for h in range(H):
                    half, at = h // (H // 2), h % (H // 2) * D
                    last = product3(ps_y[0][:, 0:D], [b[:, h, :] for b in bv], [w[:, half, at:at + D] for w in w_out],
                                    h == 0, h == H - 1)
                last.then_inc(b_full, 1)
                pe.wait_ge(bo_ok, 4)
                start_sums()

            pe.wait_ge(prep, 4)
            walk(pe, step, lambda u: None, between)


TOP_K = 2
SLOT_TILES = -(-(TOP_K * TOKENS + EXPERTS * (P - 1)) // P)
SLOT_TILES += SLOT_TILES % 2
SLOTS = SLOT_TILES * P


def stage_routing(nc, dram, route):
    with ExitStack() as ctx:
        def sb(name, shape, dt=F32):
            return ctx.enter_context(nc.sbuf_tensor(name, shape, dt))

        def sem(name):
            return ctx.enter_context(nc.semaphore(name))

        lgT = sb("lgT_r", [2 * EXPERTS, TOKENS])
        rows_b = sb("rows_b", [3 * HEADS1, HD1])
        ident = sb("ident_r2", [3 * HEADS1, 3 * HEADS1])
        lg_high = sb("lg_high", [P, TILES, EXPERTS])
        lg = sb("lg_r", [P, TILES, EXPERTS])
        work = [sb(f"work{i}", [P, TILES, EXPERTS]) for i in range(2)]
        probs = sb("probs_r", [P, TILES, EXPERTS])
        masks = [sb(f"mask{i}", [P, TILES, EXPERTS]) for i in range(TOP_K)]
        chosen = sb("chosen", [P, TILES, EXPERTS], R32)
        rank = sb("rank", [P, TILES, EXPERTS])
        totals = [sb(f"totals{i}", [P, TILES, EXPERTS]) for i in range(2)]
        row = sb("row_r", [P, TILES])
        falling = sb("falling", [P, EXPERTS])
        place = sb("place", [P, TILES])
        counts_i = sb("counts_i", [P, EXPERTS], I32)
        tiles_i = sb("tiles_i", [P, EXPERTS], I32)
        tiles_f = sb("tiles_f", [P, EXPERTS])
        ends = [sb(f"ends{i}", [P, EXPERTS]) for i in range(2)]
        first = sb("first", [P, EXPERTS])
        tile_no = sb("tile_no", [1, SLOT_TILES])
        passed = sb("passed", [1, SLOT_TILES, EXPERTS])
        expert_f = sb("expert_f", [1, SLOT_TILES])
        before_f = sb("before_f", [P, P])
        before = sb("before", [P, P], R32)
        all_f = sb("all_f", [P, P])
        ones = sb("ones_r2", [P, P], R32)
        ps_rank = ctx.enter_context(nc.psum_tensor("ps_rank", [P, 512], F32))
        ps_total = ctx.enter_context(nc.psum_tensor("ps_total", [P, 512], F32))

        got = sem("lg_got")
        ident_ok = sem("ident_ok_r")
        biases_got = sem("biases_got")
        biases_turned = sem("biases_turned")
        columns_ok = sem("columns_ok")
        columns_out = sem("columns_out")
        turned = sem("turned_r")
        rows_got = sem("rows_got_r")
        made = sem("made")
        cast = sem("cast")
        shifted = sem("shifted")
        exp_done = sem("exp_done")
        own = sem("own_r")
        chosen_ok = sem("chosen_ok")
        summed = sem("summed")
        block = ctx.enter_context(nc.Block())

        ps_bias = ctx.enter_context(nc.psum_tensor("ps_bias", [P, 512], F32))
        ps_lg = ctx.enter_context(nc.psum_tensor("ps_lg", [P, TILES, 2, EXPERTS], F32))

        def flat(t):
            return t[:].rearrange("p t e -> p (t e)")

        @block.sync
        def _(sp):
            sp.dma_start(lgT[:].rearrange("p (u n) -> p u n", u=TURNS), dram["logits"].rearrange("u p n -> p u n"))\
                .then_inc(got, 16)
            sp.dma_start(route.rows[:].rearrange("p (u t) n -> p u (t n)", u=TURNS), dram["xn1"].rearrange("u p n -> p u n"))\
                .then_inc(rows_got, 16)
            for m in range(3):
                sp.dma_start(rows_b[m * HEADS1:(m + 1) * HEADS1, :], dram["b" + "qkv"[m]].rearrange("(h p) -> h p", p=HD1))\
                    .then_inc(biases_got, 16)
            sp.wait_ge(rows_got, 16)

        @block.gpsimd
        def _(pool):
            pool.memset(route.columns[:], 0.0).then_inc(columns_ok, 1)
            pool.memset(ident[:], 0.0).then_inc(ident_ok, 1)
            pool.wait_ge(ident_ok, 1)
            pool.affine_select(out=ident[:], in_=ident[:], compare_op=ALU.not_equal, fill=1.0, base=0,
                               pattern=[[-1, 3 * HEADS1]], channel_multiplier=1).then_inc(ident_ok, 1)
            pool.memset(before_f[:], 1.0).then_inc(made, 1)
            pool.memset(all_f[:], 1.0).then_inc(made, 1)
            pool.iota(falling[:], [[-1, EXPERTS]], base=EXPERTS, channel_multiplier=0, allow_small_or_imprecise_dtypes=True)\
                .then_inc(made, 1)
            pool.iota(tile_no[:], [[1, SLOT_TILES]], base=0, channel_multiplier=0, allow_small_or_imprecise_dtypes=True)\
                .then_inc(made, 1)
            pool.wait_ge(made, 4)
            pool.affine_select(out=before_f[:], in_=before_f[:], compare_op=ALU.is_gt, fill=0.0, base=0,
                               pattern=[[1, P]], channel_multiplier=-1).then_inc(made, 1)
            pool.wait_ge(columns_ok, 4)
            for m in range(2):
                pool.dma_start(dram["w_head"][m, :, :, W_BIAS:W_HEAD].rearrange("h p n -> p h n"), route.columns[:, m, :, :])\
                    .then_inc(columns_out, 16)
            pool.wait_ge(columns_out, 32)

        @block.scalar
        def _(act):
            act.wait_ge(made, 5)
            act.activation(before[:], before_f[:], ACT.Copy).then_inc(cast, 1)
            act.activation(ones[:], all_f[:], ACT.Copy).then_inc(cast, 1)
            act.wait_ge(shifted, 1)
            act.activation(flat(work[1]), flat(work[0]), ACT.Exp).then_inc(exp_done, 1)

        @block.tensor
        def _(pe):
            pe.wait_ge(ident_ok, 2)
            pe.wait_ge(got, 16)
            for t in range(TILES):
                last = pe.transpose(ps_lg[:, t, :, :].rearrange("p i e -> p (i e)"), lgT[:, t * P:(t + 1) * P],
                                    ident[0:2 * EXPERTS, 0:2 * EXPERTS])
            last.then_inc(turned, 1)
            pe.wait_ge(biases_got, 48)
            pe.transpose(ps_bias[:, 0:3 * HEADS1], rows_b[:], ident[:]).then_inc(biases_turned, 1)
            pe.wait_ge(cast, 2)
            pe.wait_ge(chosen_ok, 1)
            n = TILES * EXPERTS
            pe.matmul(ps_rank[:, 0:n], before[:], flat(chosen), start=True, stop=True)
            pe.matmul(ps_total[:, 0:n], ones[:], flat(chosen), start=True, stop=True).then_inc(summed, 1)

        @block.vector
        def _(dve):
            steps = [0]

            def link(ins):
                steps[0] += 1
                ins.then_inc(own, 1)
                dve.wait_ge(own, steps[0])

            def wide(t):
                return t.unsqueeze(2).to_broadcast([P, TILES, EXPERTS])

            falling_w = falling[:].unsqueeze(1).to_broadcast([P, TILES, EXPERTS])
            dve.wait_ge(turned, 1)
            link(dve.tensor_copy(lg_high[:], ps_lg[:, :, 0, :]))
            link(dve.tensor_tensor(lg[:], lg_high[:], ps_lg[:, :, 1, :], ALU.add))
            dve.wait_ge(made, 5)
            link(dve.tensor_reduce(row[:], lg[:], AX.X, ALU.max))
            dve.tensor_tensor(work[0][:], lg[:], wide(row[:]), ALU.subtract).then_inc(shifted, 1)
            dve.wait_ge(columns_ok, 1)
            dve.wait_ge(biases_turned, 1)
            for m in range(3):
                dve.tensor_scalar(route.columns[:, m, :, 0], ps_bias[:, m * HEADS1:(m + 1) * HEADS1],
                                  HD1 ** -0.5 if m == 0 else 1.0, None, ALU.mult).then_inc(columns_ok, 1)
            dve.wait_ge(exp_done, 1)
            link(dve.tensor_reduce(row[:], work[1][:], AX.X, ALU.add))
            link(dve.reciprocal(place[:], row[:]))
            link(dve.tensor_tensor(probs[:], work[1][:], wide(place[:]), ALU.mult))
            for k in range(TOP_K):
                weight = route.weight[k]
                link(dve.tensor_reduce(weight[:], probs[:], AX.X, ALU.max))
                link(dve.tensor_tensor(work[0][:], probs[:], wide(weight[:]), ALU.is_equal))
                link(dve.tensor_tensor(work[1][:], work[0][:], falling_w, ALU.mult))
                link(dve.tensor_reduce(row[:], work[1][:], AX.X, ALU.max))
                link(dve.tensor_tensor(masks[k][:], falling_w, wide(row[:]), ALU.is_equal))
                if k == 0:
                    link(dve.scalar_tensor_tensor(out=flat(probs), in0=flat(masks[0]), scalar=-2.0, in1=flat(probs),
                                                  op0=ALU.mult, op1=ALU.add))
            dve.tensor_tensor(chosen[:], masks[0][:], masks[1][:], ALU.add).then_inc(chosen_ok, 1)
            dve.wait_ge(summed, 1)
            n = TILES * EXPERTS
            link(dve.tensor_copy(flat(rank), ps_rank[:, 0:n]))
            link(dve.tensor_copy(flat(totals[0]), ps_total[:, 0:n]))
            link(dve.tensor_tensor(flat(rank), flat(rank), flat(totals[0]), ALU.subtract))
            src, dst, d = totals[0], totals[1], 1
            while d < TILES:
                link(dve.tensor_copy(dst[:, 0:d, :], src[:, 0:d, :]))
                link(dve.tensor_tensor(dst[:, d:, :], src[:, d:, :], src[:, 0:TILES - d, :], ALU.add))
                src, dst, d = dst, src, 2 * d
            link(dve.tensor_tensor(rank[:], rank[:], src[:], ALU.add))
            link(dve.tensor_scalar(counts_i[:], src[:, TILES - 1, :], float(P - 1), None, ALU.add))
            link(dve.tensor_scalar(tiles_i[:], counts_i[:], P.bit_length() - 1, None, ALU.arith_shift_right))
            link(dve.tensor_copy(tiles_f[:], tiles_i[:]))
            link(dve.tensor_copy(ends[0][:], tiles_f[:]))
            a, b, d = ends[0], ends[1], 1
            while d < EXPERTS:
                link(dve.tensor_copy(b[:, 0:d], a[:, 0:d]))
                link(dve.tensor_tensor(b[:, d:], a[:, d:], a[:, 0:EXPERTS - d], ALU.add))
                a, b, d = b, a, 2 * d
            link(dve.tensor_tensor(first[:], a[:], tiles_f[:], ALU.subtract))
            link(dve.tensor_scalar(first[:], first[:], float(P), None, ALU.mult))
            link(dve.tensor_tensor(rank[:], rank[:], first[:].unsqueeze(1).to_broadcast([P, TILES, EXPERTS]), ALU.add))
            for k in range(TOP_K):
                link(dve.tensor_tensor(work[0][:], masks[k][:], rank[:], ALU.mult))
                link(dve.tensor_reduce(place[:], work[0][:], AX.X, ALU.add))
                link(dve.tensor_copy(route.slot[k][:], place[:]))
            link(dve.tensor_tensor(passed[:], a[0:1, :].unsqueeze(1).to_broadcast([1, SLOT_TILES, EXPERTS]),
                                   tile_no[:].unsqueeze(2).to_broadcast([1, SLOT_TILES, EXPERTS]), ALU.is_le))
            link(dve.tensor_reduce(expert_f[:], passed[:], AX.X, ALU.add))
            link(dve.tensor_scalar(route.expert[:], expert_f[:], float(EXPERTS - 1), None, ALU.min))


HALF = INTER // 2


def stage_experts(nc, dram, route):
    with ExitStack() as ctx:
        def sb(name, shape, dt=F32):
            return ctx.enter_context(nc.sbuf_tensor(name, shape, dt))

        def psum(name):
            return ctx.enter_context(nc.psum_tensor(name, [P, 512], F32))

        def sem(name):
            return ctx.enter_context(nc.semaphore(name))

        UP = DC * 2 * INTER
        DOWN = 2 * D
        RAW = 4
        ident = sb("ident_e", [P, P])
        w_up = [sb(f"we_up{i}", [P, EXPERTS * UP], R32) for i in range(2)]
        w_down = [sb(f"we_down{i}", [HALF, EXPERTS * DOWN], R32) for i in range(2)]
        raw_up = sb("raw_up", [P, RAW, DC, 2, INTER])
        raw_down = sb("raw_down_e", [HALF, RAW, DOWN])
        xs = sb("xs_e", [P, 4, D])
        xT = [sb(f"xTe{i}", [P, 2, D], R32) for i in range(2)]
        tanh_g = sb("tanh_e", [P, 2, INTER])
        gated = sb("gated_e", [P, 2, INTER])
        h_f = sb("h_fe", [P, 2, INTER])
        hT = [sb(f"hTe{i}", [HALF, 2, 2 * P], R32) for i in range(2)]
        ys = sb("ys_e", [P, 2, D])
        ps_x = [psum(f"ps_x{i}") for i in range(2)]
        ps_u = [psum(f"ps_u{i}") for i in range(2)]
        ps_h = [psum(f"ps_h{i}") for i in range(2)]
        ps_d = [psum(f"ps_d{i}") for i in range(2)]

        id_ok = sem("ide_ok")
        raw_got = [sem(f"raw_got{i}") for i in range(RAW)]
        sent = sem("sent")
        w_high = sem("w_high")
        w_low = sem("w_low")
        x_got = [Signal(sem(f"xs_got{i}"), 4) for i in range(4)]
        x_full = Signal(sem("xe_full"), 1, 4)
        x_high = Signal(sem("xe_high"), 1)
        x_low = Signal(sem("xe_low"), 1, 2)
        u_full = Signal(sem("ue_full"), 1)
        tanh_ok = Signal(sem("tanhe_ok"), 1)
        gate_ok = Signal(sem("gatee_ok"), 1)
        h_ok = Signal(sem("he_ok"), 1, 2)
        h_full = Signal(sem("he_full"), 1)
        h_high = Signal(sem("he_high"), 1)
        h_low = Signal(sem("he_low"), 1, 2)
        d_full = Signal(sem("de_full"), 1)
        y_ok = Signal(sem("ye_ok"), 1, 2)
        y_out = [Signal(sem(f"y_out{i}"), 8, 16) for i in range(2)]

        block = ctx.enter_context(nc.Block())

        def at(signal, base, i, n):
            return base * signal.per_turn + (signal.head + i * signal.per_turn + n)

        LAG = 3
        FILL = 8

        loaded = {}

        def steps(eng, step):
            for i in range(FILL):
                step(0, i, i)
            with eng.Fori(0, (SLOT_TILES - FILL) // FILL) as j:
                loaded.clear()
                for a in range(FILL):
                    step(j * FILL, FILL + a, FILL)
            loaded.clear()
            for i in range(LAG):
                step(SLOT_TILES, i, SLOT_TILES + i)

        @block.sync
        def _(sp):
            for e in range(EXPERTS):
                if e >= RAW:
                    sp.wait_ge(w_low, 2 * (e - RAW + 1))
                for i, m in enumerate(("w1T", "w3T")):
                    sp.dma_start(raw_up[:, e % RAW, :, i, :], dram[m][e].rearrange("(c p) n -> p c n", p=P)).then_inc(raw_got[e % RAW], 16)
                sp.dma_start(raw_down[:, e % RAW, :].rearrange("p (c n) -> p c n", n=D),
                             dram["w2T"][e].rearrange("(c p) n -> p c n", p=HALF)).then_inc(raw_got[e % RAW], 16)
            sp.wait_ge(sent, 16 * TILES * TOP_K)
            with sp.Fori(0, SLOT_TILES // 4) as j:
                for a in range(4):
                    sp.wait_ge(x_full.sem, at(x_full, j * 4, a - 4, 1))
                    sp.dma_start(xs[:, a, :], dram["xs"].rearrange("(t p) n -> t p n", p=P)[ds(j * 4 + a, 1)]
                                 .rearrange("o p n -> (o p) n")).then_inc(x_got[a].sem, 16)

        @block.gpsimd
        def _(pool):
            pool.memset(ident[:], 0.0).then_inc(id_ok, 1)
            pool.wait_ge(id_ok, 1)
            pool.affine_select(out=ident[:], in_=ident[:], compare_op=ALU.not_equal, fill=1.0, base=0,
                               pattern=[[-1, P]], channel_multiplier=1).then_inc(id_ok, 1)
            for t in range(TILES):
                for k in range(TOP_K):
                    pool.indirect_dma_start(dram["xs"], bass.IndirectOffsetOnAxis(ap=route.slot[k][:, t:t + 1], axis=0),
                                            route.rows[:, t, :], None).then_inc(sent, 16)

        def weights_of(e):
            return [(raw_up[:, e % RAW].rearrange("p c i n -> p (c i n)"), *[w[:, e * UP:(e + 1) * UP] for w in w_up]),
                    (raw_down[:, e % RAW, :], *[w[:, e * DOWN:(e + 1) * DOWN] for w in w_down])]

        @block.scalar
        def _(act):
            for e in range(EXPERTS):
                act.wait_ge(raw_got[e % RAW], 48 * (e // RAW + 1))
                for raw, high, _ in weights_of(e):
                    act.activation(high, raw, ACT.Copy).then_inc(w_high, 1)

            def step(base, i, kind):
                if kind < SLOT_TILES:
                    b = i % 2
                    act.wait_ge(x_full.sem, at(x_full, base, i, 1))
                    act.activation(xT[0][:, b, :], ps_x[b][:, 0:D], ACT.Copy).then_inc(x_high.sem, 1)
                if 1 <= kind < SLOT_TILES + 1:
                    b = (i - 1) % 2
                    act.wait_ge(u_full.sem, at(u_full, base, i - 1, 1))
                    act.activation(tanh_g[:, b, :], ps_u[b][:, 0:INTER], ACT.Tanh, scale=0.5).then_inc(tanh_ok.sem, 1)
                if 2 <= kind < SLOT_TILES + 2:
                    b = (i - 2) % 2
                    act.wait_ge(h_full.sem, at(h_full, base, i - 2, 1))
                    act.activation(hT[0][:, b, :], ps_h[b][0:HALF, 0:2 * P], ACT.Copy).then_inc(h_high.sem, 1)
                if 3 <= kind < SLOT_TILES + 3:
                    b = (i - 3) % 2
                    act.wait_ge(d_full.sem, at(d_full, base, i - 3, 1))
                    act.wait_ge(y_out[b].sem, base * 8 + 16 * ((i - 3) // 2 + 1))
                    act.activation(ys[:, b, :], ps_d[b][:, 0:D], ACT.Copy).then_inc(y_ok.sem, 1)
                    act.wait_ge(y_ok.sem, at(y_ok, base, i - 3, 1))
                    tiles = dram["ys"].rearrange("(t p) n -> t p n", p=P)
                    act.dma_start(tiles[ds(base + (i - 3), 1)].rearrange("o p n -> (o p) n"), ys[:, b, :])\
                        .then_inc(y_out[b].sem, 16)

            act.sem_inc(y_ok.sem, 2)
            for b in range(2):
                act.sem_inc(y_out[b].sem, 16)
            steps(act, step)
            for b in range(2):
                act.wait_ge(y_out[b].sem, 16 + 8 * SLOT_TILES)

        @block.vector
        def _(dve):
            for e in range(EXPERTS):
                for m, (raw, high, low) in enumerate(weights_of(e)):
                    dve.wait_ge(w_high, 2 * e + m + 1)
                    dve.tensor_tensor(low, raw, high.bitcast(F32), ALU.subtract).then_inc(w_low, 1)
            dve.sem_inc(x_low.sem, 2)
            dve.sem_inc(h_ok.sem, 2)
            dve.sem_inc(h_low.sem, 2)

            def step(base, i, kind):
                if kind < SLOT_TILES:
                    b = i % 2
                    dve.wait_ge(x_high.sem, at(x_high, base, i, 1))
                    dve.tensor_tensor(xT[1][:, b, :], ps_x[b][:, 0:D], xT[0][:, b, :].bitcast(F32), ALU.subtract).then_inc(x_low.sem, 1)
                if 1 <= kind < SLOT_TILES + 1:
                    b = (i - 1) % 2
                    dve.wait_ge(tanh_ok.sem, at(tanh_ok, base, i - 1, 1))
                    dve.scalar_tensor_tensor(out=gated[:, b, :], in0=tanh_g[:, b, :], scalar=1.0, in1=ps_u[b][:, 0:INTER],
                                             op0=ALU.add, op1=ALU.mult).then_inc(gate_ok.sem, 1)
                    dve.wait_ge(gate_ok.sem, at(gate_ok, base, i - 1, 1))
                    dve.scalar_tensor_tensor(out=h_f[:, b, :], in0=ps_u[b][:, INTER:2 * INTER], scalar=0.5, in1=gated[:, b, :],
                                             op0=ALU.mult, op1=ALU.mult).then_inc(h_ok.sem, 1)
                if 2 <= kind < SLOT_TILES + 2:
                    b = (i - 2) % 2
                    dve.wait_ge(h_high.sem, at(h_high, base, i - 2, 1))
                    dve.tensor_tensor(hT[1][:, b, :], ps_h[b][0:HALF, 0:2 * P], hT[0][:, b, :].bitcast(F32), ALU.subtract)\
                        .then_inc(h_low.sem, 1)

            steps(dve, step)

        @block.tensor
        def _(pe):
            pe.wait_ge(id_ok, 2)
            pe.wait_ge(w_low, 2 * EXPERTS)
            pe.sem_inc(x_full.sem, 4)

            def expert(base, i):
                if i not in loaded:
                    loaded[i] = pe.value_load(route.expert[0:1, ds(base + i, 1)], min_val=0, max_val=EXPERTS - 1)
                return loaded[i]

            def step(base, i, kind):
                if 1 <= kind < SLOT_TILES + 1:
                    e_up = expert(base, i - 1)
                if 3 <= kind < SLOT_TILES + 3:
                    e_down = expert(base, i - 3)
                if kind < SLOT_TILES:
                    b = i % 2
                    pe.wait_ge(x_got[i % 4].sem, base * 4 + 16 * (i // 4 + 1))
                    pe.wait_ge(x_low.sem, at(x_low, base, i - 2, 1))
                    for c in range(DC):
                        last = pe.transpose(ps_x[b][:, c * P:(c + 1) * P], xs[:, i % 4, c * P:(c + 1) * P], ident[:])
                    last.then_inc(x_full.sem, 1)
                if 1 <= kind < SLOT_TILES + 1:
                    b = (i - 1) % 2
                    pe.wait_ge(x_low.sem, at(x_low, base, i - 1, 1))
                    pe.wait_ge(h_ok.sem, at(h_ok, base, i - 3, 1))
                    for c in range(DC):
                        for n, (x, w) in enumerate(((0, 0), (0, 1), (1, 0))):
                            last = pe.matmul(ps_u[b][:, 0:2 * INTER], xT[x][:, b, c * P:(c + 1) * P],
                                             w_up[w][:, ds(e_up * UP + c * 2 * INTER, 2 * INTER)],
                                             start=(c == 0 and n == 0), stop=(c == DC - 1 and n == 2), skip_group_check=True)
                    last.then_inc(u_full.sem, 1)
                if 2 <= kind < SLOT_TILES + 2:
                    b = (i - 2) % 2
                    pe.wait_ge(h_ok.sem, at(h_ok, base, i - 2, 1))
                    pe.wait_ge(h_low.sem, at(h_low, base, i - 4, 1))
                    for c in range(2):
                        last = pe.transpose(ps_h[b][0:HALF, c * P:(c + 1) * P], h_f[:, b, c * HALF:(c + 1) * HALF], ident[:])
                    last.then_inc(h_full.sem, 1)
                if 3 <= kind < SLOT_TILES + 3:
                    b = (i - 3) % 2
                    pe.wait_ge(h_low.sem, at(h_low, base, i - 3, 1))
                    pe.wait_ge(y_ok.sem, at(y_ok, base, i - 5, 1))
                    for c in range(2):
                        for n, (x, w) in enumerate(((0, 0), (0, 1), (1, 0))):
                            last = pe.matmul(ps_d[b][:, 0:D], hT[x][:, b, c * P:(c + 1) * P],
                                             w_down[w][:, ds(e_down * DOWN + c * D, D)],
                                             start=(c == 0 and n == 0), stop=(c == 1 and n == 2), skip_group_check=True)
                    last.then_inc(d_full.sem, 1)

            steps(pe, step)


class Route:

    def __init__(self, nc, ctx):
        def sb(name, shape, dt):
            return ctx.enter_context(nc.sbuf_tensor(name, shape, dt))

        self.slot = [sb(f"slot{k}", [P, TILES], I32) for k in range(TOP_K)]
        self.weight = [sb(f"weight{k}", [P, TILES], F32) for k in range(TOP_K)]
        self.expert = sb("expert", [1, SLOT_TILES], I32)
        self.columns = sb("columns", [P, 3, HEADS1, 4], F32)


def keep_rows(nc, ctx, route):
    route.rows = ctx.enter_context(nc.sbuf_tensor("rows_s", [P, TILES, D], F32))


def program(nc, dram):
    for name, shape, dt in (
        ("q_scr", [2, D, PAIR], F32),
        ("xn1", [TURNS, P, TP * D], F32),
        ("xn1T", [2 * TURNS, P, DC * PAIR], F32),
        ("x1", [TURNS, P, TP * D], F32),
        ("scales", [4, DC, P // BLOCK, FEAT], F32),
        ("w_head", [4, HEADS1, P, W_HEAD], F32),
        ("xs", [SLOTS, D], F32),
        ("ys", [SLOTS, D], F32),
        ("logits", [TURNS, 2 * EXPERTS, PAIR], F32),
    ):
        dram[name] = nc.dram_tensor("d_" + name, shape, dt, kind="Internal").ap()
    with ExitStack() as ctx:
        stage_layer0(nc, dram)
        route = Route(nc, ctx)
        with ExitStack() as scope:
            keep_rows(nc, scope, route)
            stage_routing(nc, dram, route)
            stage_experts(nc, dram, route)
        stage_attention(nc, dram, route)


_OUTS = [((8, 256, 256), "float32")]


def kernel(**inputs):
    import numpy as _np
    import concourse.bacc as _bacc
    from concourse import mybir as _mybir
    from concourse.bass_utils import run_bass_kernel_spmd as _run

    g = lambda name: _np.asarray(inputs[name])
    halves = lambda w, rows: w.reshape(DC, HEADS1 // 2, rows, D).transpose(0, 2, 1, 3).reshape(DC, rows, FEAT)
    laid = {
        "x": g("L0_attn_x").reshape(TOKENS, D),
        "WqkvT": g("L0_attn_Wqkv_w").T, "Wqkv_b": g("L0_attn_Wqkv_b"),
        "out_wT": g("L0_attn_out_w").T, "out_b": g("L0_attn_out_b"),
        "wgateT": g("L0_ffn_wq_gate").T, "s_gate": g("L0_ffn_s_gate"),
        "wupT": g("L0_ffn_wq_up").T, "s_up": g("L0_ffn_s_up"),
        "wdownT": g("L0_ffn_wq_down").T, "s_down": g("L0_ffn_s_down"),
        "w_codes": _np.stack([g(f"L1_attn_w{m}_codes").reshape(DC, P, FEAT) for m in "qkv"] +
                             [halves(g("L1_attn_wo_codes"), P)]),
        "w_scales": _np.stack([g(f"L1_attn_w{m}_scales").reshape(DC, P // BLOCK, FEAT) for m in "qkv"] +
                              [halves(g("L1_attn_wo_scales"), P // BLOCK)]),
        "bq": g("L1_attn_bq"), "bk": g("L1_attn_bk"), "bv": g("L1_attn_bv"), "bo": g("L1_attn_bo"),
        "w1T": g("L1_ffn_w1").transpose(0, 2, 1), "w3T": g("L1_ffn_w3").transpose(0, 2, 1), "w2T": g("L1_ffn_w2").transpose(0, 2, 1),
        "gate_wT": g("L1_ffn_gate_w").T,
        "sw1T": g("L1_ffn_sw1").T, "sw2T": g("L1_ffn_sw2").T, "sw3T": g("L1_ffn_sw3").T,
    }
    nc = _bacc.Bacc("TRN2", target_bir_lowering=False, num_devices=1)
    arrays, dram = {}, {}
    for name, a in laid.items():
        a = _np.ascontiguousarray(a)
        arrays[f"in_{name}"] = a
        dram[name] = nc.dram_tensor(f"in_{name}", a.shape, _mybir.dt.from_np(a.dtype), kind="ExternalInput").ap()
    shape, dtype = _OUTS[0]
    out = nc.dram_tensor("out_0", shape, _mybir.dt.from_np(_np.dtype(dtype)), kind="ExternalOutput").ap()
    dram["out"] = out.rearrange("b s d -> (b s) d")
    program(nc, dram)
    r = _run(nc, [arrays], core_ids=[0])
    return r.results[0]["out_0"]
```
